# Optimizing a Trainium2 kernel written in Bass

```python
import numpy as np
import jax
import jax.numpy as jnp

def _softmax(x, axis=-1):
    return jax.nn.softmax(x, axis=axis)

def _gelu(x):
    return jax.nn.gelu(x, approximate=True)

def _silu(x):
    return jax.nn.silu(x)

def _sigmoid(x):
    return jax.nn.sigmoid(x)

def _layernorm(x, axis=-1, eps=1e-05):
    m = jnp.mean(x, axis=axis, keepdims=True)
    v = jnp.var(x, axis=axis, keepdims=True)
    return (x - m) / jnp.sqrt(v + eps)

def _scatter_add(tgt, idx, src, axis=0):
    return tgt.at[idx].add(src)

def _segment_sum(src, seg, n):
    return jax.ops.segment_sum(src, seg, n)
kernel_name = 'mk_decoder_preln_d1_seqx_r4_390927'

def setup_inputs(seed: int=0):
    np.random.seed(seed)
    _w = jnp.asarray

    def _rec_inputs():
        import jax
        import jax.numpy as jnp
        _rk = jax.random.key(seed)
        x = -0.0002928 + 1 * jax.random.normal(jax.random.fold_in(_rk, 1), (8, 256, 256), jnp.float32)
        _lenS = 256 - jax.random.randint(jax.random.fold_in(_rk, 7), (8,), 0, max(1, 256 // 4) + 1, jnp.int32)
        _lenS2 = 256 - jax.random.randint(jax.random.fold_in(_rk, 8), (8,), 0, max(1, 256 // 4) + 1, jnp.int32)
        _ctx_1024P = jax.random.normal(jax.random.fold_in(_rk, 11), (8, 16, 256), jnp.float32)
        _ctx_1024c = jax.random.dirichlet(jax.random.fold_in(_rk, 511), 0.3 * jnp.ones((16,), jnp.float32), (8, 256))
        _ctx_1024t = jnp.einsum('bsk,bkd->bsd', _ctx_1024c, _ctx_1024P)
        _ctx_1024t = _ctx_1024t * jax.lax.rsqrt(jnp.mean(jnp.square(_ctx_1024t)) + 1e-12) * 0.953939
        ctx_1024 = -1.39393e-06 + 0.999914 * (_ctx_1024t + 0.3 * jax.random.normal(jax.random.fold_in(_rk, 611), (8, 256, 256), jnp.float32))
        fside_Bx1xSxS2_0 = -4.48278e-06 + 1.00019 * jax.random.normal(jax.random.fold_in(_rk, 12), (8, 1, 256, 256), jnp.float32)
        return (x, ctx_1024, fside_Bx1xSxS2_0)
    x, ctx_1024, fside_Bx1xSxS2_0 = _rec_inputs()

    def _L0_attn_setup():
        import jax, jax.numpy as jnp
        import numpy as np
        D_MODEL = 256
        D_STATE = 128
        D_CONV = 4
        EXPAND = 2
        HEADDIM = 64
        CHUNK = 64
        D_INNER = EXPAND * D_MODEL
        NHEADS = D_INNER // HEADDIM
        CONV_DIM = D_INNER + 2 * D_STATE
        D_IN_PROJ = 2 * D_INNER + 2 * D_STATE + NHEADS
        BATCH = 2
        SEQ = 1024
        EPS = 1e-05

        def _segsum(x):
            T = x.shape[-1]
            strict = jnp.tril(jnp.ones((T, T), dtype=bool), k=-1)
            xe = jnp.where(strict, x[..., :, None], 0.0)
            s = jnp.cumsum(xe, axis=-2)
            lower = jnp.tril(jnp.ones((T, T), dtype=bool), k=0)
            return jnp.where(lower, s, -jnp.inf)

        def _ssd(x, A, B, C, chunk):
            b, L, h, p = x.shape
            c = L // chunk
            x = x.reshape(b, c, chunk, h, p)
            A = A.reshape(b, c, chunk, h).transpose(0, 3, 1, 2)
            B = B.reshape(b, c, chunk, -1)
            C = C.reshape(b, c, chunk, -1)
            A_cs = jnp.cumsum(A, axis=-1)
            Lmat = jnp.exp(_segsum(A))
            Y_diag = jnp.einsum('bcln,bcsn,bhcls,bcshp->bclhp', C, B, Lmat, x)
            decay_states = jnp.exp(A_cs[..., -1:] - A_cs)
            states = jnp.einsum('bcln,bhcl,bclhp->bchpn', B, decay_states, x)
            init = jnp.zeros_like(states[:, :1])
            states = jnp.concatenate([init, states], axis=1)
            A_pad = jnp.pad(A_cs[:, :, :, -1], ((0, 0), (0, 0), (1, 0)))
            decay_chunk = jnp.exp(_segsum(A_pad))
            new_states = jnp.einsum('bhzc,bchpn->bzhpn', decay_chunk, states)
            states, final = (new_states[:, :-1], new_states[:, -1])
            Y_off = jnp.einsum('bcln,bchpn,bhcl->bclhp', C, states, jnp.exp(A_cs))
            Y = (Y_diag + Y_off).reshape(b, L, h, p)
            return (Y, final)
        key = jax.random.key(seed)
        ks = jax.random.split(key, 8)
        u = jax.random.normal(ks[0], (BATCH, SEQ, D_MODEL), dtype=jnp.float32)
        in_proj_w = jax.random.normal(ks[1], (D_MODEL, D_IN_PROJ), dtype=jnp.float32) * 0.02
        conv_weight = jax.random.normal(ks[2], (CONV_DIM, 1, D_CONV), dtype=jnp.float32) * 0.02
        conv_bias = jnp.zeros((CONV_DIM,), dtype=jnp.float32)
        dt = jnp.exp(jax.random.uniform(ks[3], (NHEADS,)) * (np.log(0.1) - np.log(0.001)) + np.log(0.001))
        dt = jnp.clip(dt, 0.0001)
        dt_bias = dt + jnp.log(jnp.expm1(dt))
        A_log = jnp.log(jax.random.uniform(ks[4], (NHEADS,), minval=1.0, maxval=16.0))
        D_param = jnp.ones((NHEADS,), dtype=jnp.float32)
        norm_weight = jnp.ones((D_INNER,), dtype=jnp.float32)
        out_proj_w = jax.random.normal(ks[5], (D_INNER, D_MODEL), dtype=jnp.float32) * 0.02
        return dict(u=u, in_proj_w=in_proj_w, conv_weight=conv_weight, conv_bias=conv_bias, dt_bias=dt_bias, A_log=A_log, D_param=D_param, norm_weight=norm_weight, out_proj_w=out_proj_w)
    _L0_attn_all = _L0_attn_setup()
    _L0_attn_in = {k: v for k, v in _L0_attn_all.items() if k in ('in_proj_w', 'conv_weight', 'conv_bias', 'dt_bias', 'A_log', 'D_param', 'norm_weight', 'out_proj_w')}
    del _L0_attn_all

    def _L0_xattn_setup():
        import jax, jax.numpy as jnp
        import numpy as np
        B, S, D_FF = (2, 512, 256)
        NUM_HEADS, D_KV = (16, 64)
        INNER = NUM_HEADS * D_KV
        key = jax.random.key(seed)
        ks = jax.random.split(key, 8)
        scale = 1.0 / np.sqrt(D_FF)
        return {'q': jax.random.normal(ks[0], (B, S, D_FF), jnp.float32), 'k': jax.random.normal(ks[1], (B, S, D_FF), jnp.float32), 'v': jax.random.normal(ks[2], (B, S, D_FF), jnp.float32), 'attn_mask': jax.random.normal(ks[3], (B, 1, S, S), jnp.float32), 'Wq': jax.random.normal(ks[4], (INNER, D_FF), jnp.float32) * scale, 'Wk': jax.random.normal(ks[5], (INNER, D_FF), jnp.float32) * scale, 'Wv': jax.random.normal(ks[6], (INNER, D_FF), jnp.float32) * scale, 'Wo': jax.random.normal(ks[7], (D_FF, INNER), jnp.float32) * scale, 'num_heads': NUM_HEADS}
    _L0_xattn_all = _L0_xattn_setup()
    _L0_xattn_in = {k: v for k, v in _L0_xattn_all.items() if k in ('Wq', 'Wk', 'Wv', 'Wo')}
    del _L0_xattn_all

    def _L0_ffn_setup():
        import jax, jax.numpy as jnp
        import numpy as np
        DIM = 256
        N_HEADS = 16
        N_KV_HEADS = 4
        HEAD_DIM = DIM // N_HEADS
        N_REP = N_HEADS // N_KV_HEADS
        N_EXPERTS = 4
        TOP_K = 2
        HIDDEN = 3 * DIM
        EPS = 1.1920928955078125e-07

        def _rmsnorm(x, g):
            var = jnp.mean(jnp.square(x), axis=-1, keepdims=True)
            return x * jax.lax.rsqrt(var + EPS) * g

        def _rotate_half(x):
            x1, x2 = jnp.split(x, 2, axis=-1)
            return jnp.concatenate([-x2, x1], axis=-1)

        def _rope_tables(S):
            inv_freq = 1.0 / 10000.0 ** (jnp.arange(0, HEAD_DIM, 2, dtype=jnp.float32) / HEAD_DIM)
            freqs = jnp.arange(S, dtype=jnp.float32)[:, None] * inv_freq[None, :]
            emb = jnp.concatenate([freqs, freqs], axis=-1)
            return (jnp.cos(emb), jnp.sin(emb))

        def _attention(x, wq, wk, wv, wo):
            B, S, D = x.shape
            q = (x @ wq).reshape(B, S, N_HEADS, HEAD_DIM).transpose(0, 2, 1, 3)
            k = (x @ wk).reshape(B, S, N_KV_HEADS, HEAD_DIM).transpose(0, 2, 1, 3)
            v = (x @ wv).reshape(B, S, N_KV_HEADS, HEAD_DIM).transpose(0, 2, 1, 3)
            cos, sin = _rope_tables(S)
            q = q * cos + _rotate_half(q) * sin
            k = k * cos + _rotate_half(k) * sin
            k = jnp.repeat(k, N_REP, axis=1)
            v = jnp.repeat(v, N_REP, axis=1)
            scores = jnp.einsum('bhqd,bhkd->bhqk', q, k) / jnp.sqrt(jnp.float32(HEAD_DIM))
            causal = jnp.tril(jnp.ones((S, S), dtype=bool))
            scores = jnp.where(causal, scores, -jnp.inf)
            attn = jax.nn.softmax(scores, axis=-1)
            out = jnp.einsum('bhqk,bhkd->bhqd', attn, v)
            return out.transpose(0, 2, 1, 3).reshape(B, S, D) @ wo

        def _moe(x, gate, w1, w2, w3):
            B, S, D = x.shape
            xf = x.reshape(-1, D)
            probs = jax.nn.softmax(xf @ gate, axis=-1)
            w, idx = jax.lax.top_k(probs, TOP_K)
            w = w / jnp.sum(w, axis=-1, keepdims=True)
            oh = jax.nn.one_hot(idx, N_EXPERTS, dtype=xf.dtype)
            comb = jnp.einsum('nk,nke->ne', w, oh)
            out = jnp.zeros_like(xf)
            for e in range(N_EXPERTS):
                h = jax.nn.silu(xf @ w1[e]) * (xf @ w3[e])
                out = out + comb[:, e:e + 1] * (h @ w2[e])
            return out.reshape(B, S, D)
        key = jax.random.key(seed)
        ks = jax.random.split(key, 12)
        s = 0.02
        B, S = (2, 512)
        return {'x': jax.random.normal(ks[0], (B, S, DIM), jnp.float32), 'g1': jnp.ones((DIM,), jnp.float32), 'g2': jnp.ones((DIM,), jnp.float32), 'wq': jax.random.normal(ks[1], (DIM, N_HEADS * HEAD_DIM), jnp.float32) * s, 'wk': jax.random.normal(ks[2], (DIM, N_KV_HEADS * HEAD_DIM), jnp.float32) * s, 'wv': jax.random.normal(ks[3], (DIM, N_KV_HEADS * HEAD_DIM), jnp.float32) * s, 'wo': jax.random.normal(ks[4], (N_HEADS * HEAD_DIM, DIM), jnp.float32) * s, 'gate': jax.random.normal(ks[5], (DIM, N_EXPERTS), jnp.float32) * s, 'w1': jax.random.normal(ks[6], (N_EXPERTS, DIM, HIDDEN), jnp.float32) * s, 'w2': jax.random.normal(ks[7], (N_EXPERTS, HIDDEN, DIM), jnp.float32) * s, 'w3': jax.random.normal(ks[8], (N_EXPERTS, DIM, HIDDEN), jnp.float32) * s}
    _L0_ffn_all = _L0_ffn_setup()
    _L0_ffn_in = {k: v for k, v in _L0_ffn_all.items() if k in ('g1', 'g2', 'wq', 'wk', 'wv', 'wo', 'gate', 'w1', 'w2', 'w3')}
    del _L0_ffn_all
    return {'x': x, 'ctx_1024': ctx_1024, 'fside_Bx1xSxS2_0': fside_Bx1xSxS2_0, 'L0_attn_in_proj_w': _L0_attn_in['in_proj_w'], 'L0_attn_conv_weight': _L0_attn_in['conv_weight'], 'L0_attn_conv_bias': _L0_attn_in['conv_bias'], 'L0_attn_dt_bias': _L0_attn_in['dt_bias'], 'L0_attn_A_log': _L0_attn_in['A_log'], 'L0_attn_D_param': _L0_attn_in['D_param'], 'L0_attn_norm_weight': _L0_attn_in['norm_weight'], 'L0_attn_out_proj_w': _L0_attn_in['out_proj_w'], 'L0_xattn_Wq': _L0_xattn_in['Wq'], 'L0_xattn_Wk': _L0_xattn_in['Wk'], 'L0_xattn_Wv': _L0_xattn_in['Wv'], 'L0_xattn_Wo': _L0_xattn_in['Wo'], 'L0_ffn_g1': _L0_ffn_in['g1'], 'L0_ffn_g2': _L0_ffn_in['g2'], 'L0_ffn_wq': _L0_ffn_in['wq'], 'L0_ffn_wk': _L0_ffn_in['wk'], 'L0_ffn_wv': _L0_ffn_in['wv'], 'L0_ffn_wo': _L0_ffn_in['wo'], 'L0_ffn_gate': _L0_ffn_in['gate'], 'L0_ffn_w1': _L0_ffn_in['w1'], 'L0_ffn_w2': _L0_ffn_in['w2'], 'L0_ffn_w3': _L0_ffn_in['w3']}

def reference(x, ctx_1024, fside_Bx1xSxS2_0, L0_attn_in_proj_w, L0_attn_conv_weight, L0_attn_conv_bias, L0_attn_dt_bias, L0_attn_A_log, L0_attn_D_param, L0_attn_norm_weight, L0_attn_out_proj_w, L0_xattn_Wq, L0_xattn_Wk, L0_xattn_Wv, L0_xattn_Wo, L0_ffn_g1, L0_ffn_g2, L0_ffn_wq, L0_ffn_wk, L0_ffn_wv, L0_ffn_wo, L0_ffn_gate, L0_ffn_w1, L0_ffn_w2, L0_ffn_w3):
    import jax
    import jax.numpy as jnp

    def _L0_attn_ref(u, in_proj_w, conv_weight, conv_bias, dt_bias, A_log, D_param, norm_weight, out_proj_w):
        import jax, jax.numpy as jnp
        import numpy as np
        D_MODEL = 256
        D_STATE = 128
        D_CONV = 4
        EXPAND = 2
        HEADDIM = 64
        CHUNK = 64
        D_INNER = EXPAND * D_MODEL
        NHEADS = D_INNER // HEADDIM
        CONV_DIM = D_INNER + 2 * D_STATE
        D_IN_PROJ = 2 * D_INNER + 2 * D_STATE + NHEADS
        BATCH = 2
        SEQ = 1024
        EPS = 1e-05

        def _segsum(x):
            T = x.shape[-1]
            strict = jnp.tril(jnp.ones((T, T), dtype=bool), k=-1)
            xe = jnp.where(strict, x[..., :, None], 0.0)
            s = jnp.cumsum(xe, axis=-2)
            lower = jnp.tril(jnp.ones((T, T), dtype=bool), k=0)
            return jnp.where(lower, s, -jnp.inf)

        def _ssd(x, A, B, C, chunk):
            b, L, h, p = x.shape
            c = L // chunk
            x = x.reshape(b, c, chunk, h, p)
            A = A.reshape(b, c, chunk, h).transpose(0, 3, 1, 2)
            B = B.reshape(b, c, chunk, -1)
            C = C.reshape(b, c, chunk, -1)
            A_cs = jnp.cumsum(A, axis=-1)
            Lmat = jnp.exp(_segsum(A))
            Y_diag = jnp.einsum('bcln,bcsn,bhcls,bcshp->bclhp', C, B, Lmat, x)
            decay_states = jnp.exp(A_cs[..., -1:] - A_cs)
            states = jnp.einsum('bcln,bhcl,bclhp->bchpn', B, decay_states, x)
            init = jnp.zeros_like(states[:, :1])
            states = jnp.concatenate([init, states], axis=1)
            A_pad = jnp.pad(A_cs[:, :, :, -1], ((0, 0), (0, 0), (1, 0)))
            decay_chunk = jnp.exp(_segsum(A_pad))
            new_states = jnp.einsum('bhzc,bchpn->bzhpn', decay_chunk, states)
            states, final = (new_states[:, :-1], new_states[:, -1])
            Y_off = jnp.einsum('bcln,bchpn,bhcl->bclhp', C, states, jnp.exp(A_cs))
            Y = (Y_diag + Y_off).reshape(b, L, h, p)
            return (Y, final)
        b, L, _ = u.shape
        zxbcdt = u @ in_proj_w
        z = zxbcdt[..., :D_INNER]
        xBC = zxbcdt[..., D_INNER:D_INNER + CONV_DIM]
        dt = jax.nn.softplus(zxbcdt[..., -NHEADS:] + dt_bias)
        cw = jnp.squeeze(conv_weight, axis=1).T
        xp = jnp.pad(xBC, ((0, 0), (D_CONV - 1, 0), (0, 0)))
        conv = sum((xp[:, i:i + L, :] * cw[i] for i in range(D_CONV))) + conv_bias
        xBC = conv * jax.nn.sigmoid(conv)
        x = xBC[..., :D_INNER].reshape(b, L, NHEADS, HEADDIM)
        Bm = xBC[..., D_INNER:D_INNER + D_STATE]
        Cm = xBC[..., D_INNER + D_STATE:]
        A = -jnp.exp(A_log)
        y, _ = _ssd(x * dt[..., None], A[None, None, :] * dt, Bm, Cm, CHUNK)
        y = y + D_param[None, None, :, None] * x
        y = y.reshape(b, L, D_INNER)
        y = y * (z * jax.nn.sigmoid(z))
        y = y * jax.lax.rsqrt(jnp.mean(jnp.square(y), axis=-1, keepdims=True) + EPS) * norm_weight
        return y @ out_proj_w

    def _L0_xattn_ref(q, k, v, attn_mask, Wq, Wk, Wv, Wo, num_heads):
        import jax, jax.numpy as jnp
        import numpy as np
        B, S, D_FF = (2, 512, 256)
        NUM_HEADS, D_KV = (16, 64)
        INNER = NUM_HEADS * D_KV
        b, s, _ = q.shape

        def proj_heads(x, W):
            y = jnp.einsum('bsd,ed->bse', x, W)
            return y.reshape(b, s, num_heads, -1).transpose(0, 2, 1, 3)
        qh = proj_heads(q, Wq)
        kh = proj_heads(k, Wk)
        vh = proj_heads(v, Wv)
        scores = jnp.einsum('bhqd,bhkd->bhqk', qh, kh) + attn_mask
        probs = jax.nn.softmax(scores, axis=-1)
        ctx = jnp.einsum('bhqk,bhkd->bhqd', probs, vh)
        ctx = ctx.transpose(0, 2, 1, 3).reshape(b, s, -1)
        return jnp.einsum('bse,de->bsd', ctx, Wo)

    def _L0_ffn_ref(x, g1, g2, wq, wk, wv, wo, gate, w1, w2, w3):
        import jax, jax.numpy as jnp
        import numpy as np
        DIM = 256
        N_HEADS = 16
        N_KV_HEADS = 4
        HEAD_DIM = DIM // N_HEADS
        N_REP = N_HEADS // N_KV_HEADS
        N_EXPERTS = 4
        TOP_K = 2
        HIDDEN = 3 * DIM
        EPS = 1.1920928955078125e-07

        def _rmsnorm(x, g):
            var = jnp.mean(jnp.square(x), axis=-1, keepdims=True)
            return x * jax.lax.rsqrt(var + EPS) * g

        def _rotate_half(x):
            x1, x2 = jnp.split(x, 2, axis=-1)
            return jnp.concatenate([-x2, x1], axis=-1)

        def _rope_tables(S):
            inv_freq = 1.0 / 10000.0 ** (jnp.arange(0, HEAD_DIM, 2, dtype=jnp.float32) / HEAD_DIM)
            freqs = jnp.arange(S, dtype=jnp.float32)[:, None] * inv_freq[None, :]
            emb = jnp.concatenate([freqs, freqs], axis=-1)
            return (jnp.cos(emb), jnp.sin(emb))

        def _attention(x, wq, wk, wv, wo):
            B, S, D = x.shape
            q = (x @ wq).reshape(B, S, N_HEADS, HEAD_DIM).transpose(0, 2, 1, 3)
            k = (x @ wk).reshape(B, S, N_KV_HEADS, HEAD_DIM).transpose(0, 2, 1, 3)
            v = (x @ wv).reshape(B, S, N_KV_HEADS, HEAD_DIM).transpose(0, 2, 1, 3)
            cos, sin = _rope_tables(S)
            q = q * cos + _rotate_half(q) * sin
            k = k * cos + _rotate_half(k) * sin
            k = jnp.repeat(k, N_REP, axis=1)
            v = jnp.repeat(v, N_REP, axis=1)
            scores = jnp.einsum('bhqd,bhkd->bhqk', q, k) / jnp.sqrt(jnp.float32(HEAD_DIM))
            causal = jnp.tril(jnp.ones((S, S), dtype=bool))
            scores = jnp.where(causal, scores, -jnp.inf)
            attn = jax.nn.softmax(scores, axis=-1)
            out = jnp.einsum('bhqk,bhkd->bhqd', attn, v)
            return out.transpose(0, 2, 1, 3).reshape(B, S, D) @ wo

        def _moe(x, gate, w1, w2, w3):
            B, S, D = x.shape
            xf = x.reshape(-1, D)
            probs = jax.nn.softmax(xf @ gate, axis=-1)
            w, idx = jax.lax.top_k(probs, TOP_K)
            w = w / jnp.sum(w, axis=-1, keepdims=True)
            oh = jax.nn.one_hot(idx, N_EXPERTS, dtype=xf.dtype)
            comb = jnp.einsum('nk,nke->ne', w, oh)
            out = jnp.zeros_like(xf)
            for e in range(N_EXPERTS):
                h = jax.nn.silu(xf @ w1[e]) * (xf @ w3[e])
                out = out + comb[:, e:e + 1] * (h @ w2[e])
            return out.reshape(B, S, D)
        x = x + _attention(_rmsnorm(x, g1), wq, wk, wv, wo)
        x = x + _moe(_rmsnorm(x, g2), gate, w1, w2, w3)
        return x
    x = x + _L0_attn_ref(_layernorm(x, axis=-1), L0_attn_in_proj_w, L0_attn_conv_weight, L0_attn_conv_bias, L0_attn_dt_bias, L0_attn_A_log, L0_attn_D_param, L0_attn_norm_weight, L0_attn_out_proj_w)
    x = x + _L0_xattn_ref(_layernorm(x, axis=-1), ctx_1024, ctx_1024, fside_Bx1xSxS2_0, L0_xattn_Wq, L0_xattn_Wk, L0_xattn_Wv, L0_xattn_Wo, 16)
    x = x + _L0_ffn_ref(_layernorm(x, axis=-1), L0_ffn_g1, L0_ffn_g2, L0_ffn_wq, L0_ffn_wk, L0_ffn_wv, L0_ffn_wo, L0_ffn_gate, L0_ffn_w1, L0_ffn_w2, L0_ffn_w3)
    return x

_drawn_inputs = setup_inputs


def setup_inputs(seed=0):
    import zlib

    import numpy as np

    out = dict(_drawn_inputs(seed))
    spreads = {'L0_attn_conv_bias': (0.0, 0.1),
     'L0_attn_D_param': (1.0, 0.2),
     'L0_attn_norm_weight': (1.0, 0.2),
     'L0_ffn_g1': (1.0, 0.6),
     'L0_ffn_g2': (1.0, 0.6)}
    factors = {'L0_attn_dt_bias': 8.0,
     'L0_attn_A_log': 8.0,
     'L0_ffn_wq': 8.0,
     'L0_ffn_wk': 8.0,
     'L0_ffn_wv': 4.022,
     'L0_ffn_wo': 4.157,
     'L0_ffn_gate': 8.0,
     'L0_ffn_w1': 8.0,
     'L0_ffn_w2': 8.0,
     'L0_ffn_w3': 8.0}
    for name, (base, spread) in spreads.items():
        noise = np.random.default_rng([zlib.crc32(name.encode()), seed]).standard_normal(out[name].shape)
        drawn = base * np.exp(spread * noise) if base else spread * noise
        out[name] = jnp.asarray(drawn.astype(out[name].dtype))
    for name, factor in factors.items():
        out[name] = (out[name] * factor).astype(out[name].dtype)
    return out
```

```python
from contextlib import ExitStack

import numpy as np
import concourse.bass as bass
from concourse import mybir

F32 = mybir.dt.float32
I32 = mybir.dt.int32
FR = mybir.dt.float32r
ALU = mybir.AluOpType
ACT = mybir.ActivationFunctionType
AX_X = mybir.AxisListType.X

P = 128
B, S, D = 8, 256, 256
KD = D // P
TOK = B * S
GT = 4
NG = TOK // (P * GT)
GN = GT * P
QT = S // P

DI, NST, NH, HD, TAPS = 512, 128, 8, 64, 4
XT = DI // P
CT = XT + 2
PROJ = 2 * DI + 2 * NST + NH
LN_EPS, SSM_EPS = 1e-5, 1e-5

XH, XD = 16, 64
XI = XH * XD
ET = XI // P
VW = XD + 1

AH, AKV, AD = 16, 4, 16
REP = AH // AKV
AQKV = (AH + 2 * AKV) * AD
AVW = AD + 1
RMS_EPS = 1.1920928955078125e-07

NE, HID = 4, 3 * D
HT = HID // P

NEG = -1e30

C_ID, C_UPTO, C_AFTER, C_CAUSAL, C_ROW, C_LOW = 0, 128, 256, 384, 640, 644
C_N = C_LOW + NE * NE


def constants():
    c = np.zeros((P, C_N), np.float32)
    i = np.arange(P)
    c[:, C_ID:C_ID + P] = np.eye(P)
    c[:, C_UPTO:C_UPTO + P] = i[:, None] <= i[None, :]
    c[:, C_AFTER:C_AFTER + P] = i[:, None] > i[None, :]
    c[:, C_CAUSAL + P:C_CAUSAL + 2 * P] = np.where(i[None, :] > i[:, None], NEG, 0.0)
    c[:, C_ROW:C_ROW + REP] = (i[:, None] % (REP * AD)) // AD == np.arange(REP)[None, :]
    e = np.arange(NE)
    c[:, C_LOW:] = (e[None, :] < e[:, None]).reshape(1, NE * NE)
    return c


def rope_tables():
    inv = (1.0 / np.float32(10000.0) ** (np.arange(0, AD, 2, dtype=np.float32) / np.float32(AD))).astype(np.float32)
    ang = np.arange(S, dtype=np.float32)[:, None] * inv[None, :]
    t = np.stack([np.cos(ang), -np.sin(ang), np.sin(ang)], axis=1).astype(np.float32)
    return np.ascontiguousarray(t.reshape(QT, P, 3, AD // 2).transpose(1, 0, 2, 3))


def semaphores(nc, ctx, stage, names):
    return {n: ctx.enter_context(nc.semaphore(f"{stage}_{n}")) for n in names.split()}


def clear(sp, sems):
    for s in sems.values():
        sp.sem_clear(s)


def split_matmul(pe, out, a, b, start, stop):
    (ah, al), (bh, bl) = a, b
    pe.matmul(out, ah, bl, start=start, stop=False)
    pe.matmul(out, al, bh, start=False, stop=False)
    return pe.matmul(out, ah, bh, start=False, stop=stop)


class Chain:

    def __init__(self, eng, sem):
        self.eng, self.sem, self.n = eng, sem, 0

    def then(self, ins):
        self.n += 1
        ins.then_inc(self.sem, 1)

    def sync(self):
        if self.n:
            self.eng.wait_ge(self.sem, self.n)

    def link(self, ins):
        self.then(ins)
        self.sync()



def norm_stats(dve, ch, src, st, mv, ready):
    for t in range(GT):
        ch.then(dve.bn_stats(st[:, t, :], src[:, t, :]))
    ch.sync()
    for t in range(GT):
        dve.bn_aggr(mv[:, t, :], st[:, t, :]).then_inc(ready, 1)


def inverse_root(dve, ch, out, var, eps, tmp):
    hv, t = tmp
    ch.link(dve.tensor_scalar(t, var, eps, None, ALU.add))
    ch.then(dve.tensor_scalar(hv, t, -0.5, None, ALU.mult))
    ch.link(dve.tensor_scalar(out.bitcast(I32), t.bitcast(I32), 1, None, ALU.logical_shift_right))
    ch.link(dve.tensor_scalar(out.bitcast(I32), out.bitcast(I32), -1.0, float(0x5F3759DF), ALU.mult, ALU.add))
    for _ in range(3):
        ch.link(dve.tensor_tensor(t, out, out, ALU.mult))
        ch.link(dve.tensor_tensor(t, t, hv, ALU.mult))
        ch.link(dve.scalar_tensor_tensor(out=out, in0=t, scalar=1.5, in1=out, op0=ALU.add, op1=ALU.mult))


def transposes_in(pe, src, ident, banks, tiles, done):
    for k in range(tiles):
        for t in range(GT):
            ins = pe.transpose(banks[k][:, t * P:(t + 1) * P], src[:, t, k * P:(k + 1) * P], ident)
        ins.then_inc(done, 1)


def part_high(act, out, psum, scale=None):
    if scale is None:
        return act.activation(out, psum, ACT.Copy)
    return act.activation(out, psum, ACT.Identity, scale=scale)


def part_low(dve, out, psum, high, scale=None):
    return dve.scalar_tensor_tensor(out=out, in0=psum, scalar=1.0 if scale is None else scale,
                                    in1=high.bitcast(F32), op0=ALU.mult, op1=ALU.subtract)



def load_weights(nc, ctx, I, W, K):
    s = semaphores(nc, ctx, "w", "const high low misc alog zero")
    raws = [("win", I["win"]), ("wout", I["wout"]), ("wq", I["wq"]), ("wk", I["wk"]), ("wv", I["wv"]), ("wo", I["wo"]),
            ("aqkv", I["aqkv"]), ("awo", I["awo"]), ("gate", I["gate"])]
    loaded = {n: ctx.enter_context(nc.semaphore(f"w_{n}")) for n, _ in raws}
    with ExitStack() as own:
        raw = {n: own.enter_context(nc.sbuf_tensor(f"raw_{n}", list(src.shape), F32)) for n, src in raws}
        block = own.enter_context(nc.Block())

        @block.sync
        def _(sp):
            for n, src in raws:
                sp.dma_start(raw[n][:], src).then_inc(loaded[n], 16)

        @block.scalar
        def _(act):
            act.dma_start(K["const"][:], I["const"]).then_inc(s["const"], 16)
            for out, src in ((K["rope"], I["rope"]), (K["taps"], I["taps"]), (K["tapb"], I["tapb"]), (K["nw"], I["nw"]), (K["g1"], I["g1"]), (K["g2"], I["g2"]),
                             (K["dtb"], I["dtb"]), (K["alog"], I["alog"]), (K["dpar"], I["dpar"])):
                act.dma_start(out[:], src).then_inc(s["misc"], 16)
            for n, _ in raws:
                act.wait_ge(loaded[n], 16)
                act.activation(W[n][0][:], raw[n][:], ACT.Copy).then_inc(s["high"], 1)
            act.wait_ge(s["misc"], 144)
            act.activation(K["alog"][:], K["alog"][:], ACT.Exp).then_inc(s["alog"], 1)

        @block.vector
        def _(dve):
            for i, (n, _) in enumerate(raws):
                dve.wait_ge(s["high"], i + 1)
                dve.tensor_tensor(W[n][1][:], raw[n][:], W[n][0][:].bitcast(F32), ALU.subtract).then_inc(s["low"], 1)
            dve.wait_ge(s["alog"], 1)
            dve.tensor_scalar(K["A"][:], K["alog"][:], -1.0, None, ALU.mult).then_inc(s["zero"], 1)
            dve.tensor_scalar(K["taps"][:], K["taps"][:], 0.5, None, ALU.mult).then_inc(s["zero"], 1)
            dve.tensor_scalar(K["tapb"][:], K["tapb"][:], 0.5, None, ALU.mult).then_inc(s["zero"], 1)
            dve.wait_ge(s["const"], 16)
    return s



def stage_mamba(nc, ctx, g, I, W, K, XG, ps, s, last):
    with ExitStack() as own:
        def sb(name, shape, dt=F32):
            return own.enter_context(nc.sbuf_tensor("a_" + name, shape, dt))

        st, mv, rstd = sb("st", [P, GT, 6]), sb("mv", [P, GT, 2]), sb("rstd", [P, GT])
        nt = sb("nt", [P, 2, GT])
        xn = sb("xn", [P, GT, D])
        uh, ul = sb("uh", [P, KD, GN], FR), sb("ul", [P, KD, GN], FR)
        cv, th = sb("cv", [P, 2, GN]), sb("th", [P, 2, GN])
        xs = sb("xs", [P, CT, GN])
        zg = sb("zg", [P, GT, DI])
        dtf = sb("dtf", [NH, GN])
        v, r, e, den, zz, z2, acc, dt, a = (sb(n, [P, GT, NH]) for n in "v r e den zz z2 acc dt a".split())
        av = sb("av", [P, NH, P])
        lm = sb("lm", [P, 2, NH, P])
        gm = sb("gm", [P, 2, P])
        g01 = sb("g01", [P, P])
        dec = sb("dec", [P, 2, NH])
        xd = sb("xd", [P, 2, DI])
        xdd = sb("xdd", [P, DI])
        y = sb("y", [P, 2, DI])
        yo = sb("yo", [P, DI])
        sq = sb("sq", [P, DI])
        ss, rs = sb("ss", [P, GT]), sb("rs", [P, GT])
        yh, yl = sb("yh", [P, XT, P], FR), sb("yl", [P, XT, P], FR)

        T0, T1, J0, J1, D0, D1, YB, SM = ps
        T, J = (T0, T1), (J0, J1)
        ident = K["const"][:, C_ID:C_ID + P]
        upto, after = K["const"][:, C_UPTO:C_UPTO + P], K["const"][:, C_AFTER:C_AFTER + P]
        NJ = CT + 1 + GT
        ORDER = [XT, XT + 1, *range(XT)]
        block = own.enter_context(nc.Block())

        @block.sync
        def _(sp):
            clear(sp, last)
            sp.dma_start(XG[:], I["x"][g]).then_inc(s["x_in"], 16)

        @block.gpsimd
        def _(pool):
            for t in range(GT):
                if t == 0:
                    pool.wait_ge(s["a"], 1)
                else:
                    pool.wait_ge(s["D"], t)
                pool.tensor_tensor(av[:], a[:, t, :].unsqueeze(2).to_broadcast([P, NH, P]),
                                   upto.unsqueeze(1).to_broadcast([P, NH, P]), ALU.mult).then_inc(s["av"], 1)

        @block.tensor
        def _(pe):
            pe.wait_ge(s["xn"], GT)
            transposes_in(pe, xn, ident, T, KD, s["xnT"])
            pe.wait_ge(s["ul"], KD)
            for n in range(NJ):
                if n >= 2:
                    pe.wait_ge(s["Jfree"], n - 1)
                if n <= CT:
                    w0 = DI + ORDER[n] * P if n < CT else PROJ - NH
                    M = P if n < CT else NH
                    for k in range(KD):
                        ins = split_matmul(pe, J[n % 2][0:M, :], [w[:, k, w0:w0 + M] for w in W["win"]],
                                           (uh[:, k, :], ul[:, k, :]), k == 0, k == KD - 1)
                else:
                    t = n - CT - 1
                    for k in range(KD):
                        ins = split_matmul(pe, J[n % 2][:], (uh[:, k, t * P:(t + 1) * P], ul[:, k, t * P:(t + 1) * P]),
                                           [w[:, k, 0:DI] for w in W["win"]], k == 0, k == KD - 1)
                ins.then_inc(s["J"], 1)
            pe.wait_ge(s["dtf"], 1)
            for t in range(GT):
                ins = pe.transpose(SM[:, t * NH:(t + 1) * NH], dtf[:, t * P:(t + 1) * P], ident[0:NH, 0:NH])
            ins.then_inc(s["dtT"], 1)

            def front(t):
                c = t % QT
                if t == 0:
                    pe.wait_ge(s["xs"], CT)
                else:
                    pe.wait_ge(s["xd"], t)
                for k in range(XT):
                    ins = pe.transpose(T0[:, k * P:(k + 1) * P], xs[:, k, t * P:(t + 1) * P], ident)
                ins.then_inc(s["xT"], 1)
                if t == 0:
                    pe.wait_ge(s["a"], 1)
                else:
                    pe.wait_ge(s["small"], t)
                pe.matmul(SM[:, 0:P], xs[:, XT, t * P:(t + 1) * P], xs[:, XT + 1, t * P:(t + 1) * P], start=True, stop=True)
                if c:
                    pe.matmul(SM[:, P:2 * P], xs[:, XT, (t - 1) * P:t * P], xs[:, XT + 1, t * P:(t + 1) * P],
                              start=True, stop=True)
                ins = pe.matmul(SM[:, 2 * P:2 * P + NH], upto if c else after, a[:, t, :], start=True, stop=True)
                ins.then_inc(s["SM"], 1)
                pe.wait_ge(s["av"], t + 1)
                for i, bank in enumerate((D0, D1)):
                    if t:
                        pe.wait_ge(s["L"], 2 * t - 1 + i)
                    ins = pe.matmul(bank[:], after, av[:, i * NH // 2:(i + 1) * NH // 2, :], start=True, stop=True)
                ins.then_inc(s["D"], 1)

            def mid(t):
                pe.wait_ge(s["M"], t + 1)
                if t:
                    pe.wait_ge(s["y"], t)
                for h in range(NH):
                    ins = pe.matmul(YB[:, h * HD:(h + 1) * HD], lm[:, t % 2, h, :], xd[:, t % 2, h * HD:(h + 1) * HD],
                                    start=True, stop=True)
                ins.then_inc(s["Y"], 1)
                if t % QT:
                    pe.wait_ge(s["xdd"], t // QT + 1)
                    if t // QT:
                        pe.wait_ge(s["yo"], t // QT)
                    pe.matmul(T1[:], g01[:], xdd[:], start=True, stop=True).then_inc(s["YO"], 1)

            def end(t):
                pe.wait_ge(s["yn"], t + 1)
                if t:
                    pe.wait_ge(s["yl"], t)
                for k in range(XT):
                    ins = pe.transpose(J0[:, k * P:(k + 1) * P], y[:, t % 2, k * P:(k + 1) * P], ident)
                ins.then_inc(s["yT"], 1)
                pe.wait_ge(s["yl"], t + 1)
                if t:
                    pe.wait_ge(s["res"], t)
                for k in range(XT):
                    ins = split_matmul(pe, J1[:, 0:D], (yh[:, k, :], yl[:, k, :]), [w[:, k, :] for w in W["wout"]],
                                       k == 0, k == XT - 1)
                ins.then_inc(s["O"], 1)

            for i in range(GT + 2):
                if i < GT:
                    front(i)
                if 0 <= i - 1 < GT:
                    mid(i - 1)
                if 0 <= i - 2 < GT:
                    if i == 2:
                        pe.wait_ge(s["Jfree"], NJ)
                    end(i - 2)

        @block.scalar
        def _(act):
            for k in range(KD):
                act.wait_ge(s["xnT"], k + 1)
                part_high(act, uh[:, k, :], T[k][:]).then_inc(s["uh"], 1)
            for n in range(NJ):
                act.wait_ge(s["J"], n + 1)
                if n < CT:
                    f = ORDER[n]
                    if n >= 2:
                        act.wait_ge(s["xs"], n - 1)
                    act.activation(cv[:, n % 2, :], J[n % 2][:], ACT.Identity, bias=K["tapb"][:, f:f + 1],
                                   scale=K["taps"][:, f, TAPS - 1:TAPS]).then_inc(s["cv"], 1)
                    act.wait_ge(s["conv"], n + 1)
                    act.activation(th[:, n % 2, :], cv[:, n % 2, :], ACT.Tanh).then_inc(s["th"], 1)
                elif n == CT:
                    act.activation(dtf[:], J[n % 2][0:NH, :], ACT.Copy).then_inc(s["dtf"], 1)
                else:
                    t = n - CT - 1
                    act.activation(zg[:, t, :], J[n % 2][:], ACT.Tanh, scale=0.5).then_inc(s["zt"], 1)
            act.wait_ge(s["nv"], 1)
            act.activation(e[:], e[:], ACT.Exp).then_inc(s["e"], 1)
            for i in range(GT + 2):
                if i < GT:
                    act.wait_ge(s["D"], i + 1)
                    if i >= 2:
                        act.wait_ge(s["Y"], i - 1)
                    for j, bank in enumerate((D0, D1)):
                        act.activation(lm[:, i % 2, j * NH // 2:(j + 1) * NH // 2, :], bank[:], ACT.Exp).then_inc(s["L"], 1)
                    act.wait_ge(s["small"], i + 1)
                    act.activation(dec[:, i % 2, :], dec[:, i % 2, :], ACT.Exp).then_inc(s["dec"], 1)
                t = i - 1
                if 0 <= t < GT:
                    act.wait_ge(s["yg"], t + 1)
                    if t:
                        act.wait_ge(s["ss"], t)
                    act.activation(sq[:], y[:, t % 2, :], ACT.Square, accum_out=ss[:, t:t + 1]).then_inc(s["ss"], 1)
                t = i - 2
                if 0 <= t < GT:
                    act.wait_ge(s["yT"], t + 1)
                    if t:
                        act.wait_ge(s["O"], t)
                    for k in range(XT):
                        part_high(act, yh[:, k, :], J0[:, k * P:(k + 1) * P], K["nw"][:, k:k + 1]).then_inc(s["yh"], 1)

        @block.vector
        def _(dve):
            ch = Chain(dve, s["chain"])
            dve.wait_ge(s["x_in"], 16)
            norm_stats(dve, ch, XG, st, mv, s["var"])
            dve.wait_ge(s["var"], GT)
            inverse_root(dve, ch, rstd[:], mv[:, :, 1], LN_EPS, (nt[:, 0], nt[:, 1]))
            for t in range(GT):
                dve.tensor_scalar(xn[:, t, :], XG[:, t, :], mv[:, t, 0:1], rstd[:, t:t + 1],
                                  ALU.subtract, ALU.mult).then_inc(s["xn"], 1)
            for k in range(KD):
                dve.wait_ge(s["uh"], k + 1)
                part_low(dve, ul[:, k, :], T[k][:], uh[:, k, :]).then_inc(s["ul"], 1)
            for n in range(NJ):
                if n < CT:
                    f = ORDER[n]
                    dve.wait_ge(s["cv"], n + 1)
                    out = cv[:, n % 2, :].rearrange("p (b l) -> p b l", b=2)
                    src = J[n % 2][:].rearrange("p (b l) -> p b l", b=2)
                    for k in range(1, TAPS):
                        if k > 1:
                            ch.sync()
                        ins = dve.scalar_tensor_tensor(out=out[:, :, k:], in0=src[:, :, 0:S - k],
                                                       scalar=K["taps"][:, f, TAPS - 1 - k:TAPS - k], in1=out[:, :, k:],
                                                       op0=ALU.mult, op1=ALU.add)
                        if k < TAPS - 1:
                            ch.then(ins)
                    ins.then_inc(s["conv"], 1)
                    dve.wait_ge(s["conv"], n + 1)
                    dve.sem_inc(s["Jfree"], 1)
                    dve.wait_ge(s["th"], n + 1)
                    dve.scalar_tensor_tensor(out=xs[:, f, :], in0=th[:, n % 2, :], scalar=1.0, in1=cv[:, n % 2, :],
                                             op0=ALU.add, op1=ALU.mult).then_inc(s["xs"], 1)
                elif n == CT:
                    dve.wait_ge(s["dtf"], 1)
                    dve.sem_inc(s["Jfree"], 1)
                else:
                    t = n - CT - 1
                    dve.wait_ge(s["zt"], t + 1)
                    dve.scalar_tensor_tensor(out=zg[:, t, :], in0=zg[:, t, :], scalar=1.0, in1=J[n % 2][:],
                                             op0=ALU.add, op1=ALU.mult).then_inc(s["Jfree"], 1)
            dve.wait_ge(s["dtT"], 1)
            ch.link(dve.tensor_tensor(v[:], SM[:, 0:GT * NH].rearrange("p (t h) -> p t h", t=GT),
                                      K["dtb"][:].unsqueeze(1).to_broadcast([P, GT, NH]), ALU.add))
            ch.link(dve.tensor_scalar(r[:], v[:], 0.0, None, ALU.max))
            dve.scalar_tensor_tensor(out=e[:], in0=r[:], scalar=-2.0, in1=v[:], op0=ALU.mult,
                                     op1=ALU.add).then_inc(s["nv"], 1)
            dve.wait_ge(s["e"], 1)
            ch.link(dve.tensor_scalar(den[:], e[:], 2.0, None, ALU.add))
            ch.link(dve.reciprocal(den[:], den[:]))
            ch.link(dve.tensor_tensor(zz[:], e[:], den[:], ALU.mult))
            ch.link(dve.tensor_tensor(z2[:], zz[:], zz[:], ALU.mult))
            ch.link(dve.tensor_scalar(acc[:], z2[:], 1.0 / 15, None, ALU.mult))
            for m in (13, 11, 9, 7, 5, 3):
                ch.link(dve.scalar_tensor_tensor(out=acc[:], in0=acc[:], scalar=1.0 / m, in1=z2[:],
                                                 op0=ALU.add, op1=ALU.mult))
            ch.link(dve.scalar_tensor_tensor(out=acc[:], in0=acc[:], scalar=1.0, in1=zz[:], op0=ALU.add, op1=ALU.mult))
            ch.link(dve.scalar_tensor_tensor(out=dt[:], in0=acc[:], scalar=2.0, in1=r[:], op0=ALU.mult, op1=ALU.add))
            dve.tensor_tensor(a[:], dt[:], K["A"][:].unsqueeze(1).to_broadcast([P, GT, NH]), ALU.mult).then_inc(s["a"], 1)

            def heads(ap):
                return ap.rearrange("p (h d) -> p h d", h=NH)

            def wide(ap):
                return ap.unsqueeze(2).to_broadcast([P, NH, HD])

            def front(t):
                c = t % QT
                dve.wait_ge(s["xT"], t + 1)
                if t >= 2:
                    dve.wait_ge(s["Y"], t - 1)
                    dve.wait_ge(s["yT"], t - 1)
                dve.tensor_tensor(heads(y[:, t % 2, :]), heads(T0[:]), wide(K["dpar"][:]), ALU.mult).then_inc(s["dx"], 1)
                dve.tensor_tensor(heads(xd[:, t % 2, :]), heads(T0[:]), wide(dt[:, t, :]), ALU.mult).then_inc(s["xd"], 1)
                dve.wait_ge(s["SM"], t + 1)
                ch.link(dve.tensor_tensor(gm[:, t % 2, :], SM[:, 0:P], upto, ALU.mult))
                if c:
                    if t // QT:
                        dve.wait_ge(s["YO"], t // QT)
                    ch.link(dve.tensor_copy(g01[:], SM[:, P:2 * P]))
                dve.tensor_copy(dec[:, t % 2, :], SM[:, 2 * P:2 * P + NH]).then_inc(s["small"], 1)
                dve.wait_ge(s["L"], 2 * t + 2)
                dve.tensor_tensor(lm[:, t % 2], lm[:, t % 2], gm[:, t % 2, :].unsqueeze(1).to_broadcast([P, NH, P]),
                                  ALU.mult).then_inc(s["M"], 1)
                if c:
                    dve.wait_ge(s["dec"], t)
                    dve.wait_ge(s["xd"], t)
                    dve.tensor_tensor(heads(xdd[:]), heads(xd[:, (t - 1) % 2, :]), wide(dec[:, (t - 1) % 2, :]),
                                      ALU.mult).then_inc(s["xdd"], 1)

            def mid(t):
                dve.wait_ge(s["Y"], t + 1)
                dve.wait_ge(s["dx"], t + 1)
                dve.tensor_tensor(y[:, t % 2, :], y[:, t % 2, :], YB[:], ALU.add).then_inc(s["y"], 1)
                dve.wait_ge(s["y"], t + 1)
                if t % QT:
                    dve.wait_ge(s["YO"], t // QT + 1)
                    dve.wait_ge(s["dec"], t + 1)
                    dve.tensor_tensor(heads(yo[:]), heads(T1[:]), wide(dec[:, t % 2, :]), ALU.mult).then_inc(s["yo"], 1)
                    dve.wait_ge(s["yo"], t // QT + 1)
                    ch.link(dve.tensor_tensor(y[:, t % 2, :], y[:, t % 2, :], yo[:], ALU.add))
                dve.tensor_tensor(y[:, t % 2, :], y[:, t % 2, :], zg[:, t, :], ALU.mult).then_inc(s["yg"], 1)
                dve.wait_ge(s["yg"], t + 1)
                dve.wait_ge(s["ss"], t + 1)
                inverse_root(dve, ch, rs[:, t:t + 1], ss[:, t:t + 1], 4 * DI * SSM_EPS, (nt[:, 0, 0:1], nt[:, 1, 0:1]))
                dve.tensor_scalar(y[:, t % 2, :], y[:, t % 2, :], rs[:, t:t + 1], float(DI) ** 0.5,
                                  ALU.mult, ALU.mult).then_inc(s["yn"], 1)

            def end(t):
                if t:
                    dve.wait_ge(s["O"], t)
                dve.wait_ge(s["yh"], XT * (t + 1))
                for k in range(XT):
                    ins = part_low(dve, yl[:, k, :], J0[:, k * P:(k + 1) * P], yh[:, k, :], K["nw"][:, k:k + 1])
                ins.then_inc(s["yl"], 1)
                dve.wait_ge(s["O"], t + 1)
                dve.tensor_tensor(XG[:, t, :], XG[:, t, :], J1[:, 0:D], ALU.add).then_inc(s["res"], 1)

            for i in range(GT + 2):
                if i < GT:
                    front(i)
                if 0 <= i - 1 < GT:
                    mid(i - 1)
                if 0 <= i - 2 < GT:
                    end(i - 2)
            dve.wait_ge(s["res"], GT)



def stage_cross(nc, ctx, g, I, W, K, XG, ps, s, last):
    with ExitStack() as own:
        def sb(name, shape, dt=F32):
            return own.enter_context(nc.sbuf_tensor("b_" + name, shape, dt))

        st, mv, rstd, nt = sb("st", [P, GT, 6]), sb("mv", [P, GT, 2]), sb("rstd", [P, GT]), sb("nt", [P, 2, GT])
        xn = sb("xn", [P, GT, D])
        uh, ul = sb("uh", [P, KD, GN], FR), sb("ul", [P, KD, GN], FR)
        cr = sb("cr", [P, KD, GN])
        eh, el = sb("eh", [P, KD * GN], FR), sb("el", [P, KD * GN], FR)
        c = [e[:].rearrange("p (k n) -> p k n", k=KD) for e in (eh, el)]
        o = [e[:].rearrange("p (k n) -> p k n", k=ET) for e in (eh, el)]
        mask = sb("mask", [P, GT, S])
        q, k_ = sb("q", [P, 2, GN]), sb("k", [P, 2, GN])
        va = sb("va", [P, GT, XH, VW])
        pp = sb("pp", [P, 3, QT, S])
        nm = sb("nm", [P, 4, QT])
        pt = sb("pt", [P, 2, 2 * S])
        rc = sb("rc", [P, 2, QT, 2])
        ot = sb("ot", [P, GT, XI])

        PJ, S3, T2, O2 = ps[0], ps[1:4], ps[4:6], ps[6:8]
        ident = K["const"][:, C_ID:C_ID + P]
        NU = ET * 2
        NHD = 2 * NU
        NV = GT * 2
        block = own.enter_context(nc.Block())

        def tokens(b, qt):
            return slice((b * QT + qt) * P, (b * QT + qt + 1) * P)

        @block.sync
        def _(sp):
            clear(sp, last)
            sp.dma_start(cr[:], I["ctxT"][g]).then_inc(s["ctx_in"], 16)
            sp.dma_start(mask[:], I["mask"][g]).then_inc(s["mask_in"], 16)

        @block.gpsimd
        def _(pool):
            pool.memset(va[:, :, :, XD], 1.0).then_inc(s["ones"], 1)

        @block.tensor
        def _(pe):
            pe.wait_ge(s["cl"], 1)
            for n in range(NV):
                t, half = n // 2, n % 2
                bank = (PJ, *S3)[n % 4]
                if n >= 4:
                    pe.wait_ge((s["va"], s["v"])[n % 2], n // 2 - 1)
                for k in range(KD):
                    ins = split_matmul(pe, bank[:], [x[:, k, t * P:(t + 1) * P] for x in c],
                                       [w[:, k, half * 512:(half + 1) * 512] for w in W["wv"]], k == 0, k == KD - 1)
                ins.then_inc(s["V"], 1)
            pe.wait_ge(s["xn"], GT)
            transposes_in(pe, xn, ident, T2, KD, s["xnT"])
            pe.wait_ge(s["ul"], KD)

            def project(j, which):
                n = 2 * j + which
                if n:
                    pe.wait_ge(s["qk"], n)
                else:
                    pe.wait_ge(s["va"], NV // 2)
                    pe.wait_ge(s["v"], NV // 2)
                w, x = (W["wq"], (uh, ul)) if which == 0 else (W["wk"], c)
                for k in range(KD):
                    ins = split_matmul(pe, PJ[:], [a[:, k, j * P:(j + 1) * P] for a in w],
                                       [a[:, k, :] for a in x], k == 0, k == KD - 1)
                ins.then_inc(s["QK"], 1)

            def scores(n):
                u, hp = n // 2, n % 2
                j, b = u // 2, u % 2
                if b == 0 and hp == 0:
                    pe.wait_ge(s["qk"], 2 * j + 2)
                if n >= 3:
                    pe.wait_ge(s["sm"], 2 * (n - 2))
                r = slice(XD * hp, XD * hp + XD)
                for qt in range(QT):
                    ins = pe.matmul(S3[n % 3][:, qt * S:(qt + 1) * S], q[r, j % 2, tokens(b, qt)],
                                    k_[r, j % 2, b * S:(b + 1) * S], start=True, stop=True)
                ins.then_inc(s["S"], 1)

            def turn(n):
                pe.wait_ge(s["ex"], 2 * (n + 1))
                if n >= 2:
                    pe.wait_ge(s["pt"], n - 1)
                for kt in range(QT):
                    for qt in range(QT):
                        ins = pe.transpose(T2[n % 2][:, kt * S + qt * P:kt * S + (qt + 1) * P],
                                           pp[:, n % 3, qt, kt * P:(kt + 1) * P], ident)
                ins.then_inc(s["T"], 1)

            def values(n):
                u, hp = n // 2, n % 2
                j, b = u // 2, u % 2
                pe.wait_ge(s["pt"], n + 1)
                if hp == 0 and u >= 2:
                    pe.wait_ge(s["o"], u - 1)
                for qt in range(QT):
                    for kt in range(QT):
                        at = (hp * QT + qt) * VW
                        ins = pe.matmul(O2[u % 2][:, at:at + VW], pt[:, n % 2, kt * S + qt * P:kt * S + (qt + 1) * P],
                                        va[:, b * QT + kt, 2 * j + hp, :], start=kt == 0, stop=kt == QT - 1)
                ins.then_inc(s["PV"], 1)

            project(0, 0)
            project(0, 1)
            pe.wait_ge(s["ones"], 1)
            scores(0)
            for n in range(NHD + 1):
                if n + 1 < NHD:
                    scores(n + 1)
                if n < NHD:
                    turn(n)
                if n >= 1:
                    values(n - 1)
                if n % 4 in (0, 2) and n // 4 + 1 < ET:
                    project(n // 4 + 1, n % 4 // 2)
            for t in range(GT):
                pe.wait_ge(s["o"], NU)
                for i in range(2):
                    if t:
                        pe.wait_ge(s["ol"], 2 * t - 1 + i)
                    for m in range(4):
                        k = 4 * i + m
                        ins = pe.transpose(T2[i][:, m * P:(m + 1) * P], ot[:, t, k * P:(k + 1) * P], ident)
                    ins.then_inc(s["oT"], 1)
                pe.wait_ge(s["ol"], 2 * t + 2)
                if t:
                    pe.wait_ge(s["res"], t)
                for k in range(ET):
                    ins = split_matmul(pe, PJ[:, 0:D], [x[:, k, :] for x in o], [w[:, k, :] for w in W["wo"]],
                                       k == 0, k == ET - 1)
                ins.then_inc(s["R"], 1)

        @block.scalar
        def _(act):
            act.wait_ge(s["ctx_in"], 16)
            act.activation(eh[:].rearrange("p (k n) -> p k n", k=KD), cr[:], ACT.Copy).then_inc(s["ch"], 1)
            for n in range(0, NV, 2):
                t, half, bank = n // 2, n % 2, (PJ, *S3)[n % 4]
                act.wait_ge(s["V"], n + 1)
                act.activation(va[:, t, half * 8:half * 8 + 8, 0:XD], bank[:].rearrange("p (h d) -> p h d", h=8),
                               ACT.Copy).then_inc(s["va"], 1)
            for k in range(KD):
                act.wait_ge(s["xnT"], k + 1)
                part_high(act, uh[:, k, :], T2[k][:]).then_inc(s["uh"], 1)

            def place(n):
                j, which = n // 2, n % 2
                act.wait_ge(s["QK"], n + 1)
                if j >= 2:
                    act.wait_ge(s["S"], 4 * (j - 1))
                act.activation((q, k_)[which][:, j % 2, :], PJ[:], ACT.Copy).then_inc(s["qk"], 1)

            place(0)
            place(1)
            for n in range(NHD):
                for qt in range(QT):
                    act.wait_ge(s["sm"], 2 * n + qt + 1)
                    act.activation(pp[:, n % 3, qt, :], pp[:, n % 3, qt, :], ACT.Exp, bias=nm[:, n % 4, qt:qt + 1],
                                   scale=-1.0).then_inc(s["ex"], 1)
                if n % 4 in (0, 2) and n // 4 + 1 < ET:
                    place(2 * (n // 4 + 1) + n % 4 // 2)
            for t in range(GT):
                for i in range(2):
                    act.wait_ge(s["oT"], 2 * t + i + 1)
                    if t:
                        act.wait_ge(s["R"], t)
                    act.activation(o[0][:, 4 * i:4 * i + 4, :], T2[i][:].rearrange("p (k n) -> p k n", k=4),
                                   ACT.Copy).then_inc(s["oh"], 1)

        @block.vector
        def _(dve):
            ch = Chain(dve, s["chain"])
            norm_stats(dve, ch, XG, st, mv, s["var"])
            dve.wait_ge(s["var"], GT)
            inverse_root(dve, ch, rstd[:], mv[:, :, 1], LN_EPS, (nt[:, 0], nt[:, 1]))
            for t in range(GT):
                dve.tensor_scalar(xn[:, t, :], XG[:, t, :], mv[:, t, 0:1], rstd[:, t:t + 1],
                                  ALU.subtract, ALU.mult).then_inc(s["xn"], 1)
            dve.wait_ge(s["ch"], 1)
            dve.tensor_tensor(c[1], cr[:], c[0].bitcast(F32), ALU.subtract).then_inc(s["cl"], 1)
            for n in range(NV):
                if n % 2:
                    t, half, bank = n // 2, n % 2, (PJ, *S3)[n % 4]
                    dve.wait_ge(s["V"], n + 1)
                    dve.tensor_copy(va[:, t, half * 8:half * 8 + 8, 0:XD],
                                    bank[:].rearrange("p (h d) -> p h d", h=8)).then_inc(s["v"], 1)
            for k in range(KD):
                dve.wait_ge(s["uh"], k + 1)
                part_low(dve, ul[:, k, :], T2[k][:], uh[:, k, :]).then_inc(s["ul"], 1)
            dve.wait_ge(s["mask_in"], 16)

            def masked(n):
                b = n // 2 % 2
                dve.wait_ge(s["S"], n + 1)
                if n >= 3:
                    dve.wait_ge(s["T"], n - 2)
                for qt in range(QT):
                    dve.tensor_tensor_reduce(out=pp[:, n % 3, qt, :], in0=S3[n % 3][:, qt * S:(qt + 1) * S],
                                             in1=mask[:, b * QT + qt, :], scale=-1.0, scalar=3e38, op0=ALU.add,
                                             op1=ALU.min, accum_out=nm[:, n % 4, qt:qt + 1]).then_inc(s["sm"], 1)

            def place(n):
                dve.wait_ge(s["T"], n + 1)
                if n >= 2:
                    dve.wait_ge(s["PV"], n - 1)
                dve.tensor_copy(pt[:, n % 2, :], T2[n % 2][:]).then_inc(s["pt"], 1)

            def normalise(u):
                j, b = u // 2, u % 2
                dve.wait_ge(s["PV"], 2 * u + 2)
                src = O2[u % 2][:, 0:4 * VW].rearrange("p (h q d) -> p h q d", h=2, q=QT)
                r = rc[:, u % 2].rearrange("p a b -> p (a b)").rearrange("p (h q) -> p h q", h=2)
                ch.link(dve.reciprocal(r, src[:, :, :, XD]))
                for hp in range(2):
                    h = 2 * j + hp
                    ins = dve.tensor_tensor(ot[:, b * QT:(b + 1) * QT, h * XD:(h + 1) * XD], src[:, hp, :, 0:XD],
                                            r[:, hp, :].unsqueeze(2).to_broadcast([P, QT, XD]), ALU.mult)
                ins.then_inc(s["o"], 1)

            for n in range(NHD + 3):
                if n < NHD:
                    masked(n)
                if 1 <= n <= NHD:
                    place(n - 1)
                if n >= 3 and n % 2:
                    normalise((n - 3) // 2)
            for t in range(GT):
                for i in range(2):
                    dve.wait_ge(s["oh"], 2 * t + i + 1)
                    part_low(dve, o[1][:, 4 * i:4 * i + 4, :], T2[i][:].rearrange("p (k n) -> p k n", k=4),
                             o[0][:, 4 * i:4 * i + 4, :]).then_inc(s["ol"], 1)
                dve.wait_ge(s["R"], t + 1)
                dve.tensor_tensor(XG[:, t, :], XG[:, t, :], PJ[:, 0:D], ALU.add).then_inc(s["res"], 1)
            dve.wait_ge(s["res"], GT)



def stage_attention(nc, ctx, g, I, W, K, XG, scratch, ps, s, last):
    with ExitStack() as own:
        def sb(name, shape, dt=F32):
            return own.enter_context(nc.sbuf_tensor("c_" + name, shape, dt))

        st, mv, rstd, nt = sb("st", [P, GT, 6]), sb("mv", [P, GT, 2]), sb("rstd", [P, GT]), sb("nt", [P, 2, GT])
        ln = sb("ln", [P, GT, D])
        xr = sb("xr", [P, GT, D])
        sq, ss, rs = sb("sq", [P, D]), sb("ss", [P, 2, GT]), sb("rs", [P, GT])
        uh, ul = sb("uh", [P, KD, GN], FR), sb("ul", [P, KD, GN], FR)
        ra, rb = sb("ra", [P, 2, (AH + AKV) * AD]), sb("rb", [P, 2, (AH + AKV) * AD])
        qr = sb("qr", [P, GT, AH * AD])
        kr = sb("kr", [P, GT, AH * AD])
        v = sb("v", [P, GT, AKV, AVW])
        qT = sb("qT", [P, KD, GN])
        kT = sb("kT", [P, KD, 2, REP, S])
        NB = 3
        pp = sb("pp", [P, 4, NB * P])
        nm = sb("nm", [P, 4, QT])
        pt = sb("pt", [P, 4, NB * P])
        rc = sb("rc", [P, 2, 2 * QT])
        ot = sb("ot", [P, GT, AH * AD])
        oh, ol = sb("oh", [P, KD, GN], FR), sb("ol", [P, KD, GN], FR)
        lgf = sb("lgf", [NE, GN])
        lg, ex, rank, tmp, comb = (sb(n, [P, GT, NE]) for n in "lg ex rank tmp comb".split())
        mx, sm = sb("mx", [P, GT]), sb("sm", [P, GT])
        gt, eq = sb("gt", [P, GT, NE, NE]), sb("eq", [P, GT, NE, NE])

        ident = K["const"][:, C_ID:C_ID + P]
        causal = K["const"][:, C_CAUSAL:C_CAUSAL + QT * P]
        low = K["const"][:, C_LOW:C_LOW + NE * NE].rearrange("p (e j) -> p e j", e=NE)
        SB, TB, OB = ps[0:4], ps[4:6], ps[6:8]
        NU = 2 * AH // 2
        NHD = 2 * NU
        PER_B = NU // 2
        block = own.enter_context(nc.Block())

        def where(u):
            b, i = u // PER_B, u % PER_B
            return b, i // 4, i // 2 % 2, i % 2 * 2

        @block.sync
        def _(sp):
            clear(sp, last)
            sp.wait_ge(s["xh"], GT)
            sp.dma_start(scratch["res"][g], XG[:]).then_inc(s["stored"], 16)
            sp.wait_ge(s["l2"], KD)
            sp.dma_start(scratch["h"][g], uh[:].bitcast(F32)).then_inc(s["stored"], 16)
            sp.dma_start(scratch["l"][g], ul[:].bitcast(F32)).then_inc(s["stored"], 16)
            sp.wait_ge(s["comb"], 1)
            sp.dma_start(scratch["comb"][g], comb[:]).then_inc(s["stored"], 16)
            sp.wait_ge(s["stored"], 64)

        @block.gpsimd
        def _(pool):
            pool.memset(v[:, :, :, AD], 1.0).then_inc(s["ones"], 1)

        @block.tensor
        def _(pe):
            pe.wait_ge(s["xr"], GT)
            transposes_in(pe, xr, ident, TB, KD, s["xT"])
            pe.wait_ge(s["ul"], KD)
            for t in range(GT):
                for k in range(KD):
                    ins = split_matmul(pe, SB[t][:, 0:AQKV], (uh[:, k, t * P:(t + 1) * P], ul[:, k, t * P:(t + 1) * P]),
                                       [w[:, k, :] for w in W["aqkv"]], k == 0, k == KD - 1)
                ins.then_inc(s["QKV"], 1)
            pe.wait_ge(s["rot"], 2 * GT)
            transposes_in(pe, qr, ident, TB, KD, s["qT"])
            transposes_in(pe, kr, ident, OB, KD, s["kT"])
            pe.wait_ge(s["kTs"], 2 * KD)

            def scores(u):
                b, j, gp, r = where(u)
                if u == 0:
                    pe.wait_ge(s["qTs"], KD)
                if u >= 2:
                    pe.wait_ge(s["sm"], 4 * (u - 1))
                rows = slice(64 * gp, 64 * gp + 64)
                for qt in range(QT):
                    at = (b * QT + qt) * P
                    n = (qt + 1) * P
                    ins = pe.matmul(SB[u % 2 * 2 + qt][:, 0:2 * n].rearrange("p (r n) -> p r n", r=2),
                                    qT[rows, j, at:at + P], kT[rows, j, b, r:r + 2, 0:n], start=True, stop=True)
                ins.then_inc(s["S"], 1)

            def turn(n):
                pe.wait_ge(s["ex"], 2 * (n + 1))
                if n >= 2:
                    pe.wait_ge(s["pt"], n - 1)
                else:
                    pe.wait_ge(s["qTs"], KD)
                for i in range(NB):
                    ins = pe.transpose(TB[n % 2][:, i * P:(i + 1) * P], pp[:, n % 4, i * P:(i + 1) * P], ident)
                ins.then_inc(s["T"], 1)

            def values(n):
                u, hp = n // 2, n % 2
                b = where(u)[0]
                pe.wait_ge(s["pt"], n + 1)
                if hp == 0 and u >= 2:
                    pe.wait_ge(s["o"], u - 1)
                for qt, i, kt in ((0, 0, 0), (1, 1, 0), (1, 2, 1)):
                    at = (hp * QT + qt) * AKV * AVW
                    ins = pe.matmul(OB[u % 2][:, at:at + AKV * AVW], pt[:, n % 4, i * P:(i + 1) * P],
                                    v[:, b * QT + kt].rearrange("p a b -> p (a b)"), start=kt == 0, stop=kt == qt)
                ins.then_inc(s["PV"], 1)

            pe.wait_ge(s["ones"], 1)
            scores(0)
            for u in range(NU + 1):
                if u + 1 < NU:
                    scores(u + 1)
                for hp in range(2):
                    if u < NU:
                        turn(2 * u + hp)
                    if u >= 1:
                        values(2 * (u - 1) + hp)
            pe.wait_ge(s["o"], NU)
            transposes_in(pe, ot, ident, TB, KD, s["oT"])
            pe.wait_ge(s["ol"], KD)
            for t in range(GT):
                for k in range(KD):
                    ins = split_matmul(pe, SB[t][:, 0:D], (oh[:, k, t * P:(t + 1) * P], ol[:, k, t * P:(t + 1) * P]),
                                       [w[:, k, :] for w in W["awo"]], k == 0, k == KD - 1)
                ins.then_inc(s["R"], 1)
            pe.wait_ge(s["xr2"], GT)
            transposes_in(pe, xr, ident, TB, KD, s["x2T"])
            pe.wait_ge(s["l2"], KD)
            for k in range(KD):
                ins = split_matmul(pe, OB[0][0:NE, :], [w[:, k, :] for w in W["gate"]], (uh[:, k, :], ul[:, k, :]),
                                   k == 0, k == KD - 1)
            ins.then_inc(s["G"], 1)
            pe.wait_ge(s["lgf"], 1)
            for t in range(GT):
                ins = pe.transpose(OB[1][:, t * NE:(t + 1) * NE], lgf[:, t * P:(t + 1) * P], ident[0:NE, 0:NE])
            ins.then_inc(s["GT"], 1)

        @block.scalar
        def _(act):
            def squares(which, ready):
                for t in range(GT):
                    act.wait_ge(ready, t + 1)
                    if which or t:
                        act.wait_ge(s["ss"], which * GT + t)
                    act.activation(sq[:], ln[:, t, :], ACT.Square, accum_out=ss[:, which, t:t + 1]).then_inc(s["ss"], 1)

            squares(0, s["ln"])
            for k in range(KD):
                act.wait_ge(s["xT"], k + 1)
                part_high(act, uh[:, k, :], TB[k][:], K["g1"][:, k:k + 1]).then_inc(s["uh"], 1)
            for k in range(KD):
                act.wait_ge(s["qT"], k + 1)
                act.activation(qT[:, k, :], TB[k][:], ACT.Copy).then_inc(s["qTs"], 1)
            for n in range(NHD):
                u, hp = n // 2, n % 2
                act.wait_ge(s["sm"], 2 * n + 1)
                act.activation(pp[:, n % 4, 0:P], pp[:, n % 4, 0:P], ACT.Exp, bias=nm[:, n % 4, 0:1],
                               scale=-1.0).then_inc(s["ex"], 1)
                act.wait_ge(s["sm"], 2 * n + 2)
                act.activation(pp[:, n % 4, P:NB * P], pp[:, n % 4, P:NB * P], ACT.Exp, bias=nm[:, n % 4, 1:2],
                               scale=-1.0).then_inc(s["ex"], 1)
            for k in range(KD):
                act.wait_ge(s["oT"], k + 1)
                part_high(act, oh[:, k, :], TB[k][:]).then_inc(s["oh"], 1)
            squares(1, s["h"])
            for k in range(KD):
                act.wait_ge(s["x2T"], k + 1)
                part_high(act, uh[:, k, :], TB[k][:], K["g2"][:, k:k + 1]).then_inc(s["h2"], 1)
            act.wait_ge(s["G"], 1)
            act.activation(lgf[:], OB[0][0:NE, :], ACT.Copy).then_inc(s["lgf"], 1)
            act.wait_ge(s["lgm"], 1)
            act.activation(ex[:], ex[:], ACT.Exp).then_inc(s["gex"], 1)

        @block.vector
        def _(dve):
            ch = Chain(dve, s["chain"])

            def root_mean(which):
                dve.wait_ge(s["ss"], (which + 1) * GT)
                inverse_root(dve, ch, rs[:], ss[:, which, :], D * RMS_EPS, (nt[:, 0], nt[:, 1]))
                for t in range(GT):
                    dve.tensor_scalar(xr[:, t, :], ln[:, t, :], rs[:, t:t + 1], float(D) ** 0.5,
                                      ALU.mult, ALU.mult).then_inc((s["xr"], s["xr2"])[which], 1)

            norm_stats(dve, ch, XG, st, mv, s["var"])
            dve.wait_ge(s["var"], GT)
            inverse_root(dve, ch, rstd[:], mv[:, :, 1], LN_EPS, (nt[:, 0], nt[:, 1]))
            for t in range(GT):
                dve.tensor_scalar(ln[:, t, :], XG[:, t, :], mv[:, t, 0:1], rstd[:, t:t + 1],
                                  ALU.subtract, ALU.mult).then_inc(s["ln"], 1)
            root_mean(0)
            for k in range(KD):
                dve.wait_ge(s["uh"], k + 1)
                part_low(dve, ul[:, k, :], TB[k][:], uh[:, k, :], K["g1"][:, k:k + 1]).then_inc(s["ul"], 1)
            HALF, NR = AD // 2, AH + AKV

            def table(t, i):
                return K["rope"][:, t % QT, i, :].unsqueeze(1).to_broadcast([P, NR, HALF])

            for t in range(GT):
                dve.wait_ge(s["QKV"], t + 1)
                src = SB[t][:, 0:NR * AD].rearrange("p (h d) -> p h d", d=AD)
                a = ra[:, t % 2].rearrange("p (h d) -> p h d", d=AD)
                b = rb[:, t % 2].rearrange("p (h d) -> p h d", d=AD)
                if t >= 2:
                    dve.wait_ge(s["rot"], 2 * (t - 1))
                ch.then(dve.tensor_tensor(a[:, :, 0:HALF], src[:, :, 0:HALF], table(t, 0), ALU.mult))
                ch.then(dve.tensor_tensor(a[:, :, HALF:AD], src[:, :, HALF:AD], table(t, 0), ALU.mult))
                ch.then(dve.tensor_tensor(b[:, :, 0:HALF], src[:, :, HALF:AD], table(t, 1), ALU.mult))
                ch.then(dve.tensor_tensor(b[:, :, HALF:AD], src[:, :, 0:HALF], table(t, 2), ALU.mult))
                ch.then(dve.tensor_copy(v[:, t, :, 0:AD],
                                        SB[t][:, NR * AD:AQKV].rearrange("p (h d) -> p h d", d=AD)))
                ch.sync()
                dve.tensor_tensor(qr[:, t, :], ra[:, t % 2, 0:AH * AD], rb[:, t % 2, 0:AH * AD], ALU.add).then_inc(s["rot"], 1)
                dve.tensor_tensor(kr[:, t, :].rearrange("p (g r d) -> p g r d", g=AKV, r=REP),
                                  a[:, AH:NR, :].unsqueeze(2).to_broadcast([P, AKV, REP, AD]),
                                  b[:, AH:NR, :].unsqueeze(2).to_broadcast([P, AKV, REP, AD]), ALU.add).then_inc(s["rot"], 1)
            for k in range(KD):
                dve.wait_ge(s["kT"], k + 1)
                for b in range(2):
                    for r in range(REP):
                        ins = dve.tensor_scalar(kT[:, k, b, r, :], OB[k][:, b * S:(b + 1) * S],
                                                K["const"][:, C_ROW + r:C_ROW + r + 1], None, ALU.mult)
                    ins.then_inc(s["kTs"], 1)

            def masked(n):
                u, hp = n // 2, n % 2
                if hp == 0:
                    dve.wait_ge(s["S"], u + 1)
                if n >= 4:
                    dve.wait_ge(s["T"], n - 3)
                for qt in range(QT):
                    bank = SB[u % 2 * 2 + qt]
                    w = (qt + 1) * P
                    src, out = bank[:, hp * w:(hp + 1) * w], pp[:, n % 4, qt * P:qt * P + w]
                    dve.tensor_tensor_reduce(out=out, in0=src, in1=causal[:, (QT - 1 - qt) * P:QT * P], scale=-AD ** -0.5,
                                             scalar=3e38, op0=ALU.add, op1=ALU.min,
                                             accum_out=nm[:, n % 4, qt:qt + 1]).then_inc(s["sm"], 1)

            def place(n):
                dve.wait_ge(s["T"], n + 1)
                if n >= 4:
                    dve.wait_ge(s["PV"], n - 3)
                dve.tensor_copy(pt[:, n % 4, :], TB[n % 2][:, 0:NB * P]).then_inc(s["pt"], 1)

            def normalise(u):
                b, j, gp, r = where(u)
                kv, h = 2 * j + gp, (2 * j + gp) * REP + r
                dve.wait_ge(s["PV"], 2 * u + 2)
                src = OB[u % 2][:, 0:2 * QT * AKV * AVW].rearrange("p (h q d) -> p h q d", h=2, q=QT)
                o = rc[:, u % 2].rearrange("p (h q) -> p h q", h=2)
                ch.link(dve.reciprocal(o, src[:, :, :, kv * AVW + AD]))
                dve.tensor_tensor(ot[:, b * QT:(b + 1) * QT, h * AD:(h + 2) * AD].rearrange("p q (h d) -> p h q d", h=2),
                                  src[:, :, :, kv * AVW:kv * AVW + AD],
                                  o.unsqueeze(3).to_broadcast([P, 2, QT, AD]), ALU.mult).then_inc(s["o"], 1)

            for u in range(NU + 2):
                if u < NU:
                    masked(2 * u)
                    masked(2 * u + 1)
                if 1 <= u <= NU:
                    place(2 * u - 2)
                    place(2 * u - 1)
                if u >= 2:
                    normalise(u - 2)
            for k in range(KD):
                dve.wait_ge(s["oh"], k + 1)
                part_low(dve, ol[:, k, :], TB[k][:], oh[:, k, :]).then_inc(s["ol"], 1)
            for t in range(GT):
                dve.wait_ge(s["R"], t + 1)
                dve.tensor_tensor(ln[:, t, :], ln[:, t, :], SB[t][:, 0:D], ALU.add).then_inc(s["h"], 1)
            for t in range(GT):
                dve.wait_ge(s["h"], t + 1)
                dve.tensor_tensor(XG[:, t, :], XG[:, t, :], ln[:, t, :], ALU.add).then_inc(s["xh"], 1)
            root_mean(1)
            for k in range(KD):
                dve.wait_ge(s["h2"], k + 1)
                part_low(dve, ul[:, k, :], TB[k][:], uh[:, k, :], K["g2"][:, k:k + 1]).then_inc(s["l2"], 1)
            dve.wait_ge(s["GT"], 1)
            ch.link(dve.tensor_copy(lg[:], OB[1][:, 0:GT * NE].rearrange("p (t e) -> p t e", t=GT)))
            ch.link(dve.tensor_reduce(mx[:], lg[:], AX_X, ALU.max))
            dve.tensor_tensor(ex[:], lg[:], mx[:].unsqueeze(2).to_broadcast([P, GT, NE]), ALU.subtract).then_inc(s["lgm"], 1)
            dve.wait_ge(s["gex"], 1)
            mine = ex[:].unsqueeze(3).to_broadcast([P, GT, NE, NE])
            other = ex[:].unsqueeze(2).to_broadcast([P, GT, NE, NE])
            ch.then(dve.tensor_tensor(gt[:], other, mine, ALU.is_gt))
            ch.link(dve.tensor_tensor(eq[:], other, mine, ALU.is_equal))
            ch.link(dve.tensor_tensor(eq[:], eq[:], low.unsqueeze(1).to_broadcast([P, GT, NE, NE]), ALU.mult))
            ch.link(dve.tensor_tensor(gt[:], gt[:], eq[:], ALU.add))
            ch.link(dve.tensor_reduce(rank[:], gt[:], AX_X, ALU.add))
            ch.link(dve.scalar_tensor_tensor(out=tmp[:], in0=rank[:], scalar=1.5, in1=ex[:], op0=ALU.is_lt, op1=ALU.mult))
            ch.link(dve.tensor_reduce(sm[:], tmp[:], AX_X, ALU.add))
            ch.link(dve.reciprocal(sm[:], sm[:]))
            dve.scalar_tensor_tensor(out=comb[:], in0=tmp[:], scalar=0.5, in1=sm[:].unsqueeze(2).to_broadcast([P, GT, NE]),
                                     op0=ALU.mult, op1=ALU.mult).then_inc(s["comb"], 1)



def stage_experts(nc, ctx, I, K, scratch, out, ps, s):
    with ExitStack() as own:
        def sb(name, shape, dt=F32):
            return own.enter_context(nc.sbuf_tensor("e_" + name, shape, dt))

        acc = sb("acc", [P, NG, GT, D])
        yh, yl = sb("yh", [P, NG, KD, GN], FR), sb("yl", [P, NG, KD, GN], FR)
        comb = sb("comb", [P, NG, GT, NE])
        now = sb("now", [P, NG, GT])
        raw = [sb("raw1", [P, KD, HID]), sb("raw3", [P, KD, HID]), sb("raw2", [P, HT, D])]
        w1, w3, w2 = ((sb(n + "h", shape, FR), sb(n + "l", shape, FR)) for n, shape in
                      (("w1", [P, KD, HID]), ("w3", [P, KD, HID]), ("w2", [P, HT, D])))
        th, p3 = sb("th", [P, 2, GN]), sb("p3", [P, 2, GN])
        hh, hl = sb("hh", [P, 2, HT, GN], FR), sb("hl", [P, 2, HT, GN], FR)
        NH_ = NG * HT
        U1, U3, DN = ps[0:2], ps[2:4], ps[4:8]

        with nc.Block() as block:
            @block.sync
            def _(sp):
                for t, src in ((acc[:], scratch["res"]), (yh[:].bitcast(F32), scratch["h"]), (yl[:].bitcast(F32), scratch["l"])):
                    sp.dma_start(t.rearrange("p g a b -> p g (a b)"),
                                 src.rearrange("g p a b -> p g (a b)")).then_inc(s["first"], 16)
                sp.dma_start(comb[:].rearrange("p g a b -> p g (a b)"),
                             scratch["comb"].rearrange("g p a b -> p g (a b)")).then_inc(s["first"], 16)
                sp.wait_ge(s["first"], 64)

        with nc.Fori(0, NE) as e:
            with nc.Block() as block:
                @block.sync
                def _(sp):
                    for t, src, sem in zip(raw, (I["w1"], I["w3"], I["w2"]), (s["raw1"], s["raw3"], s["raw2"])):
                        sp.dma_start(t[:], src[e]).then_inc(sem, 16)

                def high(act, n):
                    g, m = n // HT, n % HT
                    act.wait_ge(s["p"], n + 1)
                    if g >= 2:
                        act.wait_ge(s["D"], GT * (g - 1))
                    act.activation(hh[:, g % 2, m, :], p3[:, n % 2, :], ACT.Copy).then_inc(s["hh"], 1)

                @block.scalar
                def _(act):
                    for r, w, sem in zip(raw, (w1, w3, w2), (s["raw1"], s["raw3"], s["raw2"])):
                        act.wait_ge(sem, 16)
                        act.activation(w[0][:], r[:], ACT.Copy).then_inc(s["wh"], 1)
                    for n in range(NH_):
                        act.wait_ge(s["U"], n + 1)
                        if n >= 2:
                            act.wait_ge(s["p"], n - 1)
                        act.activation(th[:, n % 2, :], U1[n % 2][:], ACT.Tanh, scale=0.5).then_inc(s["th"], 1)
                        if n >= 1:
                            high(act, n - 1)
                    high(act, NH_ - 1)

                @block.vector
                def _(dve):
                    for i, (r, w) in enumerate(zip(raw, (w1, w3, w2))):
                        dve.wait_ge(s["wh"], i + 1)
                        dve.tensor_tensor(w[1][:], r[:], w[0][:].bitcast(F32), ALU.subtract).then_inc(s["wl"], 1)
                    dve.tensor_copy(now[:], comb[:, :, :, bass.ds(e, 1)].rearrange("p g t o -> p g (t o)")).then_inc(s["now"], 1)
                    dve.wait_ge(s["now"], 1)

                    def hidden(n):
                        dve.wait_ge(s["th"], n + 1)
                        if n >= 2:
                            dve.wait_ge(s["hl"], n - 1)
                        dve.scalar_tensor_tensor(out=th[:, n % 2, :], in0=th[:, n % 2, :], scalar=1.0, in1=U1[n % 2][:],
                                                 op0=ALU.add, op1=ALU.mult).then_inc(s["q"], 1)
                        dve.wait_ge(s["q"], n + 1)
                        dve.tensor_tensor(p3[:, n % 2, :], th[:, n % 2, :], U3[n % 2][:], ALU.mult).then_inc(s["p"], 1)

                    def low(n):
                        g, m = n // HT, n % HT
                        dve.wait_ge(s["hh"], n + 1)
                        dve.tensor_tensor(hl[:, g % 2, m, :], p3[:, n % 2, :], hh[:, g % 2, m, :].bitcast(F32),
                                          ALU.subtract).then_inc(s["hl"], 1)

                    def add(g):
                        for t in range(GT):
                            i = g * GT + t
                            dve.wait_ge(s["D"], i + 1)
                            dve.scalar_tensor_tensor(out=acc[:, g, t, :], in0=DN[t][:, 0:D], scalar=now[:, g, t:t + 1],
                                                     in1=acc[:, g, t, :], op0=ALU.mult, op1=ALU.add).then_inc(s["acc"], 1)

                    for n in range(NH_ + 1):
                        if n < NH_:
                            hidden(n)
                        if n >= 1:
                            low(n - 1)
                        if n % HT == 2 and n // HT >= 1:
                            add(n // HT - 1)
                    add(NG - 1)
                    dve.wait_ge(s["acc"], NG * GT)

                @block.tensor
                def _(pe):
                    def up(n):
                        g, m = n // HT, n % HT
                        if n >= 2:
                            pe.wait_ge(s["p"], n - 1)
                        for w, bank in ((w1, U1[n % 2]), (w3, U3[n % 2])):
                            if n == 0:
                                pe.wait_ge(s["wl"], 1 if w is w1 else 2)
                            for k in range(KD):
                                ins = split_matmul(pe, bank[:], [x[:, k, m * P:(m + 1) * P] for x in w],
                                                   (yh[:, g, k, :], yl[:, g, k, :]), k == 0, k == KD - 1)
                        ins.then_inc(s["U"], 1)

                    def down(g):
                        if g == 0:
                            pe.wait_ge(s["wl"], 3)
                        pe.wait_ge(s["hl"], HT * (g + 1))
                        for t in range(GT):
                            if g:
                                pe.wait_ge(s["acc"], GT * (g - 1) + t + 1)
                            for m in range(HT):
                                ins = split_matmul(pe, DN[t][:, 0:D], (hh[:, g % 2, m, t * P:(t + 1) * P],
                                                                       hl[:, g % 2, m, t * P:(t + 1) * P]),
                                                   [x[:, m, :] for x in w2], m == 0, m == HT - 1)
                            ins.then_inc(s["D"], 1)

                    for n in range(NH_):
                        up(n)
                        if n % HT == 1 and n // HT >= 1:
                            down(n // HT - 1)
                    down(NG - 1)

            with nc.Block() as block:
                @block.sync
                def _(sp):
                    clear(sp, s)

        with nc.Block() as block:
            @block.sync
            def _(sp):
                sp.dma_start(out.rearrange("(g t p) d -> p g t d", p=P, t=GT), acc[:]).then_inc(s["out"], 16)
                sp.wait_ge(s["out"], 16)

SEM_A = ("x_in var xn xnT uh ul J Jfree cv conv th xs zt dtf dtT nv e a chain av D L small dec SM xT dx xd M xdd "
         "Y y YO yo yg ss yn yT yh yl O res")
SEM_B = ("ctx_in mask_in ones cl v V xn xnT uh ul qk QK sm S ex pt T o PV ol oT oh res R ch va var chain")
SEM_C = ("x_in xh stored l2 comb ones xr xT ul uh QKV rot qT kT kTs qTs sm S ex pt T o PV oT ol R xr2 x2T G lgf GT ln ss oh h h2 "
         "lgm gex var chain")
SEM_E = "first raw1 raw3 raw2 now wh wl U th q p hh hl D acc out"



def decoder_layer(nc, I, out):
    with ExitStack() as ctx:
        def sb(name, shape, dt=F32):
            return ctx.enter_context(nc.sbuf_tensor(name, shape, dt))

        ps = [ctx.enter_context(nc.psum_tensor(f"bank{i}", [P, 512], F32)) for i in range(8)]
        K = {"const": sb("const", [P, C_N])}
        scratch = dict(
            res=nc.dram_tensor("residual", (NG, P, GT, D), F32, kind="Internal").ap(),
            h=nc.dram_tensor("x2_high", (NG, P, KD, GN), F32, kind="Internal").ap(),
            l=nc.dram_tensor("x2_low", (NG, P, KD, GN), F32, kind="Internal").ap(),
            comb=nc.dram_tensor("combine", (NG, P, GT, NE), F32, kind="Internal").ap())
        sA = semaphores(nc, ctx, "a", SEM_A)
        sB = semaphores(nc, ctx, "b", SEM_B)
        sC = semaphores(nc, ctx, "c", SEM_C)
        sE = semaphores(nc, ctx, "e", SEM_E)
        with ExitStack() as attn:
            def sb(name, shape, dt=F32):
                return attn.enter_context(nc.sbuf_tensor(name, shape, dt))

            K["rope"], K["taps"], K["tapb"], K["nw"] = sb("rope", [P, QT, 3, AD // 2]), sb("taps", [P, CT, TAPS]), sb("tapb", [P, CT]), sb("nw", [P, XT])
            K["g1"], K["g2"] = sb("g1", [P, KD]), sb("g2", [P, KD])
            K["dtb"], K["alog"], K["A"], K["dpar"] = sb("dtb", [P, NH]), sb("alog", [P, NH]), sb("A", [P, NH]), sb("dpar", [P, NH])
            W = {}
            for n, shape in (("win", [P, KD, PROJ]), ("wout", [P, XT, D]), ("wq", [P, KD, XI]), ("wk", [P, KD, XI]),
                             ("wv", [P, KD, XI]), ("wo", [P, ET, D]), ("aqkv", [P, KD, AQKV]), ("awo", [P, KD, D]),
                             ("gate", [P, KD, NE])):
                W[n] = (sb(n + "_high", shape, FR), sb(n + "_low", shape, FR))
            XG = sb("XG", [P, GT, D])
            load_weights(nc, ctx, I, W, K)
            with nc.Fori(0, NG) as g:
                stage_mamba(nc, ctx, g, I, W, K, XG, ps, sA, sC)
                stage_cross(nc, ctx, g, I, W, K, XG, ps, sB, sA)
                stage_attention(nc, ctx, g, I, W, K, XG, scratch, ps, sC, sB)
        stage_experts(nc, ctx, I, K, scratch, out, ps, sE)


def kernel(x, ctx_1024, fside_Bx1xSxS2_0, L0_attn_in_proj_w, L0_attn_conv_weight, L0_attn_conv_bias, L0_attn_dt_bias,
           L0_attn_A_log, L0_attn_D_param, L0_attn_norm_weight, L0_attn_out_proj_w, L0_xattn_Wq, L0_xattn_Wk,
           L0_xattn_Wv, L0_xattn_Wo, L0_ffn_g1, L0_ffn_g2, L0_ffn_wq, L0_ffn_wk, L0_ffn_wv, L0_ffn_wo, L0_ffn_gate,
           L0_ffn_w1, L0_ffn_w2, L0_ffn_w3):
    import numpy as _np
    import concourse.bacc as _bacc
    from concourse.bass_utils import run_bass_kernel_spmd as _run

    def rows(w):
        w = _np.asarray(w)
        return w.reshape(w.shape[0] // P, P, -1).transpose(1, 0, 2)

    def every(v):
        return _np.broadcast_to(_np.asarray(v), (P, _np.shape(v)[0]))

    laid = {
        "x": _np.asarray(x).reshape(NG, GT, P, D).transpose(0, 2, 1, 3),
        "ctxT": _np.asarray(ctx_1024).reshape(NG, GN, KD, P).transpose(0, 3, 2, 1),
        "mask": _np.asarray(fside_Bx1xSxS2_0).reshape(NG, GT, P, S).transpose(0, 2, 1, 3),
        "win": rows(L0_attn_in_proj_w), "wout": rows(L0_attn_out_proj_w),
        "taps": _np.asarray(L0_attn_conv_weight).reshape(CT, P, TAPS).transpose(1, 0, 2),
        "tapb": _np.asarray(L0_attn_conv_bias).reshape(CT, P).T,
        "nw": _np.asarray(L0_attn_norm_weight).reshape(XT, P).T,
        "dtb": every(L0_attn_dt_bias), "alog": every(L0_attn_A_log), "dpar": every(L0_attn_D_param),
        "wq": rows(_np.asarray(L0_xattn_Wq).T), "wk": rows(_np.asarray(L0_xattn_Wk).T), "wv": rows(_np.asarray(L0_xattn_Wv).T),
        "wo": rows(_np.asarray(L0_xattn_Wo).T),
        "aqkv": _np.concatenate([rows(L0_ffn_wq), rows(L0_ffn_wk), rows(L0_ffn_wv)], axis=2),
        "awo": rows(L0_ffn_wo), "gate": rows(L0_ffn_gate),
        "g1": _np.asarray(L0_ffn_g1).reshape(KD, P).T, "g2": _np.asarray(L0_ffn_g2).reshape(KD, P).T,
        "w1": _np.stack([rows(w) for w in _np.asarray(L0_ffn_w1)]), "w3": _np.stack([rows(w) for w in _np.asarray(L0_ffn_w3)]),
        "w2": _np.stack([rows(w) for w in _np.asarray(L0_ffn_w2)]),
        "const": constants(), "rope": rope_tables(),
    }
    nc = _bacc.Bacc("TRN2", target_bir_lowering=False, num_devices=1)
    arrays = {f"in_{n}": _np.ascontiguousarray(a) for n, a in laid.items()}
    I = {n: nc.dram_tensor(f"in_{n}", a.shape, F32, kind="ExternalInput").ap()
                           for n, a in ((n, arrays[f"in_{n}"]) for n in laid)}
    out = nc.dram_tensor("out", (TOK, D), F32, kind="ExternalOutput").ap()
    decoder_layer(nc, I, out)
    r = _run(nc, [arrays], core_ids=[0])
    return r.results[0]["out"].reshape(B, S, D)
```

```python
from contextlib import ExitStack

import numpy as np
import concourse.bass as bass
from concourse import mybir

F32 = mybir.dt.float32
I32 = mybir.dt.int32
FR = mybir.dt.float32r
ALU = mybir.AluOpType
ACT = mybir.ActivationFunctionType
AX_X = mybir.AxisListType.X

P = 128
B, S, D = 8, 256, 256
KD = D // P
TOK = B * S
GT = 4
NG = TOK // (P * GT)
GN = GT * P
QT = S // P

DI, NST, NH, HD, TAPS = 512, 128, 8, 64, 4
XT = DI // P
CT = XT + 2
PROJ = 2 * DI + 2 * NST + NH
LN_EPS, SSM_EPS = 1e-5, 1e-5

XH, XD = 16, 64
XI = XH * XD
ET = XI // P
VW = XD + 1

AH, AKV, AD = 16, 4, 16
REP = AH // AKV
AQKV = (AH + 2 * AKV) * AD
AVW = AD + 1
RMS_EPS = 1.1920928955078125e-07

NE, HID = 4, 3 * D
HT = HID // P

NEG = -1e30

C_ID, C_UPTO, C_AFTER, C_CAUSAL, C_ROW, C_LOW = 0, 128, 256, 384, 640, 644
C_N = C_LOW + NE * NE


def constants():
    c = np.zeros((P, C_N), np.float32)
    i = np.arange(P)
    c[:, C_ID:C_ID + P] = np.eye(P)
    c[:, C_UPTO:C_UPTO + P] = i[:, None] <= i[None, :]
    c[:, C_AFTER:C_AFTER + P] = i[:, None] > i[None, :]
    c[:, C_CAUSAL + P:C_CAUSAL + 2 * P] = np.where(i[None, :] > i[:, None], NEG, 0.0)
    c[:, C_ROW:C_ROW + REP] = (i[:, None] % (REP * AD)) // AD == np.arange(REP)[None, :]
    e = np.arange(NE)
    c[:, C_LOW:] = (e[None, :] < e[:, None]).reshape(1, NE * NE)
    return c


def rope_tables():
    inv = (1.0 / np.float32(10000.0) ** (np.arange(0, AD, 2, dtype=np.float32) / np.float32(AD))).astype(np.float32)
    ang = np.arange(S, dtype=np.float32)[:, None] * inv[None, :]
    t = np.stack([np.cos(ang), -np.sin(ang), np.sin(ang)], axis=1).astype(np.float32)
    return np.ascontiguousarray(t.reshape(QT, P, 3, AD // 2).transpose(1, 0, 2, 3))


def semaphores(nc, ctx, stage, names):
    return {n: ctx.enter_context(nc.semaphore(f"{stage}_{n}")) for n in names.split()}


def clear(sp, sems):
    for s in sems.values():
        sp.sem_clear(s)


def split_matmul(pe, out, a, b, start, stop):
    (ah, al), (bh, bl) = a, b
    pe.matmul(out, ah, bl, start=start, stop=False)
    pe.matmul(out, al, bh, start=False, stop=False)
    return pe.matmul(out, ah, bh, start=False, stop=stop)


class Chain:

    def __init__(self, eng, sem):
        self.eng, self.sem, self.n = eng, sem, 0

    def then(self, ins):
        self.n += 1
        ins.then_inc(self.sem, 1)

    def sync(self):
        if self.n:
            self.eng.wait_ge(self.sem, self.n)

    def link(self, ins):
        self.then(ins)
        self.sync()



def moments(dve, ch, src, st, mv):
    ch.link(dve.bn_stats(st, src))
    ch.then(dve.bn_aggr(mv, st))


def inverse_root(dve, ch, out, var, eps, tmp):
    hv, t = tmp
    ch.link(dve.tensor_scalar(t, var, eps, None, ALU.add))
    ch.then(dve.tensor_scalar(hv, t, -0.5, None, ALU.mult))
    ch.link(dve.tensor_scalar(out.bitcast(I32), t.bitcast(I32), 1, None, ALU.logical_shift_right))
    ch.link(dve.tensor_scalar(out.bitcast(I32), out.bitcast(I32), -1.0, float(0x5F3759DF), ALU.mult, ALU.add))
    for _ in range(3):
        ch.link(dve.tensor_tensor(t, out, out, ALU.mult))
        ch.link(dve.tensor_tensor(t, t, hv, ALU.mult))
        ch.link(dve.scalar_tensor_tensor(out=out, in0=t, scalar=1.5, in1=out, op0=ALU.add, op1=ALU.mult))


def transposes_in(pe, src, ident, banks, tiles, ready, done):
    for t in range(GT):
        pe.wait_ge(ready, t + 1)
        for k in range(tiles):
            ins = pe.transpose(banks[k][:, t * P:(t + 1) * P], src[:, t, k * P:(k + 1) * P], ident)
            if t == GT - 1:
                ins.then_inc(done, 1)


def part_high(act, out, psum, scale=None):
    if scale is None:
        return act.activation(out, psum, ACT.Copy)
    return act.activation(out, psum, ACT.Identity, scale=scale)


def part_low(dve, out, psum, high, scale=None):
    return dve.scalar_tensor_tensor(out=out, in0=psum, scalar=1.0 if scale is None else scale,
                                    in1=high.bitcast(F32), op0=ALU.mult, op1=ALU.subtract)



def load_weights(nc, ctx, I, W, K, XN):
    s = semaphores(nc, ctx, "w", "x_in chain identr const high low misc alog zero")
    raws = [("win", I["win"]), ("wout", I["wout"]), ("wq", I["wq"]), ("wk", I["wk"]), ("wv", I["wv"]), ("wo", I["wo"]),
            ("aqkv", I["aqkv"]), ("awo", I["awo"])]
    loaded = {n: ctx.enter_context(nc.semaphore(f"w_{n}")) for n, _ in raws}
    with ExitStack() as own:
        raw = {n: own.enter_context(nc.sbuf_tensor(f"raw_{n}", list(src.shape), F32)) for n, src in raws}
        block = own.enter_context(nc.Block())

        @block.sync
        def _(sp):
            sp.dma_start(XN[:], I["x"][0]).then_inc(s["x_in"], 16)
            for n, src in raws:
                sp.dma_start(raw[n][:], src).then_inc(loaded[n], 16)
            sp.wait_ge(s["x_in"], 16)

        @block.scalar
        def _(act):
            act.dma_start(K["const"][:], I["const"]).then_inc(s["const"], 16)
            for out, src in ((K["rope"], I["rope"]), (K["taps"], I["taps"]), (K["tapb"], I["tapb"]), (K["nw"], I["nw"]), (K["g1"], I["g1"]), (K["g2"], I["g2"]),
                             (K["dtb"], I["dtb"]), (K["alog"], I["alog"]), (K["dpar"], I["dpar"])):
                act.dma_start(out[:], src).then_inc(s["misc"], 16)
            for n, _ in raws:
                act.wait_ge(loaded[n], 16)
                act.activation(W[n][0][:], raw[n][:], ACT.Copy).then_inc(s["high"], 1)
            act.wait_ge(s["const"], 16)
            act.activation(K["identr"][:], K["const"][:, C_ID:C_ID + P], ACT.Copy).then_inc(s["identr"], 1)
            act.wait_ge(s["misc"], 144)
            act.activation(K["alog"][:], K["alog"][:], ACT.Exp).then_inc(s["alog"], 1)

        @block.vector
        def _(dve):
            for i, (n, _) in enumerate(raws):
                dve.wait_ge(s["high"], i + 1)
                dve.tensor_tensor(W[n][1][:], raw[n][:], W[n][0][:].bitcast(F32), ALU.subtract).then_inc(s["low"], 1)
            dve.wait_ge(s["alog"], 1)
            dve.tensor_scalar(K["A"][:], K["alog"][:], -1.0, None, ALU.mult).then_inc(s["zero"], 1)
            dve.tensor_scalar(K["taps"][:], K["taps"][:], 0.5, None, ALU.mult).then_inc(s["zero"], 1)
            dve.tensor_scalar(K["tapb"][:], K["tapb"][:], 0.5, None, ALU.mult).then_inc(s["zero"], 1)
            dve.tensor_scalar(K["nw"][:], K["nw"][:], float(DI) ** 0.5, None, ALU.mult).then_inc(s["zero"], 1)
            dve.wait_ge(s["const"], 16)
            ch = Chain(dve, s["chain"])
            dve.wait_ge(s["x_in"], 16)
            for t in range(GT):
                moments(dve, ch, XN[:, t, :], K["stats"][:, t, :], K["moments_n"][:, t, :])
            ch.sync()
    return s



def stage_mamba(nc, ctx, g, I, W, K, XN, XG, CX, ps, s, last):
    with ExitStack() as own:
        def sb(name, shape, dt=F32):
            return own.enter_context(nc.sbuf_tensor("a_" + name, shape, dt))

        st, rstd, nt = sb("st", [P, GT, 6]), sb("rstd", [P, GT]), sb("nt", [P, 2, GT])
        mv = K["moments_n"]
        xn = sb("xn", [P, GT, D])
        uh, ul = sb("uh", [P, KD, GN], FR), sb("ul", [P, KD, GN], FR)
        cv, th = sb("cv", [P, 2, GN]), sb("th", [P, 2, GN])
        xs = sb("xs", [P, CT, GN])
        zg = sb("zg", [P, GT, DI])
        dtf = sb("dtf", [NH, GN])
        v, r, e, den, zz, z2, acc, dt, a = (sb(n, [P, GT, NH]) for n in "v r e den zz z2 acc dt a".split())
        av = sb("av", [P, 2, NH, P])
        lm = sb("lm", [P, 2, NH, P])
        gm = sb("gm", [P, 2, P])
        g01 = sb("g01", [P, P])
        dec = sb("dec", [P, GT, NH])
        xd = sb("xd", [P, 2, DI])
        xdd = sb("xdd", [P, DI])
        y = sb("y", [P, GT, DI])
        yo, sq = cv[:, 0, :], th[:, 0, :]
        ss, rs = sb("ss", [P, GT]), sb("rs", [P, GT])
        yh, yl = sb("yh", [P, 2, XT, P], FR), sb("yl", [P, 2, XT, P], FR)

        T, J, DB, YO, SM = ps[0:2], ps[2:4], ps[4:6], ps[6], ps[7]
        ident = K["const"][:, C_ID:C_ID + P]
        upto, after = K["const"][:, C_UPTO:C_UPTO + P], K["const"][:, C_AFTER:C_AFTER + P]
        ORDER = [XT, XT + 1, *range(XT)]
        HH = NH // 2
        block = own.enter_context(nc.Block())

        @block.sync
        def _(sp):
            sp.dma_start(CX[0][:], I["ctxT"][g]).then_inc(s["next_ctx"], 16)
            sp.dma_start(CX[1][:], I["mask"][g]).then_inc(s["next_mask"], 16)
            clear(sp, last)
            sp.wait_ge(s["next_ctx"], 16)
            sp.wait_ge(s["next_mask"], 16)

        @block.gpsimd
        def _(pool):
            pool.wait_ge(s["a"], 1)
            for t in range(GT):
                if t >= 2:
                    pool.wait_ge(s["D"], t - 1)
                pool.tensor_tensor(av[:, t % 2], a[:, t, :].unsqueeze(2).to_broadcast([P, NH, P]),
                                   upto.unsqueeze(1).to_broadcast([P, NH, P]), ALU.mult).then_inc(s["av"], 1)

        @block.tensor
        def _(pe):
            transposes_in(pe, xn, ident, T, KD, s["xn"], s["xnT"])
            pe.wait_ge(s["ul"], KD)

            def dt_projection():
                for k in range(KD):
                    ins = split_matmul(pe, SM[0:NH, :], [w[:, k, PROJ - NH:PROJ] for w in W["win"]],
                                       (uh[:, k, :], ul[:, k, :]), k == 0, k == KD - 1)
                ins.then_inc(s["dtp"], 1)

            def turn_dt():
                pe.wait_ge(s["dtf"], 1)
                for t in range(GT):
                    ins = pe.transpose(SM[:, t * NH:(t + 1) * NH], dtf[:, t * P:(t + 1) * P], ident[0:NH, 0:NH])
                ins.then_inc(s["dtT"], 1)

            dt_projection()
            for n in range(CT):
                if n >= 2:
                    pe.wait_ge(s["conv"], n - 1)
                w0 = DI + ORDER[n] * P
                for k in range(KD):
                    ins = split_matmul(pe, J[n % 2][:], [w[:, k, w0:w0 + P] for w in W["win"]],
                                       (uh[:, k, :], ul[:, k, :]), k == 0, k == KD - 1)
                ins.then_inc(s["J"], 1)
                if n == 0:
                    turn_dt()
            for t in range(GT):
                bank = (YO, J[1], J[0], DB[0])[t]
                if t in (1, 2):
                    pe.wait_ge(s["conv"], CT + 1 - t)
                for k in range(KD):
                    ins = split_matmul(pe, bank[:], (uh[:, k, t * P:(t + 1) * P], ul[:, k, t * P:(t + 1) * P]),
                                       [w[:, k, 0:DI] for w in W["win"]], k == 0, k == KD - 1)
                ins.then_inc(s["Z"], 1)

            def front(t):
                c = t % QT
                if t == 0:
                    pe.wait_ge(s["xs"], CT)
                if t >= 2:
                    pe.wait_ge(s["xd"], t - 1)
                for k in range(XT):
                    ins = pe.transpose(T[t % 2][:, k * P:(k + 1) * P], xs[:, k, t * P:(t + 1) * P], ident)
                ins.then_inc(s["xT"], 1)
                if t == 0:
                    pe.wait_ge(s["a"], 1)
                else:
                    pe.wait_ge(s["small"], t)
                pe.matmul(SM[:, 0:P], xs[:, XT, t * P:(t + 1) * P], xs[:, XT + 1, t * P:(t + 1) * P], start=True, stop=True)
                if c:
                    pe.matmul(SM[:, P:2 * P], xs[:, XT, (t - 1) * P:t * P], xs[:, XT + 1, t * P:(t + 1) * P],
                              start=True, stop=True)
                ins = pe.matmul(SM[:, 2 * P:2 * P + NH], upto if c else after, a[:, t, :], start=True, stop=True)
                ins.then_inc(s["SM"], 1)
                pe.wait_ge(s["av"], t + 1)
                for i, bank in enumerate(DB):
                    if t:
                        pe.wait_ge(s["L"], 2 * t - 1 + i)
                    elif i == 0:
                        pe.wait_ge(s["zg"], GT)
                    ins = pe.matmul(bank[:], after, av[:, t % 2, i * HH:(i + 1) * HH, :], start=True, stop=True)
                    ins.then_inc(s["Dhalf"], 1)
                pe.wait_ge(s["Dhalf"], 2 * t + 2)
                pe.sem_inc(s["D"], 1)

            def mid(t):
                pe.wait_ge(s["M"], t + 1)
                if t >= 2:
                    pe.wait_ge(s["y"], t - 1)
                for h in range(NH):
                    ins = pe.matmul(J[t % 2][:, h * HD:(h + 1) * HD], lm[:, t % 2, h, :], xd[:, t % 2, h * HD:(h + 1) * HD],
                                    start=True, stop=True)
                ins.then_inc(s["Y"], 1)
                if t % QT:
                    pe.wait_ge(s["xdd"], t // QT + 1)
                    if t // QT:
                        pe.wait_ge(s["yo"], t // QT)
                    pe.matmul(YO[:], g01[:], xdd[:], start=True, stop=True).then_inc(s["YO"], 1)

            for i in range(GT + 1):
                if i < GT:
                    front(i)
                if i >= 1:
                    mid(i - 1)

            def turn(t):
                pe.wait_ge(s["yn"], t + 1)
                if t >= 2:
                    pe.wait_ge(s["yl"], t - 1)
                for k in range(XT):
                    ins = pe.transpose(T[t % 2][:, k * P:(k + 1) * P], y[:, t, k * P:(k + 1) * P], ident)
                ins.then_inc(s["yT"], 1)

            def project(t):
                pe.wait_ge(s["yl"], t + 1)
                if t >= 2:
                    pe.wait_ge(s["res"], t - 1)
                for k in range(XT):
                    ins = split_matmul(pe, DB[t % 2][:, 0:D], (yh[:, t % 2, k, :], yl[:, t % 2, k, :]),
                                       [w[:, k, :] for w in W["wout"]], k == 0, k == XT - 1)
                ins.then_inc(s["O"], 1)

            turn(0)
            for t in range(GT):
                if t + 1 < GT:
                    turn(t + 1)
                project(t)

        @block.scalar
        def _(act):
            for k in range(KD):
                act.wait_ge(s["xnT"], k + 1)
                part_high(act, uh[:, k, :], T[k][:]).then_inc(s["uh"], 1)
            act.wait_ge(s["dtp"], 1)
            act.activation(dtf[:], SM[0:NH, :], ACT.Copy).then_inc(s["dtf"], 1)
            for n in range(CT + 1):
                if n < CT:
                    f = ORDER[n]
                    act.wait_ge(s["J"], n + 1)
                    if n >= 2:
                        act.wait_ge(s["xs"], n - 1)
                    act.activation(cv[:, n % 2, :], J[n % 2][:], ACT.Identity, bias=K["tapb"][:, f:f + 1],
                                   scale=K["taps"][:, f, TAPS - 1:TAPS]).then_inc(s["cv"], 1)
                if n >= 1:
                    act.wait_ge(s["conv"], n)
                    act.activation(th[:, (n - 1) % 2, :], cv[:, (n - 1) % 2, :], ACT.Tanh).then_inc(s["th"], 1)
                if n == 1:
                    act.wait_ge(s["nv"], 1)
                    act.activation(e[:], e[:], ACT.Exp).then_inc(s["e"], 1)
            for t in range(GT):
                act.wait_ge(s["Z"], t + 1)
                bank = (YO, J[1], J[0], DB[0])[t]
                act.activation(zg[:, t, :], bank[:], ACT.Tanh, scale=0.5).then_inc(s["zt"], 1)

            def squares(t):
                act.wait_ge(s["yg"], t + 1)
                if t:
                    act.wait_ge(s["ss"], t)
                act.activation(sq, y[:, t, :], ACT.Square, accum_out=ss[:, t:t + 1]).then_inc(s["ss"], 1)

            for t in range(GT):
                if t >= 2:
                    act.wait_ge(s["Y"], t - 1)
                for j, bank in enumerate(DB):
                    act.wait_ge(s["Dhalf"], 2 * t + j + 1)
                    act.activation(lm[:, t % 2, j * HH:(j + 1) * HH, :], bank[:], ACT.Exp).then_inc(s["L"], 1)
                act.wait_ge(s["small"], t + 1)
                act.activation(dec[:, t, :], dec[:, t, :], ACT.Exp).then_inc(s["dec"], 1)
                if t >= 2:
                    squares(t - 2)
            squares(GT - 2)
            squares(GT - 1)
            for t in range(GT):
                act.wait_ge(s["yT"], t + 1)
                if t >= 2:
                    act.wait_ge(s["O"], t - 1)
                part_high(act, yh[:, t % 2].rearrange("p k n -> p (k n)"), T[t % 2][:]).then_inc(s["yh"], 1)

        @block.vector
        def _(dve):
            ch = Chain(dve, s["chain"])
            inverse_root(dve, ch, rstd[:], mv[:, :, 1], LN_EPS, (nt[:, 0], nt[:, 1]))
            for t in range(GT):
                dve.tensor_scalar(xn[:, t, :], XN[:, t, :], mv[:, t, 0:1], rstd[:, t:t + 1],
                                  ALU.subtract, ALU.mult).then_inc(s["xn"], 1)
            for k in range(KD):
                dve.wait_ge(s["uh"], k + 1)
                part_low(dve, ul[:, k, :], T[k][:], uh[:, k, :]).then_inc(s["ul"], 1)

            def convolve(n):
                f = ORDER[n]
                dve.wait_ge(s["cv"], n + 1)
                out = cv[:, n % 2, :].rearrange("p (b l) -> p b l", b=2)
                src = J[n % 2][:].rearrange("p (b l) -> p b l", b=2)
                for k in range(1, TAPS):
                    if k > 1:
                        ch.sync()
                    ins = dve.scalar_tensor_tensor(out=out[:, :, k:], in0=src[:, :, 0:S - k],
                                                   scalar=K["taps"][:, f, TAPS - 1 - k:TAPS - k], in1=out[:, :, k:],
                                                   op0=ALU.mult, op1=ALU.add)
                    if k < TAPS - 1:
                        ch.then(ins)
                ins.then_inc(s["conv"], 1)

            def activate(n):
                dve.wait_ge(s["th"], n + 1)
                dve.wait_ge(s["conv"], n + 1)
                dve.scalar_tensor_tensor(out=xs[:, ORDER[n], :], in0=th[:, n % 2, :], scalar=1.0, in1=cv[:, n % 2, :],
                                         op0=ALU.add, op1=ALU.mult).then_inc(s["xs"], 1)

            convolve(0)
            dve.wait_ge(s["dtT"], 1)
            ch.link(dve.tensor_tensor(v[:], SM[:, 0:GT * NH].rearrange("p (t h) -> p t h", t=GT),
                                      K["dtb"][:].unsqueeze(1).to_broadcast([P, GT, NH]), ALU.add))
            ch.link(dve.tensor_scalar(r[:], v[:], 0.0, None, ALU.max))
            dve.scalar_tensor_tensor(out=e[:], in0=r[:], scalar=-2.0, in1=v[:], op0=ALU.mult,
                                     op1=ALU.add).then_inc(s["nv"], 1)
            convolve(1)
            activate(0)
            dve.wait_ge(s["e"], 1)
            ch.link(dve.tensor_scalar(den[:], e[:], 2.0, None, ALU.add))
            ch.link(dve.reciprocal(den[:], den[:]))
            ch.link(dve.tensor_tensor(zz[:], e[:], den[:], ALU.mult))
            ch.link(dve.tensor_tensor(z2[:], zz[:], zz[:], ALU.mult))
            ch.link(dve.tensor_scalar(acc[:], z2[:], 1.0 / 15, None, ALU.mult))
            for m in (13, 11, 9, 7, 5, 3):
                ch.link(dve.scalar_tensor_tensor(out=acc[:], in0=acc[:], scalar=1.0 / m, in1=z2[:],
                                                 op0=ALU.add, op1=ALU.mult))
            ch.link(dve.scalar_tensor_tensor(out=acc[:], in0=acc[:], scalar=1.0, in1=zz[:], op0=ALU.add, op1=ALU.mult))
            ch.link(dve.scalar_tensor_tensor(out=dt[:], in0=acc[:], scalar=2.0, in1=r[:], op0=ALU.mult, op1=ALU.add))
            dve.tensor_tensor(a[:], dt[:], K["A"][:].unsqueeze(1).to_broadcast([P, GT, NH]), ALU.mult).then_inc(s["a"], 1)
            for n in range(2, CT):
                convolve(n)
                activate(n - 1)
            activate(CT - 1)

            def heads(ap):
                return ap.rearrange("p (h d) -> p h d", h=NH)

            def wide(ap):
                return ap.unsqueeze(2).to_broadcast([P, NH, HD])

            def gates():
                for t in range(GT):
                    dve.wait_ge(s["zt"], t + 1)
                    bank = (YO, J[1], J[0], DB[0])[t]
                    dve.scalar_tensor_tensor(out=zg[:, t, :], in0=zg[:, t, :], scalar=1.0, in1=bank[:],
                                             op0=ALU.add, op1=ALU.mult).then_inc(s["zg"], 1)

            def front(t):
                c = t % QT
                dve.wait_ge(s["SM"], t + 1)
                ch.link(dve.tensor_tensor(gm[:, t % 2, :], SM[:, 0:P], upto, ALU.mult))
                if c:
                    if t // QT:
                        dve.wait_ge(s["YO"], t // QT)
                    ch.link(dve.tensor_copy(g01[:], SM[:, P:2 * P]))
                dve.tensor_copy(dec[:, t, :], SM[:, 2 * P:2 * P + NH]).then_inc(s["small"], 1)
                if t >= 2:
                    dve.wait_ge(s["Y"], t - 1)
                dve.tensor_tensor(heads(xd[:, t % 2, :]), heads(T[t % 2][:]), wide(dt[:, t, :]), ALU.mult).then_inc(s["dx"], 1)
                dve.tensor_tensor(heads(y[:, t, :]), heads(T[t % 2][:]), wide(K["dpar"][:]), ALU.mult).then_inc(s["xd"], 1)

            def decays(t):
                dve.wait_ge(s["L"], 2 * t + 2)
                dve.tensor_tensor(lm[:, t % 2], lm[:, t % 2], gm[:, t % 2, :].unsqueeze(1).to_broadcast([P, NH, P]),
                                  ALU.mult).then_inc(s["M"], 1)
                if t % QT:
                    dve.wait_ge(s["dec"], t)
                    dve.wait_ge(s["dx"], t)
                    if t // QT:
                        dve.wait_ge(s["YO"], t // QT)
                    dve.tensor_tensor(heads(xdd[:]), heads(xd[:, (t - 1) % 2, :]), wide(dec[:, t - 1, :]),
                                      ALU.mult).then_inc(s["xdd"], 1)

            def mid(t):
                dve.wait_ge(s["Y"], t + 1)
                dve.wait_ge(s["xd"], t + 1)
                dve.tensor_tensor(y[:, t, :], y[:, t, :], J[t % 2][:], ALU.add).then_inc(s["y"], 1)
                dve.wait_ge(s["y"], t + 1)
                if t % QT:
                    dve.wait_ge(s["YO"], t // QT + 1)
                    dve.wait_ge(s["dec"], t + 1)
                    dve.tensor_tensor(heads(yo), heads(YO[:]), wide(dec[:, t, :]), ALU.mult).then_inc(s["yo"], 1)
                    dve.wait_ge(s["yo"], t // QT + 1)
                    ch.link(dve.tensor_tensor(y[:, t, :], y[:, t, :], yo, ALU.add))
                dve.tensor_tensor(y[:, t, :], y[:, t, :], zg[:, t, :], ALU.mult).then_inc(s["yg"], 1)

            for i in range(GT + 1):
                if i < GT:
                    dve.wait_ge(s["xT"], i + 1)
                    if i == 0:
                        gates()
                    front(i)
                    decays(i)
                if i >= 1:
                    mid(i - 1)
            dve.wait_ge(s["ss"], GT)
            inverse_root(dve, ch, rs[:], ss[:], 4 * DI * SSM_EPS, (nt[:, 0], nt[:, 1]))
            dve.wait_ge(s["yg"], GT)
            for t in range(GT):
                dve.scalar_tensor_tensor(out=y[:, t, :], in0=y[:, t, :], scalar=rs[:, t:t + 1], in1=K["nw"][:],
                                         op0=ALU.mult, op1=ALU.mult).then_inc(s["yn"], 1)

            def low(t):
                dve.wait_ge(s["yh"], t + 1)
                if t >= 2:
                    dve.wait_ge(s["O"], t - 1)
                part_low(dve, yl[:, t % 2].rearrange("p k n -> p (k n)"), T[t % 2][:],
                         yh[:, t % 2].rearrange("p k n -> p (k n)")).then_inc(s["yl"], 1)

            for t in range(GT + 1):
                if t < GT:
                    low(t)
                if t >= 1:
                    dve.wait_ge(s["O"], t)
                    dve.tensor_tensor(XG[:, t - 1, :], XN[:, t - 1, :], DB[(t - 1) % 2][:, 0:D], ALU.add).then_inc(s["res"], 1)
                    dve.wait_ge(s["res"], t)
                    moments(dve, ch, XG[:, t - 1, :], st[:, t - 1, :], K["moments"][:, t - 1, :])
            ch.sync()



def stage_cross(nc, ctx, g, W, K, XG, CX, ps, s, last):
    with ExitStack() as own:
        def sb(name, shape, dt=F32):
            return own.enter_context(nc.sbuf_tensor("b_" + name, shape, dt))

        st, rstd, nt = sb("st", [P, GT, 6]), sb("rstd", [P, GT]), sb("nt", [P, 2, GT])
        mv = K["moments"]
        xn = sb("xn", [P, GT, D])
        uh, ul = sb("uh", [P, KD, GN], FR), sb("ul", [P, KD, GN], FR)
        cr, mask = CX
        eh, el = sb("eh", [P, KD * GN], FR), sb("el", [P, KD * GN], FR)
        c = [e[:].rearrange("p (k n) -> p k n", k=KD) for e in (eh, el)]
        o = [e[:].rearrange("p (k n) -> p k n", k=ET) for e in (eh, el)]
        q, k_ = sb("q", [P, 2, GN]), sb("k", [P, 2, GN])
        va = sb("va", [P, GT, XH, VW])
        pp = sb("pp", [P, 3, QT, S])
        nm = sb("nm", [P, 4, QT])
        pt = sb("pt", [P, 2, 2 * S])
        rc = sb("rc", [P, 2, QT, 2])
        ot = sb("ot", [P, GT, XI])

        PJ, S3, T2, O2 = ps[0], ps[1:4], ps[4:6], ps[6:8]
        ident = K["const"][:, C_ID:C_ID + P]
        NU = ET * 2
        NHD = 2 * NU
        NV = GT * 2
        block = own.enter_context(nc.Block())

        def tokens(b, qt):
            return slice((b * QT + qt) * P, (b * QT + qt + 1) * P)

        @block.sync
        def _(sp):
            clear(sp, last)

        @block.gpsimd
        def _(pool):
            pool.memset(va[:, :, :, XD], 1.0).then_inc(s["ones"], 1)

        @block.tensor
        def _(pe):
            pe.wait_ge(s["cl"], 1)
            for n in range(NV):
                t, half = n // 2, n % 2
                bank = (PJ, *S3)[n % 4]
                if n >= 4:
                    pe.wait_ge((s["va"], s["v"])[n % 2], n // 2 - 1)
                for k in range(KD):
                    ins = split_matmul(pe, bank[:], [x[:, k, t * P:(t + 1) * P] for x in c],
                                       [w[:, k, half * 512:(half + 1) * 512] for w in W["wv"]], k == 0, k == KD - 1)
                ins.then_inc(s["V"], 1)
            transposes_in(pe, xn, ident, T2, KD, s["xn"], s["xnT"])
            pe.wait_ge(s["ul"], KD)

            def project(j, which):
                n = 2 * j + which
                if n:
                    pe.wait_ge(s["qk"], n)
                else:
                    pe.wait_ge(s["va"], NV // 2)
                    pe.wait_ge(s["v"], NV // 2)
                w, x = (W["wq"], (uh, ul)) if which == 0 else (W["wk"], c)
                for k in range(KD):
                    ins = split_matmul(pe, PJ[:], [a[:, k, j * P:(j + 1) * P] for a in w],
                                       [a[:, k, :] for a in x], k == 0, k == KD - 1)
                ins.then_inc(s["QK"], 1)

            def scores(n):
                u, hp = n // 2, n % 2
                j, b = u // 2, u % 2
                if b == 0 and hp == 0:
                    pe.wait_ge(s["qk"], 2 * j + 2)
                if n >= 3:
                    pe.wait_ge(s["sm"], 2 * (n - 2))
                r = slice(XD * hp, XD * hp + XD)
                for qt in range(QT):
                    ins = pe.matmul(S3[n % 3][:, qt * S:(qt + 1) * S], q[r, j % 2, tokens(b, qt)],
                                    k_[r, j % 2, b * S:(b + 1) * S], start=True, stop=True)
                ins.then_inc(s["S"], 1)

            def turn(n):
                pe.wait_ge(s["ex"], 2 * (n + 1))
                if n >= 2:
                    pe.wait_ge(s["pt"], n - 1)
                for kt in range(QT):
                    for qt in range(QT):
                        ins = pe.transpose(T2[n % 2][:, kt * S + qt * P:kt * S + (qt + 1) * P],
                                           pp[:, n % 3, qt, kt * P:(kt + 1) * P], ident)
                ins.then_inc(s["T"], 1)

            def values(n):
                u, hp = n // 2, n % 2
                j, b = u // 2, u % 2
                pe.wait_ge(s["pt"], n + 1)
                if hp == 0 and u >= 2:
                    pe.wait_ge(s["o"], u - 1)
                for qt in range(QT):
                    for kt in range(QT):
                        at = (hp * QT + qt) * VW
                        ins = pe.matmul(O2[u % 2][:, at:at + VW], pt[:, n % 2, kt * S + qt * P:kt * S + (qt + 1) * P],
                                        va[:, b * QT + kt, 2 * j + hp, :], start=kt == 0, stop=kt == QT - 1)
                ins.then_inc(s["PV"], 1)

            project(0, 0)
            project(0, 1)
            pe.wait_ge(s["ones"], 1)
            scores(0)
            project(1, 0)
            scores(1)
            for n in range(NHD + 1):
                if n + 2 < NHD:
                    scores(n + 2)
                if n < NHD:
                    turn(n)
                if n >= 1:
                    values(n - 1)
                if n % 4 == 3 and n // 4 + 2 < ET:
                    project(n // 4 + 2, 0)
                if n % 4 == 0 and n // 4 + 1 < ET:
                    project(n // 4 + 1, 1)
            pe.wait_ge(s["o"], NU)

            def turn_heads(t, i):
                if t:
                    pe.wait_ge(s["ol"], 2 * t - 1 + i)
                for m in range(4):
                    k = 4 * i + m
                    ins = pe.transpose(T2[i][:, m * P:(m + 1) * P], ot[:, t, k * P:(k + 1) * P], ident)
                ins.then_inc(s["oT"], 1)

            def project_out(t, i):
                pe.wait_ge(s["ol"], 2 * t + i + 1)
                if i == 0 and t >= 2:
                    pe.wait_ge(s["res"], t - 1)
                for k in range(4 * i, 4 * i + 4):
                    ins = split_matmul(pe, O2[t % 2][:, 0:D], [x[:, k, :] for x in o], [w[:, k, :] for w in W["wo"]],
                                       k == 0, k == ET - 1)
                ins.then_inc(s["R"], 1)

            turn_heads(0, 0)
            turn_heads(0, 1)
            for t in range(GT):
                for i in range(2):
                    project_out(t, i)
                    if t + 1 < GT:
                        turn_heads(t + 1, i)

        @block.scalar
        def _(act):
            act.activation(eh[:].rearrange("p (k n) -> p k n", k=KD), cr[:], ACT.Copy).then_inc(s["ch"], 1)
            for n in range(0, NV, 2):
                t, half, bank = n // 2, n % 2, (PJ, *S3)[n % 4]
                act.wait_ge(s["V"], n + 1)
                act.activation(va[:, t, half * 8:half * 8 + 8, 0:XD], bank[:].rearrange("p (h d) -> p h d", h=8),
                               ACT.Copy).then_inc(s["va"], 1)
            for k in range(KD):
                act.wait_ge(s["xnT"], k + 1)
                part_high(act, uh[:, k, :], T2[k][:]).then_inc(s["uh"], 1)

            def place(n):
                j, which = n // 2, n % 2
                act.wait_ge(s["QK"], n + 1)
                if j >= 2:
                    act.wait_ge(s["S"], 4 * (j - 1))
                act.activation((q, k_)[which][:, j % 2, :], PJ[:], ACT.Copy).then_inc(s["qk"], 1)

            place(0)
            place(1)
            for n in range(NHD):
                for qt in range(QT):
                    act.wait_ge(s["sm"], 2 * n + qt + 1)
                    act.activation(pp[:, n % 3, qt, :], pp[:, n % 3, qt, :], ACT.Exp, bias=nm[:, n % 4, qt:qt + 1],
                                   scale=-1.0).then_inc(s["ex"], 1)
                if n % 4 < 2 and n // 4 + 1 < ET:
                    place(2 * (n // 4 + 1) + n % 4)
            for t in range(GT):
                for i in range(2):
                    act.wait_ge(s["oT"], 2 * t + i + 1)
                    if t:
                        act.wait_ge(s["R"], 2 * t - 1 + i)
                    act.activation(o[0][:, 4 * i:4 * i + 4, :], T2[i][:].rearrange("p (k n) -> p k n", k=4),
                                   ACT.Copy).then_inc(s["oh"], 1)

        @block.vector
        def _(dve):
            ch = Chain(dve, s["chain"])
            inverse_root(dve, ch, rstd[:], mv[:, :, 1], LN_EPS, (nt[:, 0], nt[:, 1]))
            for t in range(GT):
                dve.tensor_scalar(xn[:, t, :], XG[:, t, :], mv[:, t, 0:1], rstd[:, t:t + 1],
                                  ALU.subtract, ALU.mult).then_inc(s["xn"], 1)
            dve.wait_ge(s["ch"], 1)
            dve.tensor_tensor(c[1], cr[:], c[0].bitcast(F32), ALU.subtract).then_inc(s["cl"], 1)
            for n in range(NV):
                if n % 2:
                    t, half, bank = n // 2, n % 2, (PJ, *S3)[n % 4]
                    dve.wait_ge(s["V"], n + 1)
                    dve.tensor_copy(va[:, t, half * 8:half * 8 + 8, 0:XD],
                                    bank[:].rearrange("p (h d) -> p h d", h=8)).then_inc(s["v"], 1)
            for k in range(KD):
                dve.wait_ge(s["uh"], k + 1)
                part_low(dve, ul[:, k, :], T2[k][:], uh[:, k, :]).then_inc(s["ul"], 1)

            def masked(n):
                b = n // 2 % 2
                dve.wait_ge(s["S"], n + 1)
                if n >= 3:
                    dve.wait_ge(s["T"], n - 2)
                for qt in range(QT):
                    dve.tensor_tensor_reduce(out=pp[:, n % 3, qt, :], in0=S3[n % 3][:, qt * S:(qt + 1) * S],
                                             in1=mask[:, b * QT + qt, :], scale=-1.0, scalar=3e38, op0=ALU.add,
                                             op1=ALU.min, accum_out=nm[:, n % 4, qt:qt + 1]).then_inc(s["sm"], 1)

            def place(n):
                dve.wait_ge(s["T"], n + 1)
                if n >= 2:
                    dve.wait_ge(s["PV"], n - 1)
                dve.tensor_copy(pt[:, n % 2, :], T2[n % 2][:]).then_inc(s["pt"], 1)

            def normalise(u):
                j, b = u // 2, u % 2
                dve.wait_ge(s["PV"], 2 * u + 2)
                src = O2[u % 2][:, 0:4 * VW].rearrange("p (h q d) -> p h q d", h=2, q=QT)
                r = rc[:, u % 2].rearrange("p a b -> p (a b)").rearrange("p (h q) -> p h q", h=2)
                ch.link(dve.reciprocal(r, src[:, :, :, XD]))
                for hp in range(2):
                    h = 2 * j + hp
                    ins = dve.tensor_tensor(ot[:, b * QT:(b + 1) * QT, h * XD:(h + 1) * XD], src[:, hp, :, 0:XD],
                                            r[:, hp, :].unsqueeze(2).to_broadcast([P, QT, XD]), ALU.mult)
                ins.then_inc(s["o"], 1)

            for n in range(NHD + 3):
                if n < NHD:
                    masked(n)
                if 1 <= n <= NHD:
                    place(n - 1)
                if n >= 3 and n % 2:
                    normalise((n - 3) // 2)
            def add(t):
                dve.wait_ge(s["R"], 2 * t + 2)
                dve.tensor_tensor(XG[:, t, :], XG[:, t, :], O2[t % 2][:, 0:D], ALU.add).then_inc(s["res"], 1)
                dve.wait_ge(s["res"], t + 1)
                moments(dve, ch, XG[:, t, :], st[:, t, :], mv[:, t, :])

            for t in range(GT):
                for i in range(2):
                    dve.wait_ge(s["oh"], 2 * t + i + 1)
                    part_low(dve, o[1][:, 4 * i:4 * i + 4, :], T2[i][:].rearrange("p (k n) -> p k n", k=4),
                             o[0][:, 4 * i:4 * i + 4, :]).then_inc(s["ol"], 1)
                if t:
                    add(t - 1)
            add(GT - 1)
            ch.sync()



def stage_attention(nc, ctx, g, I, W, K, XN, XG, scratch, ps, s, last):
    with ExitStack() as own:
        def sb(name, shape, dt=F32):
            return own.enter_context(nc.sbuf_tensor("c_" + name, shape, dt))

        st, rstd, nt = sb("st", [P, GT, 6]), sb("rstd", [P, GT]), sb("nt", [P, 2, GT])
        mv = K["moments"]
        ln = sb("ln", [P, GT, D])
        xr = sb("xr", [P, GT, D])
        sq, ss, rs = sb("sq", [P, D]), sb("ss", [P, GT]), sb("rs", [P, GT])
        uh, ul = sb("uh", [P, KD, GN], FR), sb("ul", [P, KD, GN], FR)
        NR, HALF = AH + AKV, AD // 2
        ra, rb = sb("ra", [P, 2, NR * AD]), sb("rb", [P, 2, NR * AD])
        rot = sb("rot", [P, 2, NR * AD])
        qs = sb("qs", [P, GT, AKV, 2, REP * AD], FR)
        ks = sb("ks", [P, GT, AKV, 2, AD], FR)
        v = sb("v", [P, GT, AKV, AVW])
        qv = sb("qv", [P, 2, REP, GN], FR)
        kv = sb("kv", [P, 2, 2, GN], FR)
        kT = sb("kT", [P, GN], FR)
        repeat = sb("repeat", [P, 2 * AKV, 2 * REP, AD], FR)
        NB = 3
        pp = sb("pp", [P, 4, NB * P])
        nm = sb("nm", [P, 4, QT])
        pt = sb("pt", [P, 4, NB * P])
        rc = sb("rc", [P, 2, 2 * QT])
        ot = sb("ot", [P, GT, AH * AD])

        ident, identr = K["const"][:, C_ID:C_ID + P], K["identr"][:]
        causal = K["const"][:, C_CAUSAL:C_CAUSAL + QT * P]
        BB, SB, TB, OB = ps[0], ps[1:4], ps[4:6], ps[6:8]
        NHD = 2 * AH
        PER = 2 * REP
        block = own.enter_context(nc.Block())

        def where(n):
            return n // PER, n % PER // REP, n % REP

        @block.sync
        def _(sp):
            sp.dma_start(XN[:], I["x"][(g + 1) % NG]).then_inc(s["next_x"], 16)
            clear(sp, last)
            sp.wait_ge(s["xh"], GT)
            sp.dma_start(scratch["res"][g], XG[:]).then_inc(s["stored"], 16)
            sp.wait_ge(s["l2"], KD)
            sp.dma_start(scratch["h"][g], uh[:].bitcast(F32)).then_inc(s["stored"], 16)
            sp.dma_start(scratch["l"][g], ul[:].bitcast(F32)).then_inc(s["stored"], 16)
            sp.wait_ge(s["stored"], 48)

        @block.gpsimd
        def _(pool):
            pool.memset(v[:, :, :, AD], 1.0).then_inc(s["ones"], 1)
            pool.tensor_copy(repeat[:], identr.bitcast(F32).rearrange("p (a d) -> p a d", d=AD).unsqueeze(2)
                             .to_broadcast([P, 2 * AKV, 2 * REP, AD])).then_inc(s["repeat"], 1)
            for t in range(GT):
                pool.wait_ge(s["qkh"], 2 * t + 2)
                q = rot[:, t % 2, 0:AH * AD].rearrange("p (g d) -> p g d", g=AKV)
                k = rot[:, t % 2, AH * AD:NR * AD].rearrange("p (g d) -> p g d", g=AKV)
                pool.tensor_tensor(qs[:, t, :, 1, :], q, qs[:, t, :, 0, :].bitcast(F32), ALU.subtract).then_inc(s["qkl"], 1)
                pool.tensor_tensor(ks[:, t, :, 1, :], k, ks[:, t, :, 0, :].bitcast(F32), ALU.subtract).then_inc(s["qkl"], 1)

        @block.tensor
        def _(pe):
            transposes_in(pe, xr, ident, TB, KD, s["xr"], s["xT"])
            pe.wait_ge(s["ul"], KD)
            for t in range(GT):
                for k in range(KD):
                    ins = split_matmul(pe, ps[t][:, 0:AQKV], (uh[:, k, t * P:(t + 1) * P], ul[:, k, t * P:(t + 1) * P]),
                                       [w[:, k, :] for w in W["aqkv"]], k == 0, k == KD - 1)
                ins.then_inc(s["QKV"], 1)
            pe.wait_ge(s["qkl"], 2 * GT)

            def build(i):
                m, what = i // 3, i % 3
                if i:
                    pe.wait_ge(s["built"], i)
                if what:
                    pe.matmul(BB[:], repeat[:, 2 * m + what - 1].rearrange("p a d -> p (a d)"), kT[:], start=True,
                              stop=True).then_inc(s["B"], 1)
                    return
                for t in range(GT):
                    ins = pe.transpose(BB[:, t * P:(t + 1) * P].bitcast(FR), qs[:, t, m].rearrange("p a b -> p (a b)"), identr)
                ins.then_inc(s["B"], 1)

            def scores(n):
                m, b, r = where(n)
                if n % PER == 0:
                    pe.wait_ge(s["built"], 3 * m + 3)
                if n >= 3:
                    pe.wait_ge(s["sm"], 2 * (n - 2))
                for qt in range(QT):
                    at, w = (b * QT + qt) * P, (qt + 1) * P
                    for part in range(2):
                        ins = pe.matmul(SB[n % 3][:, qt * P:qt * P + w], qv[:, m % 2, r, at:at + P],
                                        kv[:, m % 2, part, b * S:b * S + w], start=part == 0, stop=part == 1)
                ins.then_inc(s["S"], 1)

            def turn(n):
                pe.wait_ge(s["ex"], 2 * (n + 1))
                if n >= 2:
                    pe.wait_ge((s["pta"], s["ptv"])[n % 2], n // 2)
                for i in range(NB):
                    ins = pe.transpose(TB[n % 2][:, i * P:(i + 1) * P], pp[:, n % 4, i * P:(i + 1) * P], ident)
                ins.then_inc(s["T"], 1)

            def values(n):
                u, hp = n // 2, n % 2
                b = where(n)[1]
                pe.wait_ge((s["pta"], s["ptv"])[n % 2], n // 2 + 1)
                if hp == 0 and u >= 2:
                    pe.wait_ge(s["o"], u - 1)
                for qt, i, kt in ((0, 0, 0), (1, 1, 0), (1, 2, 1)):
                    at = (hp * QT + qt) * AKV * AVW
                    ins = pe.matmul(OB[u % 2][:, at:at + AKV * AVW], pt[:, n % 4, i * P:(i + 1) * P],
                                    v[:, b * QT + kt].rearrange("p a b -> p (a b)"), start=kt == 0, stop=kt == qt)
                ins.then_inc(s["PV"], 1)

            for t in range(GT):
                ins = pe.transpose(SB[2][:, t * P:(t + 1) * P].bitcast(FR), ks[:, t].rearrange("p g c d -> p (g c d)"), identr)
            ins.then_inc(s["kB"], 1)
            pe.wait_ge(s["ones"], 1)
            pe.wait_ge(s["repeat"], 1)
            pe.wait_ge(s["kT"], 1)
            for i in range(3):
                build(i)
            scores(0)
            scores(1)
            for n in range(NHD + 1):
                if n + 2 < NHD:
                    scores(n + 2)
                if n < NHD:
                    turn(n)
                if n >= 1:
                    values(n - 1)
                if n % PER in (0, 2, 4) and n // PER + 1 < AKV:
                    build(3 * (n // PER + 1) + n % PER // 2)
            pe.wait_ge(s["o"], NHD // 2)
            transposes_in(pe, ot, ident, TB, KD, s["o"], s["oT"])
            pe.wait_ge(s["ol"], KD)
            for t in range(GT):
                for k in range(KD):
                    ins = split_matmul(pe, ps[t][:, 0:D], (uh[:, k, t * P:(t + 1) * P], ul[:, k, t * P:(t + 1) * P]),
                                       [w[:, k, :] for w in W["awo"]], k == 0, k == KD - 1)
                ins.then_inc(s["R"], 1)
            transposes_in(pe, xr, ident, TB, KD, s["xr2"], s["x2T"])

        @block.scalar
        def _(act):
            for k in range(KD):
                act.wait_ge(s["xT"], k + 1)
                part_high(act, uh[:, k, :], TB[k][:], K["g1"][:, k:k + 1]).then_inc(s["uh"], 1)
            for t in range(GT):
                act.wait_ge(s["rot"], t + 1)
                q = rot[:, t % 2, 0:AH * AD].rearrange("p (g d) -> p g d", g=AKV)
                k = rot[:, t % 2, AH * AD:NR * AD].rearrange("p (g d) -> p g d", g=AKV)
                act.activation(qs[:, t, :, 0, :], q, ACT.Copy).then_inc(s["qkh"], 1)
                act.activation(ks[:, t, :, 0, :], k, ACT.Copy).then_inc(s["qkh"], 1)

            def built(i):
                m, what = i // 3, i % 3
                act.wait_ge(s["B"], i + 1)
                if m >= 2:
                    act.wait_ge(s["S"], PER * (m - 1))
                if what == 0:
                    for r in range(REP):
                        ins = act.activation(qv[:, m % 2, r, :], BB[:], ACT.Copy, scale=K["const"][:, C_ROW + r:C_ROW + r + 1])
                else:
                    ins = act.activation(kv[:, m % 2, what - 1, :], BB[:], ACT.Copy)
                ins.then_inc(s["built"], 1)

            act.wait_ge(s["kB"], 1)
            act.activation(kT[:], SB[2][:], ACT.Copy).then_inc(s["kT"], 1)
            for i in range(3):
                built(i)
            for n in range(NHD + 1):
                if n < NHD:
                    act.wait_ge(s["sm"], 2 * n + 1)
                    act.activation(pp[:, n % 4, 0:P], pp[:, n % 4, 0:P], ACT.Exp, bias=nm[:, n % 4, 0:1],
                                   scale=-1.0).then_inc(s["ex"], 1)
                    act.wait_ge(s["sm"], 2 * n + 2)
                    act.activation(pp[:, n % 4, P:NB * P], pp[:, n % 4, P:NB * P], ACT.Exp, bias=nm[:, n % 4, 1:2],
                                   scale=-1.0).then_inc(s["ex"], 1)
                if n >= 1 and n % 2:
                    place = n - 1
                    act.wait_ge(s["T"], place + 1)
                    if place >= 4:
                        act.wait_ge(s["PV"], place - 3)
                    act.activation(pt[:, place % 4, :], TB[place % 2][:, 0:NB * P], ACT.Copy).then_inc(s["pta"], 1)
                if n % PER in (1, 3, 5) and n // PER + 1 < AKV:
                    built(3 * (n // PER + 1) + n % PER // 2)
            for k in range(KD):
                act.wait_ge(s["oT"], k + 1)
                part_high(act, uh[:, k, :], TB[k][:]).then_inc(s["oh"], 1)
            for t in range(GT):
                act.wait_ge(s["h"], t + 1)
                if t:
                    act.wait_ge(s["ss"], t)
                act.activation(sq[:], ln[:, t, :], ACT.Square, accum_out=ss[:, t:t + 1]).then_inc(s["ss"], 1)
            for k in range(KD):
                act.wait_ge(s["x2T"], k + 1)
                part_high(act, uh[:, k, :], TB[k][:], K["g2"][:, k:k + 1]).then_inc(s["h2"], 1)

        @block.vector
        def _(dve):
            ch = Chain(dve, s["chain"])
            tmp = (nt[:, 0], nt[:, 1])
            inverse_root(dve, ch, rstd[:], mv[:, :, 1], LN_EPS, tmp)
            for t in range(GT):
                dve.tensor_scalar(ln[:, t, :], XG[:, t, :], mv[:, t, 0:1], rstd[:, t:t + 1],
                                  ALU.subtract, ALU.mult).then_inc(s["ln"], 1)
            ch.link(dve.tensor_tensor(ss[:], mv[:, :, 1], rstd[:], ALU.mult))
            ch.link(dve.tensor_tensor(ss[:], ss[:], rstd[:], ALU.mult))
            inverse_root(dve, ch, rs[:], ss[:], RMS_EPS, tmp)
            for t in range(GT):
                dve.wait_ge(s["ln"], t + 1)
                dve.tensor_scalar(xr[:, t, :], ln[:, t, :], rs[:, t:t + 1], None, ALU.mult).then_inc(s["xr"], 1)
            for k in range(KD):
                dve.wait_ge(s["uh"], k + 1)
                part_low(dve, ul[:, k, :], TB[k][:], uh[:, k, :], K["g1"][:, k:k + 1]).then_inc(s["ul"], 1)

            def halves(ap):
                return ap.rearrange("p (h c d) -> p h c d", c=2, d=HALF)

            def table(t, i):
                return K["rope"][:, t % QT, i, :].unsqueeze(1).to_broadcast([P, NR, HALF])

            for t in range(GT):
                dve.wait_ge(s["QKV"], t + 1)
                src, a, b = halves(ps[t][:, 0:NR * AD]), halves(ra[:, t % 2]), halves(rb[:, t % 2])
                if t >= 2:
                    dve.wait_ge(s["rot"], t - 1)
                ch.then(dve.tensor_tensor(a, src, K["rope"][:, t % QT, 0, :].unsqueeze(1).unsqueeze(1)
                                          .to_broadcast([P, NR, 2, HALF]), ALU.mult))
                ch.then(dve.tensor_tensor(b[:, :, 0], src[:, :, 1], table(t, 1), ALU.mult))
                ch.then(dve.tensor_tensor(b[:, :, 1], src[:, :, 0], table(t, 2), ALU.mult))
                ch.then(dve.tensor_copy(v[:, t, :, 0:AD],
                                        ps[t][:, NR * AD:AQKV].rearrange("p (h d) -> p h d", d=AD)))
                ch.sync()
                if t >= 2:
                    dve.wait_ge(s["qkl"], 2 * (t - 1))
                dve.tensor_tensor(rot[:, t % 2, :], ra[:, t % 2, :], rb[:, t % 2, :], ALU.add).then_inc(s["rot"], 1)

            def masked(n):
                dve.wait_ge(s["S"], n + 1)
                if n >= 4:
                    dve.wait_ge(s["T"], n - 3)
                for qt in range(QT):
                    w = slice(qt * P, qt * P + (qt + 1) * P)
                    dve.tensor_tensor_reduce(out=pp[:, n % 4, w], in0=SB[n % 3][:, w], in1=causal[:, (QT - 1 - qt) * P:QT * P],
                                             scale=-AD ** -0.5, scalar=3e38, op0=ALU.add, op1=ALU.min,
                                             accum_out=nm[:, n % 4, qt:qt + 1]).then_inc(s["sm"], 1)

            def place(n):
                dve.wait_ge(s["T"], n + 1)
                if n >= 4:
                    dve.wait_ge(s["PV"], n - 3)
                dve.tensor_copy(pt[:, n % 4, :], TB[n % 2][:, 0:NB * P]).then_inc(s["ptv"], 1)

            def normalise(u):
                m, b, r = where(2 * u)
                h = m * REP + r
                dve.wait_ge(s["PV"], 2 * u + 2)
                src = OB[u % 2][:, 0:2 * QT * AKV * AVW].rearrange("p (h q d) -> p h q d", h=2, q=QT)
                o = rc[:, u % 2].rearrange("p (h q) -> p h q", h=2)
                ch.link(dve.reciprocal(o, src[:, :, :, m * AVW + AD]))
                dve.tensor_tensor(ot[:, b * QT:(b + 1) * QT, h * AD:(h + 2) * AD].rearrange("p q (h d) -> p h q d", h=2),
                                  src[:, :, :, m * AVW:m * AVW + AD],
                                  o.unsqueeze(3).to_broadcast([P, 2, QT, AD]), ALU.mult).then_inc(s["o"], 1)

            for n in range(NHD + 3):
                if n < NHD:
                    masked(n)
                if 1 <= n <= NHD and (n - 1) % 2:
                    place(n - 1)
                if n >= 3 and n % 2:
                    normalise((n - 3) // 2)
            dve.wait_ge(s["next_x"], 16)
            for t in range(GT):
                moments(dve, ch, XN[:, t, :], st[:, t, :], K["moments_n"][:, t, :])
            for k in range(KD):
                dve.wait_ge(s["oh"], k + 1)
                part_low(dve, ul[:, k, :], TB[k][:], uh[:, k, :]).then_inc(s["ol"], 1)
            for t in range(GT):
                dve.wait_ge(s["R"], t + 1)
                dve.tensor_tensor(ln[:, t, :], ln[:, t, :], ps[t][:, 0:D], ALU.add).then_inc(s["h"], 1)
            for t in range(GT):
                dve.wait_ge(s["h"], t + 1)
                dve.tensor_tensor(XG[:, t, :], XG[:, t, :], ln[:, t, :], ALU.add).then_inc(s["xh"], 1)
            dve.wait_ge(s["ss"], GT)
            inverse_root(dve, ch, rs[:], ss[:], D * RMS_EPS, tmp)
            for t in range(GT):
                dve.tensor_scalar(xr[:, t, :], ln[:, t, :], rs[:, t:t + 1], float(D) ** 0.5,
                                  ALU.mult, ALU.mult).then_inc(s["xr2"], 1)
            for k in range(KD):
                dve.wait_ge(s["h2"], k + 1)
                part_low(dve, ul[:, k, :], TB[k][:], uh[:, k, :], K["g2"][:, k:k + 1]).then_inc(s["l2"], 1)
            ch.sync()



def stage_experts(nc, ctx, I, K, scratch, out, ps, s):
    with ExitStack() as own:
        def sb(name, shape, dt=F32):
            return own.enter_context(nc.sbuf_tensor("e_" + name, shape, dt))

        acc = sb("acc", [P, NG, GT, D])
        yh, yl = sb("yh", [P, NG, KD, GN], FR), sb("yl", [P, NG, KD, GN], FR)
        comb = sb("comb", [P, NG, GT, NE])
        now = sb("now", [P, NG, GT])
        raw = [sb("raw1", [P, KD, HID]), sb("raw3", [P, KD, HID]), sb("raw2", [P, HT, D])]
        w1, w3, w2 = ((sb(n + "h", shape, FR), sb(n + "l", shape, FR)) for n, shape in
                      (("w1", [P, KD, HID]), ("w3", [P, KD, HID]), ("w2", [P, HT, D])))
        th, p3 = sb("th", [P, 2, GN]), sb("p3", [P, 2, GN])
        hh, hl = sb("hh", [P, 2, HT, GN], FR), sb("hl", [P, 2, HT, GN], FR)
        NH_ = NG * HT
        U1, U3, DN = ps[0:2], ps[2:4], ps[4:8]

        ident = K["const"][:, C_ID:C_ID + P]
        low_of = K["const"][:, C_LOW:C_LOW + NE * NE].rearrange("p (e j) -> p e j", e=NE)
        NT = NG * GT

        with ExitStack() as own_gate:
            def sg(name, shape, dt=F32):
                return own_gate.enter_context(nc.sbuf_tensor("g_" + name, shape, dt))

            graw, gh, gl = sg("raw", [P, KD, NE]), sg("high", [P, KD, NE], FR), sg("low", [P, KD, NE], FR)
            lgf = sg("lgf", [NE, NG, GN])
            lg, ex, rank, tmp = (sg(n, [P, NT, NE]) for n in "lg ex rank tmp".split())
            mx, sm = sg("mx", [P, NT]), sg("sm", [P, NT])
            gt, eq = sg("gt", [P, NT, NE, NE]), sg("eq", [P, NT, NE, NE])
            block = own_gate.enter_context(nc.Block())

            @block.sync
            def _(sp):
                sp.dma_start(graw[:], I["gate"]).then_inc(s["gate_in"], 16)
                for t, src, sem in ((yh[:].bitcast(F32), scratch["h"], s["yh_in"]), (yl[:].bitcast(F32), scratch["l"], s["yl_in"]),
                                    (acc[:], scratch["res"], s["acc_in"])):
                    sp.dma_start(t.rearrange("p g a b -> p g (a b)"), src.rearrange("g p a b -> p g (a b)")).then_inc(sem, 16)
                sp.wait_ge(s["acc_in"], 16)

            @block.scalar
            def _(act):
                for t, src in zip(raw, (I["w1"], I["w3"], I["w2"])):
                    act.dma_start(t[:], src[0]).then_inc(s["raw_in"], 16)
                act.wait_ge(s["gate_in"], 16)
                act.activation(gh[:], graw[:], ACT.Copy).then_inc(s["gh"], 1)
                for g in range(NG):
                    act.wait_ge(s["G"], g + 1)
                    act.activation(lgf[:, g, :], ps[g][0:NE, :], ACT.Copy).then_inc(s["lgf"], 1)
                act.wait_ge(s["lgm"], 1)
                act.activation(ex[:], ex[:], ACT.Exp).then_inc(s["gex"], 1)
                act.wait_ge(s["raw_in"], 48)

            @block.tensor
            def _(pe):
                pe.wait_ge(s["gl"], 1)
                pe.wait_ge(s["yh_in"], 16)
                pe.wait_ge(s["yl_in"], 16)
                for g in range(NG):
                    for k in range(KD):
                        ins = split_matmul(pe, ps[g][0:NE, :], (gh[:, k, :], gl[:, k, :]), (yh[:, g, k, :], yl[:, g, k, :]),
                                           k == 0, k == KD - 1)
                    ins.then_inc(s["G"], 1)
                for g in range(NG):
                    pe.wait_ge(s["lgf"], g + 1)
                    for t in range(GT):
                        at = (g * GT + t) * NE
                        ins = pe.transpose(ps[4][:, at:at + NE], lgf[:, g, t * P:(t + 1) * P], ident[0:NE, 0:NE])
                ins.then_inc(s["GT"], 1)

            @block.vector
            def _(dve):
                ch = Chain(dve, s["chain"])
                dve.wait_ge(s["gh"], 1)
                dve.tensor_tensor(gl[:], graw[:], gh[:].bitcast(F32), ALU.subtract).then_inc(s["gl"], 1)
                dve.wait_ge(s["GT"], 1)
                ch.link(dve.tensor_copy(lg[:], ps[4][:, 0:NT * NE].rearrange("p (t e) -> p t e", t=NT)))
                ch.link(dve.tensor_reduce(mx[:], lg[:], AX_X, ALU.max))
                dve.tensor_tensor(ex[:], lg[:], mx[:].unsqueeze(2).to_broadcast([P, NT, NE]), ALU.subtract).then_inc(s["lgm"], 1)
                dve.wait_ge(s["gex"], 1)
                mine = ex[:].unsqueeze(3).to_broadcast([P, NT, NE, NE])
                other = ex[:].unsqueeze(2).to_broadcast([P, NT, NE, NE])
                ch.then(dve.tensor_tensor(gt[:], other, mine, ALU.is_gt))
                ch.link(dve.tensor_tensor(eq[:], other, mine, ALU.is_equal))
                ch.link(dve.tensor_tensor(eq[:], eq[:], low_of.unsqueeze(1).to_broadcast([P, NT, NE, NE]), ALU.mult))
                ch.link(dve.tensor_tensor(gt[:], gt[:], eq[:], ALU.add))
                ch.link(dve.tensor_reduce(rank[:], gt[:], AX_X, ALU.add))
                ch.link(dve.scalar_tensor_tensor(out=tmp[:], in0=rank[:], scalar=1.5, in1=ex[:], op0=ALU.is_lt, op1=ALU.mult))
                ch.link(dve.tensor_reduce(sm[:], tmp[:], AX_X, ALU.add))
                ch.link(dve.reciprocal(sm[:], sm[:]))
                ch.link(dve.scalar_tensor_tensor(out=comb[:].rearrange("p g t e -> p (g t) e"), in0=tmp[:], scalar=0.5,
                                                 in1=sm[:].unsqueeze(2).to_broadcast([P, NT, NE]), op0=ALU.mult, op1=ALU.mult))

        with nc.Fori(0, NE) as e:
            with nc.Block() as block:
                @block.sync
                def _(sp):
                    sp.sem_clear(s["raw_in"])
                    for i, (t, src) in enumerate(zip(raw, (I["w1"], I["w3"], I["w2"]))):
                        sp.wait_ge(s["wl"], i + 1)
                        sp.dma_start(t[:], src[(e + 1) % NE]).then_inc(s["next"], 16)
                    sp.wait_ge(s["next"], 48)

                def high(act, n):
                    g, m = n // HT, n % HT
                    act.wait_ge(s["p"], n + 1)
                    if g >= 2:
                        act.wait_ge(s["D"], GT * (g - 1))
                    act.activation(hh[:, g % 2, m, :], p3[:, n % 2, :], ACT.Copy).then_inc(s["hh"], 1)

                @block.scalar
                def _(act):
                    for r, w in zip(raw, (w1, w3, w2)):
                        act.activation(w[0][:], r[:], ACT.Copy).then_inc(s["wh"], 1)
                    for n in range(NH_):
                        act.wait_ge(s["U"], n + 1)
                        if n >= 2:
                            act.wait_ge(s["p"], n - 1)
                        act.activation(th[:, n % 2, :], U1[n % 2][:], ACT.Tanh, scale=0.5).then_inc(s["th"], 1)
                        if n >= 1:
                            high(act, n - 1)
                    high(act, NH_ - 1)

                @block.vector
                def _(dve):
                    for i, (r, w) in enumerate(zip(raw, (w1, w3, w2))):
                        dve.wait_ge(s["wh"], i + 1)
                        dve.tensor_tensor(w[1][:], r[:], w[0][:].bitcast(F32), ALU.subtract).then_inc(s["wl"], 1)
                    dve.tensor_copy(now[:], comb[:, :, :, bass.ds(e, 1)].rearrange("p g t o -> p g (t o)")).then_inc(s["now"], 1)
                    dve.wait_ge(s["now"], 1)

                    def hidden(n):
                        dve.wait_ge(s["th"], n + 1)
                        if n >= 2:
                            dve.wait_ge(s["hl"], n - 1)
                        dve.scalar_tensor_tensor(out=th[:, n % 2, :], in0=th[:, n % 2, :], scalar=1.0, in1=U1[n % 2][:],
                                                 op0=ALU.add, op1=ALU.mult).then_inc(s["q"], 1)
                        dve.wait_ge(s["q"], n + 1)
                        dve.tensor_tensor(p3[:, n % 2, :], th[:, n % 2, :], U3[n % 2][:], ALU.mult).then_inc(s["p"], 1)

                    def low(n):
                        g, m = n // HT, n % HT
                        dve.wait_ge(s["hh"], n + 1)
                        dve.tensor_tensor(hl[:, g % 2, m, :], p3[:, n % 2, :], hh[:, g % 2, m, :].bitcast(F32),
                                          ALU.subtract).then_inc(s["hl"], 1)

                    def add(g):
                        for t in range(GT):
                            i = g * GT + t
                            dve.wait_ge(s["D"], i + 1)
                            dve.scalar_tensor_tensor(out=acc[:, g, t, :], in0=DN[t][:, 0:D], scalar=now[:, g, t:t + 1],
                                                     in1=acc[:, g, t, :], op0=ALU.mult, op1=ALU.add).then_inc(s["acc"], 1)

                    for n in range(NH_ + 1):
                        if n < NH_:
                            hidden(n)
                        if n >= 1:
                            low(n - 1)
                        if n % HT == 2 and n // HT >= 1:
                            add(n // HT - 1)
                    add(NG - 1)
                    dve.wait_ge(s["acc"], NG * GT)

                @block.tensor
                def _(pe):
                    def up(n):
                        g, m = n // HT, n % HT
                        if n >= 2:
                            pe.wait_ge(s["p"], n - 1)
                        for w, bank in ((w1, U1[n % 2]), (w3, U3[n % 2])):
                            if n == 0:
                                pe.wait_ge(s["wl"], 1 if w is w1 else 2)
                            for k in range(KD):
                                ins = split_matmul(pe, bank[:], [x[:, k, m * P:(m + 1) * P] for x in w],
                                                   (yh[:, g, k, :], yl[:, g, k, :]), k == 0, k == KD - 1)
                        ins.then_inc(s["U"], 1)

                    def down(g):
                        if g == 0:
                            pe.wait_ge(s["wl"], 3)
                        pe.wait_ge(s["hl"], HT * (g + 1))
                        for t in range(GT):
                            if g:
                                pe.wait_ge(s["acc"], GT * (g - 1) + t + 1)
                            for m in range(HT):
                                ins = split_matmul(pe, DN[t][:, 0:D], (hh[:, g % 2, m, t * P:(t + 1) * P],
                                                                       hl[:, g % 2, m, t * P:(t + 1) * P]),
                                                   [x[:, m, :] for x in w2], m == 0, m == HT - 1)
                            ins.then_inc(s["D"], 1)

                    for n in range(NH_):
                        up(n)
                        if n % HT == 1 and n // HT >= 1:
                            down(n // HT - 1)
                    down(NG - 1)

            with nc.Block() as block:
                @block.sync
                def _(sp):
                    clear(sp, s)

        with nc.Block() as block:
            @block.sync
            def _(sp):
                sp.dma_start(out.rearrange("(g t p) d -> p g t d", p=P, t=GT), acc[:]).then_inc(s["out"], 16)
                sp.wait_ge(s["out"], 16)

SEM_A = ("next_ctx next_mask xn xnT uh ul dtp dtf dtT J cv conv th xs Z zt zg nv e a chain av D Dhalf L small dec SM "
         "xT dx xd M xdd Y y YO yo yg ss yn yT yh yl O res")
SEM_B = "ones cl v V xn xnT uh ul qk QK sm S ex pt T o PV ol oT oh res R ch va chain"
SEM_C = ("repeat kB kT next_x xh stored l2 ones qkh qkl xr xT ul uh QKV rot built B sm S ex pta ptv T o PV oT ol R xr2 x2T ln ss "
         "oh h h2 chain")
SEM_E = ("gate_in yh_in yl_in acc_in raw_in gh gl G lgf GT lgm gex chain next now wh wl U th q p hh hl D acc out")



def decoder_layer(nc, I, out):
    with ExitStack() as ctx:
        def sb(name, shape, dt=F32):
            return ctx.enter_context(nc.sbuf_tensor(name, shape, dt))

        ps = [ctx.enter_context(nc.psum_tensor(f"bank{i}", [P, 512], F32)) for i in range(8)]
        K = {"const": sb("const", [P, C_N])}
        scratch = dict(
            res=nc.dram_tensor("residual", (NG, P, GT, D), F32, kind="Internal").ap(),
            h=nc.dram_tensor("x2_high", (NG, P, KD, GN), F32, kind="Internal").ap(),
            l=nc.dram_tensor("x2_low", (NG, P, KD, GN), F32, kind="Internal").ap())
        sA = semaphores(nc, ctx, "a", SEM_A)
        sB = semaphores(nc, ctx, "b", SEM_B)
        sC = semaphores(nc, ctx, "c", SEM_C)
        sE = semaphores(nc, ctx, "e", SEM_E)
        with ExitStack() as attn:
            def sb(name, shape, dt=F32):
                return attn.enter_context(nc.sbuf_tensor(name, shape, dt))

            K["rope"], K["taps"], K["tapb"], K["nw"] = sb("rope", [P, QT, 3, AD // 2]), sb("taps", [P, CT, TAPS]), sb("tapb", [P, CT]), sb("nw", [P, DI])
            K["moments"], K["moments_n"], K["stats"] = sb("moments", [P, GT, 2]), sb("moments_n", [P, GT, 2]), sb("stats", [P, GT, 6])
            K["identr"] = sb("identr", [P, P], FR)
            K["g1"], K["g2"] = sb("g1", [P, KD]), sb("g2", [P, KD])
            K["dtb"], K["alog"], K["A"], K["dpar"] = sb("dtb", [P, NH]), sb("alog", [P, NH]), sb("A", [P, NH]), sb("dpar", [P, NH])
            W = {}
            for n, shape in (("win", [P, KD, PROJ]), ("wout", [P, XT, D]), ("wq", [P, KD, XI]), ("wk", [P, KD, XI]),
                             ("wv", [P, KD, XI]), ("wo", [P, ET, D]), ("aqkv", [P, KD, AQKV]), ("awo", [P, KD, D])):
                W[n] = (sb(n + "_high", shape, FR), sb(n + "_low", shape, FR))
            XN, XG = sb("XN", [P, GT, D]), sb("XG", [P, GT, D])
            CX = sb("context", [P, KD, GN]), sb("mask", [P, GT, S])
            load_weights(nc, ctx, I, W, K, XN)
            with nc.Fori(0, NG) as g:
                stage_mamba(nc, ctx, g, I, W, K, XN, XG, CX, ps, sA, sC)
                stage_cross(nc, ctx, g, W, K, XG, CX, ps, sB, sA)
                stage_attention(nc, ctx, g, I, W, K, XN, XG, scratch, ps, sC, sB)
        stage_experts(nc, ctx, I, K, scratch, out, ps, sE)


def kernel(x, ctx_1024, fside_Bx1xSxS2_0, L0_attn_in_proj_w, L0_attn_conv_weight, L0_attn_conv_bias, L0_attn_dt_bias,
           L0_attn_A_log, L0_attn_D_param, L0_attn_norm_weight, L0_attn_out_proj_w, L0_xattn_Wq, L0_xattn_Wk,
           L0_xattn_Wv, L0_xattn_Wo, L0_ffn_g1, L0_ffn_g2, L0_ffn_wq, L0_ffn_wk, L0_ffn_wv, L0_ffn_wo, L0_ffn_gate,
           L0_ffn_w1, L0_ffn_w2, L0_ffn_w3):
    import numpy as _np
    import concourse.bacc as _bacc
    from concourse.bass_utils import run_bass_kernel_spmd as _run

    def rows(w):
        w = _np.asarray(w)
        return w.reshape(w.shape[0] // P, P, -1).transpose(1, 0, 2)

    def every(v):
        return _np.broadcast_to(_np.asarray(v), (P, _np.shape(v)[0]))

    laid = {
        "x": _np.asarray(x).reshape(NG, GT, P, D).transpose(0, 2, 1, 3),
        "ctxT": _np.asarray(ctx_1024).reshape(NG, GN, KD, P).transpose(0, 3, 2, 1),
        "mask": _np.asarray(fside_Bx1xSxS2_0).reshape(NG, GT, P, S).transpose(0, 2, 1, 3),
        "win": rows(L0_attn_in_proj_w), "wout": rows(L0_attn_out_proj_w),
        "taps": _np.asarray(L0_attn_conv_weight).reshape(CT, P, TAPS).transpose(1, 0, 2),
        "tapb": _np.asarray(L0_attn_conv_bias).reshape(CT, P).T,
        "nw": every(L0_attn_norm_weight),
        "dtb": every(L0_attn_dt_bias), "alog": every(L0_attn_A_log), "dpar": every(L0_attn_D_param),
        "wq": rows(_np.asarray(L0_xattn_Wq).T), "wk": rows(_np.asarray(L0_xattn_Wk).T), "wv": rows(_np.asarray(L0_xattn_Wv).T),
        "wo": rows(_np.asarray(L0_xattn_Wo).T),
        "aqkv": _np.concatenate([rows(L0_ffn_wq), rows(L0_ffn_wk), rows(L0_ffn_wv)], axis=2),
        "awo": rows(L0_ffn_wo), "gate": rows(L0_ffn_gate),
        "g1": _np.asarray(L0_ffn_g1).reshape(KD, P).T, "g2": _np.asarray(L0_ffn_g2).reshape(KD, P).T,
        "w1": _np.stack([rows(w) for w in _np.asarray(L0_ffn_w1)]), "w3": _np.stack([rows(w) for w in _np.asarray(L0_ffn_w3)]),
        "w2": _np.stack([rows(w) for w in _np.asarray(L0_ffn_w2)]),
        "const": constants(), "rope": rope_tables(),
    }
    nc = _bacc.Bacc("TRN2", target_bir_lowering=False, num_devices=1)
    arrays = {f"in_{n}": _np.ascontiguousarray(a) for n, a in laid.items()}
    I = {n: nc.dram_tensor(f"in_{n}", a.shape, F32, kind="ExternalInput").ap()
                           for n, a in ((n, arrays[f"in_{n}"]) for n in laid)}
    out = nc.dram_tensor("out", (TOK, D), F32, kind="ExternalOutput").ap()
    decoder_layer(nc, I, out)
    r = _run(nc, [arrays], core_ids=[0])
    return r.results[0]["out"].reshape(B, S, D)
```

```python
from contextlib import ExitStack

import numpy as np
import concourse.bass as bass
from concourse import mybir

F32 = mybir.dt.float32
I32 = mybir.dt.int32
FR = mybir.dt.float32r
ALU = mybir.AluOpType
ACT = mybir.ActivationFunctionType
AX_X = mybir.AxisListType.X

P = 128
B, S, D = 8, 256, 256
KD = D // P
TOK = B * S
GT = 4
NG = TOK // (P * GT)
GN = GT * P
QT = S // P

DI, NST, NH, HD, TAPS = 512, 128, 8, 64, 4
XT = DI // P
CT = XT + 2
PROJ = 2 * DI + 2 * NST + NH
LN_EPS, SSM_EPS = 1e-5, 1e-5

XH, XD = 16, 64
XI = XH * XD
ET = XI // P
VW = XD + 1

AH, AKV, AD = 16, 4, 16
REP = AH // AKV
AQKV = (AH + 2 * AKV) * AD
AVW = AD + 1
RMS_EPS = 1.1920928955078125e-07

NE, HID = 4, 3 * D
HT = HID // P

NEG = -1e30

C_ID, C_UPTO, C_AFTER, C_CAUSAL, C_ROW, C_LOW = 0, 128, 256, 384, 640, 644
C_N = C_LOW + NE * NE


def constants():
    c = np.zeros((P, C_N), np.float32)
    i = np.arange(P)
    c[:, C_ID:C_ID + P] = np.eye(P)
    c[:, C_UPTO:C_UPTO + P] = i[:, None] <= i[None, :]
    c[:, C_AFTER:C_AFTER + P] = i[:, None] > i[None, :]
    c[:, C_CAUSAL + P:C_CAUSAL + 2 * P] = np.where(i[None, :] > i[:, None], NEG, 0.0)
    c[:, C_ROW:C_ROW + REP] = (i[:, None] % (REP * AD)) // AD == np.arange(REP)[None, :]
    e = np.arange(NE)
    c[:, C_LOW:] = (e[None, :] < e[:, None]).reshape(1, NE * NE)
    return c


def rope_tables():
    inv = (1.0 / np.float32(10000.0) ** (np.arange(0, AD, 2, dtype=np.float32) / np.float32(AD))).astype(np.float32)
    ang = np.arange(S, dtype=np.float32)[:, None] * inv[None, :]
    t = np.stack([np.cos(ang), -np.sin(ang), np.sin(ang)], axis=1).astype(np.float32)
    return np.ascontiguousarray(t.reshape(QT, P, 3, AD // 2).transpose(1, 0, 2, 3))


def semaphores(nc, ctx, stage, names):
    return {n: ctx.enter_context(nc.semaphore(f"{stage}_{n}")) for n in names.split()}


def clear(sp, sems):
    for s in sems.values():
        sp.sem_clear(s)


def split_matmul(pe, out, a, b, start, stop):
    (ah, al), (bh, bl) = a, b
    pe.matmul(out, ah, bl, start=start, stop=False)
    pe.matmul(out, al, bh, start=False, stop=False)
    return pe.matmul(out, ah, bh, start=False, stop=stop)


class Chain:

    def __init__(self, eng, sem):
        self.eng, self.sem, self.n = eng, sem, 0

    def then(self, ins):
        self.n += 1
        ins.then_inc(self.sem, 1)

    def sync(self):
        if self.n:
            self.eng.wait_ge(self.sem, self.n)

    def link(self, ins):
        self.then(ins)
        self.sync()



def moments(dve, ch, src, st, mv):
    ch.link(dve.bn_stats(st, src))
    ch.then(dve.bn_aggr(mv, st))


def inverse_root(dve, ch, out, var, eps, tmp):
    ch.link(dve.tensor_scalar(tmp[1], var, eps, None, ALU.add))
    inverse_root_of(dve, ch, out, tmp)


def inverse_root_of(dve, ch, out, tmp):
    hv, t = tmp
    ch.then(dve.tensor_scalar(hv, t, -0.5, None, ALU.mult))
    ch.link(dve.tensor_scalar(out.bitcast(I32), t.bitcast(I32), 1, None, ALU.logical_shift_right))
    ch.link(dve.tensor_scalar(out.bitcast(I32), out.bitcast(I32), -1.0, float(0x5F3759DF), ALU.mult, ALU.add))
    for _ in range(3):
        ch.link(dve.tensor_tensor(t, out, out, ALU.mult))
        ch.link(dve.tensor_tensor(t, t, hv, ALU.mult))
        ch.link(dve.scalar_tensor_tensor(out=out, in0=t, scalar=1.5, in1=out, op0=ALU.add, op1=ALU.mult))


def normed(dve, ch, out, x, st, mv, rstd, nt, ready):
    for t in range(GT):
        moments(dve, ch, x[:, t, :], st[:, t, :], mv[:, t, :])
    ch.sync()
    inverse_root(dve, ch, rstd[:], mv[:, :, 1], LN_EPS, (nt[:, 0], nt[:, 1]))
    for t in range(GT):
        dve.tensor_scalar(out[:, t, :], x[:, t, :], mv[:, t, 0:1], rstd[:, t:t + 1],
                          ALU.subtract, ALU.mult).then_inc(ready, 1)


def transposes_in(pe, src, ident, banks, tiles, ready, done):
    for t in range(GT):
        pe.wait_ge(ready, t + 1)
        for k in range(tiles):
            ins = pe.transpose(banks[k][:, t * P:(t + 1) * P], src[:, t, k * P:(k + 1) * P], ident)
            if t == GT - 1:
                ins.then_inc(done, 1)


def part_high(act, out, psum, scale=None):
    if scale is None:
        return act.activation(out, psum, ACT.Copy)
    return act.activation(out, psum, ACT.Identity, scale=scale)


def part_low(dve, out, psum, high, scale=None):
    return dve.scalar_tensor_tensor(out=out, in0=psum, scalar=1.0 if scale is None else scale,
                                    in1=high.bitcast(F32), op0=ALU.mult, op1=ALU.subtract)



def load_weights(nc, ctx, I, W, K, XN, ps, stored):
    s = semaphores(nc, ctx, "w", "x_in chain identity_rounded const_in high_parts low_parts small_in wout_scaled "
                                 "alog_exp constants_ready x_normed x_turned x_high x_low")
    raws = [("win", I["win"]), ("wq", I["wq"]), ("wk", I["wk"]), ("wv", I["wv"]), ("wo", I["wo"]),
            ("aqkv", I["aqkv"]), ("awo", I["awo"]), ("wout", I["wout"])]
    by_pool = ("wk", "wo")
    loaded = {n: ctx.enter_context(nc.semaphore(f"w_{n}_in")) for n, _ in raws}
    with ExitStack() as own:
        st, mv, rstd, nt = (own.enter_context(nc.sbuf_tensor(f"w_{n}", shape, F32)) for n, shape in
                            (("st", [P, GT, 6]), ("mv", [P, GT, 2]), ("rstd", [P, GT]), ("nt", [P, 2, GT])))
        xn = own.enter_context(nc.sbuf_tensor("w_xn", [P, GT, D], F32))
        raw = {n: own.enter_context(nc.sbuf_tensor(f"raw_{n}", list(src.shape), F32)) for n, src in raws}
        block = own.enter_context(nc.Block())

        @block.sync
        def _(sp):
            sp.dma_start(XN[:], I["x"][0]).then_inc(s["x_in"], 16)
            for n, src in raws:
                sp.dma_start(raw[n][:], src).then_inc(loaded[n], 16)
            sp.wait_ge(s["x_in"], 16)
            sp.sem_inc(stored, 48)

        @block.tensor
        def _(pe):
            pe.wait_ge(s["const_in"], 16)
            transposes_in(pe, xn, K["const"][:, C_ID:C_ID + P], ps, KD, s["x_normed"], s["x_turned"])

        @block.scalar
        def _(act):
            act.dma_start(K["const"][:], I["const"]).then_inc(s["const_in"], 16)
            for n in ("rope", "taps", "tapb", "nw", "g1", "g2", "dtb", "alog", "dpar"):
                act.dma_start(K[n][:], I[n]).then_inc(s["small_in"], 16)
            for i, (n, _) in enumerate(raws):
                if n == "wout":
                    act.wait_ge(s["wout_scaled"], 1)
                act.wait_ge(loaded[n], 16)
                act.activation(W[n][0][:], raw[n][:], ACT.Copy).then_inc(s["high_parts"], 1)
                if i == 1:
                    for k in range(KD):
                        act.wait_ge(s["x_turned"], k + 1)
                        part_high(act, K["uh"][:, k, :], ps[k][:]).then_inc(s["x_high"], 1)
            act.wait_ge(s["const_in"], 16)
            act.activation(K["identr"][:], K["const"][:, C_ID:C_ID + P], ACT.Copy).then_inc(s["identity_rounded"], 1)
            act.wait_ge(s["small_in"], 144)
            act.activation(K["alog"][:], K["alog"][:], ACT.Exp).then_inc(s["alog_exp"], 1)

        @block.gpsimd
        def _(pool):
            for i, (n, _) in enumerate(raws):
                if n in by_pool:
                    pool.wait_ge(s["high_parts"], i + 1)
                    pool.tensor_tensor(W[n][1][:], raw[n][:], W[n][0][:].bitcast(F32), ALU.subtract).then_inc(s["low_parts"], 1)

        @block.vector
        def _(dve):
            ch = Chain(dve, s["chain"])
            dve.wait_ge(s["x_in"], 16)
            normed(dve, ch, xn, XN, st, mv, rstd, nt, s["x_normed"])
            for i, (n, _) in enumerate(raws):
                if i == 2:
                    for k in range(KD):
                        dve.wait_ge(s["x_high"], k + 1)
                        part_low(dve, K["ul"][:, k, :], ps[k][:], K["uh"][:, k, :]).then_inc(s["x_low"], 1)
                if n in by_pool:
                    continue
                if n == "wout":
                    dve.wait_ge(s["small_in"], 144)
                    ch.link(dve.tensor_scalar(K["nw"][:], K["nw"][:], float(DI) ** 0.5, None, ALU.mult))
                    dve.wait_ge(loaded[n], 16)
                    dve.tensor_tensor(raw[n][:], raw[n][:], K["nw"][:].unsqueeze(2).to_broadcast([P, XT, D]),
                                      ALU.mult).then_inc(s["wout_scaled"], 1)
                    dve.wait_ge(s["wout_scaled"], 1)
                dve.wait_ge(s["high_parts"], i + 1)
                dve.tensor_tensor(W[n][1][:], raw[n][:], W[n][0][:].bitcast(F32), ALU.subtract).then_inc(s["low_parts"], 1)
            dve.wait_ge(s["alog_exp"], 1)
            dve.tensor_scalar(K["A"][:], K["alog"][:], -1.0, None, ALU.mult).then_inc(s["constants_ready"], 1)
            dve.tensor_scalar(K["taps"][:], K["taps"][:], 0.5, None, ALU.mult).then_inc(s["constants_ready"], 1)
            dve.tensor_scalar(K["tapb"][:], K["tapb"][:], 0.5, None, ALU.mult).then_inc(s["constants_ready"], 1)
            ch.sync()
    return s



def stage_mamba(nc, ctx, g, I, W, K, XN, XG, CX, ps, s, last):
    with ExitStack() as own:
        def sb(name, shape, dt=F32):
            return own.enter_context(nc.sbuf_tensor("a_" + name, shape, dt))

        y = sb("y", [P, GT, DI])
        st, nt = sb("st", [P, GT, 6]), sb("nt", [P, 2, GT])
        uh, ul = K["uh"], K["ul"]
        cv, th = sb("cv", [P, 2, GN]), sb("th", [P, 2, GN])
        xs = sb("xs", [P, CT, GN])
        zg = sb("zg", [P, GT, DI])
        dtf = th[0:NH, 1, :]
        v, r, e, den, zz, z2, acc, dt, a = (sb(n, [P, GT, NH]) for n in "v r e den zz z2 acc dt a".split())
        av = sb("av", [P, 2, NH, P])
        lm = sb("lm", [P, 2, NH, P])
        gm = sb("gm", [P, 2, P])
        g01 = sb("g01", [P, P])
        dec = sb("dec", [P, GT, NH])
        xd = sb("xd", [P, 2, DI])
        xdd = sb("xdd", [P, DI])
        yo, sq = cv[:, 0, :], th[:, 0, :]
        ss, rs = sb("ss", [P, GT]), sb("rs", [P, GT])
        yh, yl = sb("yh", [P, GT, XT, P], FR), sb("yl", [P, GT, XT, P], FR)

        T, J, DB, YO, SM = ps[0:2], ps[2:4], ps[4:6], ps[6], ps[7]
        ZB = (YO, DB[1], T[1], DB[0])
        ident = K["const"][:, C_ID:C_ID + P]
        upto, after = K["const"][:, C_UPTO:C_UPTO + P], K["const"][:, C_AFTER:C_AFTER + P]
        ORDER = [XT, XT + 1, *range(XT)]
        HH = NH // 2
        block = own.enter_context(nc.Block())

        @block.sync
        def _(sp):
            sp.dma_start(CX[0][:], I["ctxT"][g]).then_inc(s["next_ctx"], 16)
            sp.dma_start(CX[1][:], I["mask"][g]).then_inc(s["next_mask"], 16)
            sp.wait_ge(s["x_times_dt"], 1)
            clear(sp, last)
            sp.wait_ge(s["next_ctx"], 16)
            sp.wait_ge(s["next_mask"], 16)

        @block.gpsimd
        def _(pool):
            pool.wait_ge(s["decay_rates"], 1)
            for t in range(GT):
                if t >= 2:
                    pool.wait_ge(s["decay_sums"], t - 1)
                pool.tensor_tensor(av[:, t % 2], a[:, t, :].unsqueeze(2).to_broadcast([P, NH, P]),
                                   upto.unsqueeze(1).to_broadcast([P, NH, P]), ALU.mult).then_inc(s["decays_masked"], 1)

        @block.tensor
        def _(pe):
            def dt_projection():
                for k in range(KD):
                    ins = split_matmul(pe, SM[0:NH, :], [w[:, k, PROJ - NH:PROJ] for w in W["win"]],
                                       (uh[:, k, :], ul[:, k, :]), k == 0, k == KD - 1)
                ins.then_inc(s["dt_projected"], 1)

            def turn_dt():
                pe.wait_ge(s["dt_copied"], 1)
                for t in range(GT):
                    ins = pe.transpose(SM[:, t * NH:(t + 1) * NH], dtf[:, t * P:(t + 1) * P], ident[0:NH, 0:NH])
                ins.then_inc(s["dt_turned"], 1)

            dt_projection()
            for n in range(CT):
                if n >= 2:
                    pe.wait_ge(s["conv_done"], n - 1)
                w0 = DI + ORDER[n] * P
                for k in range(KD):
                    ins = split_matmul(pe, J[n % 2][:], [w[:, k, w0:w0 + P] for w in W["win"]],
                                       (uh[:, k, :], ul[:, k, :]), k == 0, k == KD - 1)
                ins.then_inc(s["conv_projected"], 1)
                if n == 0:
                    turn_dt()
                elif n <= GT:
                    t = n - 1
                    for k in range(KD):
                        ins = split_matmul(pe, ZB[t][:], (uh[:, k, t * P:(t + 1) * P], ul[:, k, t * P:(t + 1) * P]),
                                           [w[:, k, 0:DI] for w in W["win"]], k == 0, k == KD - 1)
                    ins.then_inc(s["z_projected"], 1)

            def front(t):
                c = t % QT
                if t == 0:
                    pe.wait_ge(s["conv_silu"], CT)
                if t >= 2:
                    pe.wait_ge(s["x_bank_read"], t - 1)
                for k in range(XT):
                    ins = pe.transpose(T[t % 2][:, k * P:(k + 1) * P], xs[:, k, t * P:(t + 1) * P], ident)
                ins.then_inc(s["x_turned"], 1)
                if t == 0:
                    pe.wait_ge(s["decay_rates"], 1)
                else:
                    pe.wait_ge(s["small_bank_read"], t)
                pe.matmul(SM[:, 0:P], xs[:, XT, t * P:(t + 1) * P], xs[:, XT + 1, t * P:(t + 1) * P], start=True, stop=True)
                if c:
                    pe.matmul(SM[:, P:2 * P], xs[:, XT, (t - 1) * P:t * P], xs[:, XT + 1, t * P:(t + 1) * P],
                              start=True, stop=True)
                ins = pe.matmul(SM[:, 2 * P:2 * P + NH], upto if c else after, a[:, t, :], start=True, stop=True)
                ins.then_inc(s["chunk_scores"], 1)
                pe.wait_ge(s["decays_masked"], t + 1)
                for i, bank in enumerate(DB):
                    if t:
                        pe.wait_ge(s["decays_exp"], 2 * t - 1 + i)
                    elif i == 0:
                        pe.wait_ge(s["z_gated"], GT)
                    ins = pe.matmul(bank[:], after, av[:, t % 2, i * HH:(i + 1) * HH, :], start=True, stop=True)
                    ins.then_inc(s["decay_sums_half"], 1)
                pe.wait_ge(s["decay_sums_half"], 2 * t + 2)
                pe.sem_inc(s["decay_sums"], 1)

            def mid(t):
                pe.wait_ge(s["scores_decayed"], t + 1)
                if t >= 2:
                    pe.wait_ge(s["y_bank_read"], t - 1)
                for h in range(NH):
                    ins = pe.matmul(J[t % 2][:, h * HD:(h + 1) * HD], lm[:, t % 2, h, :], xd[:, t % 2, h * HD:(h + 1) * HD],
                                    start=True, stop=True)
                ins.then_inc(s["y_product"], 1)
                if t % QT:
                    pe.wait_ge(s["x_decayed"], t // QT + 1)
                    if t // QT:
                        pe.wait_ge(s["state_part"], t // QT)
                    pe.matmul(YO[:], g01[:], xdd[:], start=True, stop=True).then_inc(s["state_product"], 1)

            def turn(t):
                pe.wait_ge(s["y_gated"], t + 1)
                pe.wait_ge(s["x_bank_read"], min(t + 3, GT))
                if t >= 2:
                    pe.wait_ge(s["y_low"], t - 1)
                for k in range(XT):
                    ins = pe.transpose(T[t % 2][:, k * P:(k + 1) * P], y[:, t, k * P:(k + 1) * P], ident)
                ins.then_inc(s["y_turned"], 1)

            def project(t):
                pe.wait_ge(s["y_low"], t + 1)
                if t >= 2:
                    pe.wait_ge(s["residual_added"], t - 1)
                for k in range(XT):
                    ins = split_matmul(pe, DB[t % 2][:, 0:D], (yh[:, t, k, :], yl[:, t, k, :]),
                                       [w[:, k, :] for w in W["wout"]], k == 0, k == XT - 1)
                ins.then_inc(s["out_projected"], 1)

            for i in range(GT + 1):
                if i < GT:
                    front(i)
                if i >= 1:
                    mid(i - 1)
                if i >= 2:
                    turn(i - 2)
            for t in range(GT):
                project(t)
                if t == 0:
                    turn(GT - 1)

        @block.scalar
        def _(act):
            act.wait_ge(s["dt_projected"], 1)
            act.activation(dtf, SM[0:NH, :], ACT.Copy).then_inc(s["dt_copied"], 1)
            for n in range(CT + 1):
                if n < CT:
                    f = ORDER[n]
                    act.wait_ge(s["conv_projected"], n + 1)
                    if n >= 2:
                        act.wait_ge(s["conv_silu"], n - 1)
                    act.activation(cv[:, n % 2, :], J[n % 2][:], ACT.Identity, bias=K["tapb"][:, f:f + 1],
                                   scale=K["taps"][:, f, TAPS - 1:TAPS]).then_inc(s["conv_begun"], 1)
                if n >= 1:
                    act.wait_ge(s["conv_done"], n)
                    act.activation(th[:, (n - 1) % 2, :], cv[:, (n - 1) % 2, :], ACT.Tanh).then_inc(s["conv_tanh"], 1)
                if n == 1:
                    act.wait_ge(s["minus_abs_dt"], 1)
                    act.activation(e[:], e[:], ACT.Exp).then_inc(s["exp_dt"], 1)
                if 2 <= n < GT + 2:
                    t = n - 2
                    act.wait_ge(s["z_projected"], t + 1)
                    act.activation(zg[:, t, :], ZB[t][:], ACT.Tanh, scale=0.5).then_inc(s["z_tanh"], 1)

            def high(t):
                act.wait_ge(s["y_turned"], t + 1)
                part_high(act, yh[:, t].rearrange("p k n -> p (k n)"), T[t % 2][:]).then_inc(s["y_high"], 1)

            def squares(t):
                act.wait_ge(s["y_gated"], t + 1)
                if t:
                    act.wait_ge(s["y_squares"], t)
                act.activation(sq, y[:, t, :], ACT.Square, accum_out=ss[:, t:t + 1]).then_inc(s["y_squares"], 1)

            for t in range(GT):
                if t >= 2:
                    act.wait_ge(s["y_product"], t - 1)
                for j, bank in enumerate(DB):
                    act.wait_ge(s["decay_sums_half"], 2 * t + j + 1)
                    act.activation(lm[:, t % 2, j * HH:(j + 1) * HH, :], bank[:], ACT.Exp).then_inc(s["decays_exp"], 1)
                act.wait_ge(s["small_bank_read"], t + 1)
                act.activation(dec[:, t, :], dec[:, t, :], ACT.Exp).then_inc(s["chunk_decays_exp"], 1)
                if t >= 2:
                    high(t - 2)
                    squares(t - 2)
            for t in (GT - 2, GT - 1):
                high(t)
                squares(t)

        @block.vector
        def _(dve):
            ch = Chain(dve, s["chain"])

            def convolve(n):
                f = ORDER[n]
                dve.wait_ge(s["conv_begun"], n + 1)
                out = cv[:, n % 2, :].rearrange("p (b l) -> p b l", b=2)
                src = J[n % 2][:].rearrange("p (b l) -> p b l", b=2)
                for k in range(1, TAPS):
                    if k > 1:
                        ch.sync()
                    ins = dve.scalar_tensor_tensor(out=out[:, :, k:], in0=src[:, :, 0:S - k],
                                                   scalar=K["taps"][:, f, TAPS - 1 - k:TAPS - k], in1=out[:, :, k:],
                                                   op0=ALU.mult, op1=ALU.add)
                    if k < TAPS - 1:
                        ch.then(ins)
                ins.then_inc(s["conv_done"], 1)

            def activate(n):
                dve.wait_ge(s["conv_tanh"], n + 1)
                dve.wait_ge(s["conv_done"], n + 1)
                dve.scalar_tensor_tensor(out=xs[:, ORDER[n], :], in0=th[:, n % 2, :], scalar=1.0, in1=cv[:, n % 2, :],
                                         op0=ALU.add, op1=ALU.mult).then_inc(s["conv_silu"], 1)

            convolve(0)
            dve.wait_ge(s["dt_turned"], 1)
            ch.link(dve.tensor_tensor(v[:], SM[:, 0:GT * NH].rearrange("p (t h) -> p t h", t=GT),
                                      K["dtb"][:].unsqueeze(1).to_broadcast([P, GT, NH]), ALU.add))
            ch.link(dve.tensor_scalar(r[:], v[:], 0.0, None, ALU.max))
            dve.scalar_tensor_tensor(out=e[:], in0=r[:], scalar=-2.0, in1=v[:], op0=ALU.mult,
                                     op1=ALU.add).then_inc(s["minus_abs_dt"], 1)
            convolve(1)
            activate(0)
            dve.wait_ge(s["exp_dt"], 1)
            ch.link(dve.tensor_scalar(den[:], e[:], 2.0, None, ALU.add))
            ch.link(dve.reciprocal(den[:], den[:]))
            ch.link(dve.tensor_tensor(zz[:], e[:], den[:], ALU.mult))
            ch.link(dve.tensor_tensor(z2[:], zz[:], zz[:], ALU.mult))
            ch.link(dve.tensor_scalar(acc[:], z2[:], 1.0 / 15, None, ALU.mult))
            for m in (13, 11, 9, 7, 5, 3):
                ch.link(dve.scalar_tensor_tensor(out=acc[:], in0=acc[:], scalar=1.0 / m, in1=z2[:],
                                                 op0=ALU.add, op1=ALU.mult))
            ch.link(dve.scalar_tensor_tensor(out=acc[:], in0=acc[:], scalar=1.0, in1=zz[:], op0=ALU.add, op1=ALU.mult))
            ch.link(dve.scalar_tensor_tensor(out=dt[:], in0=acc[:], scalar=2.0, in1=r[:], op0=ALU.mult, op1=ALU.add))
            dve.tensor_tensor(a[:], dt[:], K["A"][:].unsqueeze(1).to_broadcast([P, GT, NH]), ALU.mult).then_inc(s["decay_rates"], 1)
            for n in range(2, CT):
                convolve(n)
                activate(n - 1)
            activate(CT - 1)

            def heads(ap):
                return ap.rearrange("p (h d) -> p h d", h=NH)

            def wide(ap):
                return ap.unsqueeze(2).to_broadcast([P, NH, HD])

            def gates():
                for t in range(GT):
                    dve.wait_ge(s["z_tanh"], t + 1)
                    dve.scalar_tensor_tensor(out=zg[:, t, :], in0=zg[:, t, :], scalar=1.0, in1=ZB[t][:],
                                             op0=ALU.add, op1=ALU.mult).then_inc(s["z_gated"], 1)

            def front(t):
                c = t % QT
                dve.wait_ge(s["chunk_scores"], t + 1)
                ch.link(dve.tensor_tensor(gm[:, t % 2, :], SM[:, 0:P], upto, ALU.mult))
                if c:
                    if t // QT:
                        dve.wait_ge(s["state_product"], t // QT)
                    ch.link(dve.tensor_copy(g01[:], SM[:, P:2 * P]))
                dve.tensor_copy(dec[:, t, :], SM[:, 2 * P:2 * P + NH]).then_inc(s["small_bank_read"], 1)
                if t >= 2:
                    dve.wait_ge(s["y_product"], t - 1)
                dve.tensor_tensor(heads(xd[:, t % 2, :]), heads(T[t % 2][:]), wide(dt[:, t, :]), ALU.mult).then_inc(s["x_times_dt"], 1)
                dve.tensor_tensor(heads(y[:, t, :]), heads(T[t % 2][:]), wide(K["dpar"][:]), ALU.mult).then_inc(s["x_bank_read"], 1)

            def decays(t):
                dve.wait_ge(s["decays_exp"], 2 * t + 2)
                dve.tensor_tensor(lm[:, t % 2], lm[:, t % 2], gm[:, t % 2, :].unsqueeze(1).to_broadcast([P, NH, P]),
                                  ALU.mult).then_inc(s["scores_decayed"], 1)
                if t % QT:
                    dve.wait_ge(s["chunk_decays_exp"], t)
                    dve.wait_ge(s["x_times_dt"], t)
                    if t // QT:
                        dve.wait_ge(s["state_product"], t // QT)
                    dve.tensor_tensor(heads(xdd[:]), heads(xd[:, (t - 1) % 2, :]), wide(dec[:, t - 1, :]),
                                      ALU.mult).then_inc(s["x_decayed"], 1)

            def mid(t):
                dve.wait_ge(s["y_product"], t + 1)
                dve.wait_ge(s["x_bank_read"], t + 1)
                dve.tensor_tensor(y[:, t, :], y[:, t, :], J[t % 2][:], ALU.add).then_inc(s["y_bank_read"], 1)
                dve.wait_ge(s["y_bank_read"], t + 1)
                if t % QT:
                    dve.wait_ge(s["state_product"], t // QT + 1)
                    dve.wait_ge(s["chunk_decays_exp"], t + 1)
                    dve.tensor_tensor(heads(yo), heads(YO[:]), wide(dec[:, t, :]), ALU.mult).then_inc(s["state_part"], 1)
                    dve.wait_ge(s["state_part"], t // QT + 1)
                    ch.link(dve.tensor_tensor(y[:, t, :], y[:, t, :], yo, ALU.add))
                dve.tensor_tensor(y[:, t, :], y[:, t, :], zg[:, t, :], ALU.mult).then_inc(s["y_gated"], 1)

            def low(t):
                dve.wait_ge(s["y_high"], t + 1)
                part_low(dve, yl[:, t].rearrange("p k n -> p (k n)"), T[t % 2][:],
                         yh[:, t].rearrange("p k n -> p (k n)")).then_inc(s["y_low"], 1)

            for i in range(GT + 1):
                if i < GT:
                    if i == 0:
                        gates()
                        dve.wait_ge(last["stored"], 48)
                    dve.wait_ge(s["x_turned"], i + 1)
                    front(i)
                    decays(i)
                if i >= 1:
                    mid(i - 1)
                if i >= 2:
                    low(i - 2)
            low(GT - 1)
            dve.wait_ge(s["y_squares"], GT)
            inverse_root(dve, ch, rs[:], ss[:], 4 * DI * SSM_EPS, (nt[:, 0], nt[:, 1]))
            for t in range(GT):
                dve.wait_ge(s["out_projected"], t + 1)
                dve.scalar_tensor_tensor(out=XG[:, t, :], in0=DB[t % 2][:, 0:D], scalar=rs[:, t:t + 1],
                                         in1=XN[:, t, :], op0=ALU.mult, op1=ALU.add).then_inc(s["residual_added"], 1)
                dve.wait_ge(s["residual_added"], t + 1)
                moments(dve, ch, XG[:, t, :], st[:, t, :], K["moments"][:, t, :])
            ch.sync()



def stage_cross(nc, ctx, g, W, K, XG, CX, ps, s, last):
    with ExitStack() as own:
        def sb(name, shape, dt=F32):
            return own.enter_context(nc.sbuf_tensor("b_" + name, shape, dt))

        st, rstd, nt = sb("st", [P, GT, 6]), sb("rstd", [P, GT]), sb("nt", [P, 2, GT])
        mv = K["moments"]
        uh, ul = K["uh"], K["ul"]
        cr, mask = CX
        eh, el = sb("eh", [P, KD * GN], FR), sb("el", [P, KD * GN], FR)
        c = [e[:].rearrange("p (k n) -> p k n", k=KD) for e in (eh, el)]
        qst, kst = sb("qst", [P, 2, 2, GN], FR), sb("kst", [P, 2, 2, GN], FR)
        ql, kh, kl = sb("ql", [P, GN], FR), sb("kh", [P, GN], FR), sb("kl", [P, 2, GN], FR)
        va = sb("va", [P, GT, XH, VW])
        pp = sb("pp", [P, 3, QT, S])
        xn = pp[:].rearrange("p a q k -> p (a q k)")[:, 0:GT * D].rearrange("p (t d) -> p t d", t=GT)
        nm = sb("nm", [P, 4, QT])
        pt = sb("pt", [P, 2, 2 * S])
        rc = sb("rc", [P, 2, QT, 2])
        ot = sb("ot", [P, GT, XI])

        PJ, S3, T2, O2 = ps[0], ps[1:4], ps[4:6], ps[6:8]
        ident = K["const"][:, C_ID:C_ID + P]
        NU = ET * 2
        NHD = 2 * NU
        NV = GT * 2
        EARLY = (NHD - 6, NHD - 4, NHD - 2, NHD)
        TB = (PJ, PJ, PJ, PJ, T2[0], T2[1], PJ, T2[0])
        RB = (*S3, O2[0])
        block = own.enter_context(nc.Block())

        def heads(part, t):
            x = ((eh, el)[part][:, t * 4 * P:(t + 1) * 4 * P] if t < 2 else K[("uh", "ul")[part]][:, t - 2, :])
            return x.rearrange("p (k n) -> p k n", k=4)

        def bank_of(n):
            return (*O2, *T2)[n] if n < 4 else PJ

        def tokens(b, qt):
            return slice((b * QT + qt) * P, (b * QT + qt + 1) * P)

        own_rows = (slice(0, XD), slice(XD, P))
        PT = (s["probs_placed_by_scalar"], s["probs_placed_by_vector"])
        Q_AT, K_AT = 1, 3
        MQ, MK = (s["q_moved_even"], s["q_moved_odd"]), (s["k_moved_even"], s["k_moved_odd"])

        @block.sync
        def _(sp):
            clear(sp, last)
            for j in range(ET):
                sp.wait_ge(s["q_low"], j + 1)
                for hp in range(2):
                    sp.dma_start(qst[own_rows[1 - hp], j % 2, hp, :].bitcast(F32),
                                 ql[own_rows[hp], :].bitcast(F32)).then_inc(MQ[j % 2], 16)
                sp.wait_ge(s["k_high"], j + 1)
                for hp in range(2):
                    for rows in own_rows:
                        sp.dma_start(kst[rows, j % 2, hp, :].bitcast(F32),
                                     kh[own_rows[hp], :].bitcast(F32)).then_inc(MK[j % 2], 16)

        @block.gpsimd
        def _(pool):
            pool.memset(va[:, :, :, XD], 1.0).then_inc(s["ones_set"], 1)

        @block.tensor
        def _(pe):
            def project_v(n):
                t, half = n // 2, n % 2
                bank = (PJ, *S3)[n % 4]
                if n >= 4:
                    pe.wait_ge((s["v_placed_by_scalar"], s["v_placed_by_vector"])[n % 2], n // 2 - 1)
                for k in range(KD):
                    ins = split_matmul(pe, bank[:], [x[:, k, t * P:(t + 1) * P] for x in c],
                                       [w[:, k, half * 512:(half + 1) * 512] for w in W["wv"]], k == 0, k == KD - 1)
                ins.then_inc(s["v_projected"], 1)

            def project(j, which):
                n = 2 * j + which
                if n >= 4:
                    pe.wait_ge(*((s["q_low"], j + 1) if which else (s["k_low"], j)))
                w, x = (W["wq"], (uh, ul)) if which == 0 else (W["wk"], c)
                for k in range(KD):
                    ins = split_matmul(pe, bank_of(n)[:], [a[:, k, j * P:(j + 1) * P] for a in w],
                                       [a[:, k, :] for a in x], k == 0, k == KD - 1)
                ins.then_inc(s["qk_projected"], 1)

            def scores(n):
                u, hp = n // 2, n % 2
                j, b = u // 2, u % 2
                if b == 0 and hp == 0:
                    pe.wait_ge(s["k_low"], j + 1)
                    pe.wait_ge(MQ[j % 2], 32 * (j // 2 + 1))
                    pe.wait_ge(MK[j % 2], 64 * (j // 2 + 1))
                if n >= 3:
                    pe.wait_ge(s["scores_masked"], 2 * (n - 2))
                r = own_rows[hp]
                for qt in range(QT):
                    out = S3[n % 3][:, qt * S:(qt + 1) * S]
                    pe.matmul(out, qst[r, j % 2, hp, tokens(b, qt)], kl[r, j % 2, b * S:(b + 1) * S], start=True, stop=False)
                    ins = pe.matmul(out, qst[:, j % 2, hp, tokens(b, qt)], kst[:, j % 2, hp, b * S:(b + 1) * S],
                                    start=False, stop=True)
                ins.then_inc(s["scores_ready"], 1)

            def turn(n):
                pe.wait_ge(s["probs_exp"], 2 * (n + 1))
                if n >= 2:
                    pe.wait_ge(PT[n % 2], n // 2)
                else:
                    pe.wait_ge((s["q_low"], s["k_low"])[n], 2)
                for kt in range(QT):
                    for qt in range(QT):
                        ins = pe.transpose(T2[n % 2][:, kt * S + qt * P:kt * S + (qt + 1) * P],
                                           pp[:, n % 3, qt, kt * P:(kt + 1) * P], ident)
                ins.then_inc(s["probs_turned"], 1)

            def values(n):
                u, hp = n // 2, n % 2
                j, b = u // 2, u % 2
                pe.wait_ge(PT[n % 2], n // 2 + 1)
                if hp == 0 and u >= 2:
                    pe.wait_ge(s["heads_normalised"], u - 1)
                for qt in range(QT):
                    for kt in range(QT):
                        at = (hp * QT + qt) * VW
                        ins = pe.matmul(O2[u % 2][:, at:at + VW], pt[:, n % 2, kt * S + qt * P:kt * S + (qt + 1) * P],
                                        va[:, b * QT + kt, 2 * j + hp, :], start=kt == 0, stop=kt == QT - 1)
                ins.then_inc(s["values_ready"], 1)

            def turn_heads(i):
                t, h = i % GT, i // GT
                if TB[i] in TB[:i]:
                    pe.wait_ge(s["heads_low"], i - TB[:i][::-1].index(TB[i]))
                for m in range(4):
                    k = 4 * h + m
                    ins = pe.transpose(TB[i][:, m * P:(m + 1) * P], ot[:, t, k * P:(k + 1) * P], ident)
                ins.then_inc(s["heads_turned"], 1)

            pe.wait_ge(s["context_low"], 1)
            for n in range(4):
                project_v(n)
            transposes_in(pe, xn, ident, T2, KD, s["x_normed"], s["x_turned"])
            project_v(4)
            project_v(5)
            pe.wait_ge(s["x_low"], KD)
            project(0, 0)
            project(0, 1)
            project_v(6)
            project_v(7)
            project(1, 0)
            project(1, 1)
            pe.wait_ge(s["ones_set"], 1)
            pe.wait_ge(s["v_placed_by_scalar"], NV // 2)
            pe.wait_ge(s["v_placed_by_vector"], NV // 2)
            scores(0)
            scores(1)
            for n in range(NHD + 1):
                if n + 2 < NHD:
                    scores(n + 2)
                if n < NHD:
                    turn(n)
                if n % 4 in (Q_AT, K_AT) and n // 4 + 2 < ET:
                    project(n // 4 + 2, (Q_AT, K_AT).index(n % 4))
                if n >= 1:
                    values(n - 1)
                if n in EARLY:
                    i = EARLY.index(n)
                    if i == 0:
                        pe.wait_ge(s["k_low"], ET)
                        pe.wait_ge(s["heads_normalised"], NU // 2)
                    turn_heads(i)

            def project_out(i):
                t, h = i % GT, i // GT
                pe.wait_ge(s["heads_low"], i + 1)
                for m in range(4):
                    k = 4 * h + m
                    ins = split_matmul(pe, RB[t][:, 0:D], [heads(part, t)[:, m, :] for part in range(2)],
                                       [w[:, k, :] for w in W["wo"]], k == 0, k == ET - 1)
                ins.then_inc(s["out_projected"], 1)

            pe.wait_ge(s["scores_masked"], 2 * NHD)
            project_out(0)
            project_out(1)
            pe.wait_ge(s["heads_normalised"], NU)
            turn_heads(4)
            turn_heads(5)
            project_out(2)
            project_out(3)
            turn_heads(6)
            project_out(4)
            turn_heads(7)
            project_out(5)
            project_out(6)
            project_out(7)

        @block.scalar
        def _(act):
            act.activation(eh[:].rearrange("p (k n) -> p k n", k=KD), cr[:], ACT.Copy).then_inc(s["context_high"], 1)

            def place_v(n):
                t, half, bank = n // 2, n % 2, (PJ, *S3)[n % 4]
                act.wait_ge(s["v_projected"], n + 1)
                act.activation(va[:, t, half * 8:half * 8 + 8, 0:XD], bank[:].rearrange("p (h d) -> p h d", h=8),
                               ACT.Copy).then_inc(s["v_placed_by_scalar"], 1)

            def place(n):
                j, which = n // 2, n % 2
                act.wait_ge(s["qk_projected"], n + 1)
                if j >= 2:
                    act.wait_ge(s["scores_ready"], 4 * (j - 1))
                if which == 0:
                    for hp, r in enumerate(own_rows):
                        ins = act.activation(qst[r, j % 2, hp, :], bank_of(n)[r, :], ACT.Copy)
                    ins.then_inc(s["q_high"], 1)
                else:
                    if j:
                        act.wait_ge(MK[(j - 1) % 2], 64 * ((j - 1) // 2 + 1))
                        act.wait_ge(s["k_low"], j)
                    act.activation(kh[:], bank_of(n)[:], ACT.Copy).then_inc(s["k_high"], 1)

            def high(i):
                act.wait_ge(s["heads_turned"], i + 1)
                if i >= GT:
                    act.wait_ge(s["out_projected"], i - GT + 1)
                act.activation(heads(0, i % GT), TB[i][:].rearrange("p (k n) -> p k n", k=4), ACT.Copy).then_inc(s["heads_high"], 1)

            place_v(0)
            place_v(2)
            for k in range(KD):
                act.wait_ge(s["x_turned"], k + 1)
                part_high(act, uh[:, k, :], T2[k][:]).then_inc(s["x_high"], 1)
            place_v(4)
            place(0)
            place(1)
            place_v(6)
            place(2)
            place(3)
            for n in range(NHD):
                for qt in range(QT):
                    act.wait_ge(s["scores_masked"], 2 * n + qt + 1)
                    act.activation(pp[:, n % 3, qt, :], pp[:, n % 3, qt, :], ACT.Exp, bias=nm[:, n % 4, qt:qt + 1],
                                   scale=-1.0).then_inc(s["probs_exp"], 1)
                if n % 2:
                    act.wait_ge(s["probs_turned"], n)
                    if n >= 3:
                        act.wait_ge(s["values_ready"], n - 2)
                    act.activation(pt[:, 0, :], T2[0][:], ACT.Copy).then_inc(s["probs_placed_by_scalar"], 1)
                if n >= 1 and (n - 1) % 4 in (Q_AT, K_AT) and (n - 1) // 4 + 2 < ET:
                    place(2 * ((n - 1) // 4 + 2) + (Q_AT, K_AT).index((n - 1) % 4))
                if n - 1 in EARLY:
                    high(EARLY.index(n - 1))
            for i in range(EARLY.index(NHD), 2 * GT):
                high(i)

        @block.vector
        def _(dve):
            ch = Chain(dve, s["chain"])
            dve.wait_ge(s["context_high"], 1)
            dve.tensor_tensor(c[1], cr[:], c[0].bitcast(F32), ALU.subtract).then_inc(s["context_low"], 1)
            inverse_root(dve, ch, rstd[:], mv[:, :, 1], LN_EPS, (nt[:, 0], nt[:, 1]))
            for t in range(GT):
                dve.tensor_scalar(xn[:, t, :], XG[:, t, :], mv[:, t, 0:1], rstd[:, t:t + 1],
                                  ALU.subtract, ALU.mult).then_inc(s["x_normed"], 1)

            def place_v(n):
                t, half, bank = n // 2, n % 2, (PJ, *S3)[n % 4]
                dve.wait_ge(s["v_projected"], n + 1)
                dve.tensor_copy(va[:, t, half * 8:half * 8 + 8, 0:XD],
                                bank[:].rearrange("p (h d) -> p h d", h=8)).then_inc(s["v_placed_by_vector"], 1)

            def masked(n):
                b = n // 2 % 2
                dve.wait_ge(s["scores_ready"], n + 1)
                if n >= 3:
                    dve.wait_ge(s["probs_turned"], n - 2)
                for qt in range(QT):
                    dve.tensor_tensor_reduce(out=pp[:, n % 3, qt, :], in0=S3[n % 3][:, qt * S:(qt + 1) * S],
                                             in1=mask[:, b * QT + qt, :], scale=-1.0, scalar=3e38, op0=ALU.add,
                                             op1=ALU.min, accum_out=nm[:, n % 4, qt:qt + 1]).then_inc(s["scores_masked"], 1)

            def place(n):
                dve.wait_ge(s["probs_turned"], n + 1)
                if n >= 2:
                    dve.wait_ge(s["values_ready"], n - 1)
                dve.tensor_copy(pt[:, n % 2, :], T2[n % 2][:]).then_inc(s["probs_placed_by_vector"], 1)

            def normalise(u):
                j, b = u // 2, u % 2
                dve.wait_ge(s["values_ready"], 2 * u + 2)
                src = O2[u % 2][:, 0:4 * VW].rearrange("p (h q d) -> p h q d", h=2, q=QT)
                r = rc[:, u % 2].rearrange("p a b -> p (a b)").rearrange("p (h q) -> p h q", h=2)
                ch.link(dve.reciprocal(r, src[:, :, :, XD]))
                for hp in range(2):
                    h = 2 * j + hp
                    ins = dve.tensor_tensor(ot[:, b * QT:(b + 1) * QT, h * XD:(h + 1) * XD], src[:, hp, :, 0:XD],
                                            r[:, hp, :].unsqueeze(2).to_broadcast([P, QT, XD]), ALU.mult)
                ins.then_inc(s["heads_normalised"], 1)

            def low(i):
                dve.wait_ge(s["heads_high"], i + 1)
                part_low(dve, heads(1, i % GT), TB[i][:].rearrange("p (k n) -> p k n", k=4),
                         heads(0, i % GT)).then_inc(s["heads_low"], 1)

            def place_low(n):
                j, which = n // 2, n % 2
                if which == 0:
                    dve.wait_ge(s["q_high"], j + 1)
                    if j:
                        dve.wait_ge(MQ[(j - 1) % 2], 32 * ((j - 1) // 2 + 1))
                    for hp, r in enumerate(own_rows):
                        ins = part_low(dve, ql[r, :], bank_of(n)[r, :], qst[r, j % 2, hp, :])
                    ins.then_inc(s["q_low"], 1)
                else:
                    dve.wait_ge(s["k_high"], j + 1)
                    if j >= 2:
                        dve.wait_ge(s["scores_ready"], 4 * (j - 1))
                    part_low(dve, kl[:, j % 2, :], bank_of(n)[:], kh[:]).then_inc(s["k_low"], 1)

            place_v(1)
            place_v(3)
            for k in range(KD):
                dve.wait_ge(s["x_high"], k + 1)
                part_low(dve, ul[:, k, :], T2[k][:], uh[:, k, :]).then_inc(s["x_low"], 1)
            place_v(5)
            place_low(0)
            place_low(1)
            place_v(7)
            place_low(2)
            place_low(3)
            for n in range(NHD + 3):
                if n < NHD:
                    masked(n)
                if n >= 2 and (n - 2) % 4 in (Q_AT, K_AT) and (n - 2) // 4 + 2 < ET:
                    place_low(2 * ((n - 2) // 4 + 2) + (Q_AT, K_AT).index((n - 2) % 4))
                if 1 <= n <= NHD and (n - 1) % 2:
                    place(n - 1)
                if n >= 3 and n % 2:
                    normalise((n - 3) // 2)
                if n - 2 in EARLY:
                    low(EARLY.index(n - 2))

            def add(t):
                dve.wait_ge(s["out_projected"], GT + t + 1)
                dve.tensor_tensor(XG[:, t, :], XG[:, t, :], RB[t][:, 0:D], ALU.add).then_inc(s["residual_added"], 1)
                dve.wait_ge(s["residual_added"], t + 1)
                moments(dve, ch, XG[:, t, :], st[:, t, :], mv[:, t, :])

            low(4)
            low(5)
            low(6)
            low(7)
            for t in range(GT):
                add(t)
            ch.sync()



def stage_attention(nc, ctx, g, I, W, K, XN, XG, scratch, ps, s, last):
    with ExitStack() as own:
        def sb(name, shape, dt=F32):
            return own.enter_context(nc.sbuf_tensor("c_" + name, shape, dt))

        parts = sb("parts", [P, 2 * KD * GN], FR)
        qs = parts[:].rearrange("p (t g c d) -> p t g c d", t=GT, g=AKV, c=2)
        oh, ol = (x.rearrange("p (k n) -> p k n", k=KD) for x in (parts[:, 0:KD * GN], parts[:, KD * GN:2 * KD * GN]))
        st, mvn, rstn = sb("st", [P, GT, 6]), sb("mvn", [P, GT, 2]), sb("rstn", [P, GT])
        nt, nt2, roots = sb("nt", [P, 2, GT]), sb("nt2", [P, 2, 2, GT]), sb("roots", [P, 2, GT])
        rstd, scale = roots[:, 0], roots[:, 1]
        mv = K["moments"]
        ln = sb("ln", [P, GT, D])
        xr = sb("xr", [P, GT, D])
        sq, ss, rs = sb("sq", [P, D]), sb("ss", [P, GT]), sb("rs", [P, GT])
        uh, ul = K["uh"], K["ul"]
        NR, HALF = AH + AKV, AD // 2
        ra, rb = sb("ra", [P, 2, NR * AD]), sb("rb", [P, 2, NR * AD])
        rot = sb("rot", [P, 2, NR * AD])
        ks = sb("ks", [P, GT, AKV, 2, AD], FR)
        v = sb("v", [P, GT, AKV, AVW])
        qv = sb("qv", [P, 2, REP, GN], FR)
        kv = sb("kv", [P, 2, 2, GN], FR)
        qb = rot[:].rearrange("p a b -> p (a b)")[:, 0:GN]
        kT = sb("kT", [P, GN], FR)
        repeat = sb("repeat", [P, 2 * AKV, 2 * REP, AD], FR)
        NB = 3
        pp = sb("pp", [P, 4, NB * P])
        nm = sb("nm", [P, 4, QT])
        pt = sb("pt", [P, 4, NB * P])
        rc = sb("rc", [P, 2, 2 * QT])
        ot = sb("ot", [P, GT, AH * AD])

        ident, identr = K["const"][:, C_ID:C_ID + P], K["identr"][:]
        causal = K["const"][:, C_CAUSAL:C_CAUSAL + QT * P]
        BB, SB, TB, OB = ps[0], ps[1:4], ps[4:6], ps[6:8]
        RB = (*SB, OB[0])
        NHD = 2 * AH
        PER = 2 * REP
        NEXT = (NHD - 10, NHD - 6)
        block = own.enter_context(nc.Block())

        FIRST = 2
        BANKS = (BB, OB[0], OB[1])

        def rows(r):
            return K["const"][:, C_ROW + r:C_ROW + r + 1]

        def half(t, hf):
            return t[:, :, hf * 2 * P:(hf + 1) * 2 * P]

        def turned(bank):
            return bank[:].rearrange("p (k n) -> p k n", k=KD)

        def where(n):
            return n // PER, n % PER // REP, n % REP

        @block.sync
        def _(sp):
            sp.dma_start(XN[:], I["x"][(g + 1) % NG]).then_inc(s["next_x_in"], 16)
            clear(sp, last)
            sp.wait_ge(s["residual_added"], GT)
            sp.dma_start(scratch["res"][g], XG[:]).then_inc(s["stored"], 16)
            sp.wait_ge(s["h_low"], 2 * KD)
            sp.dma_start(scratch["h"][g], oh.bitcast(F32)).then_inc(s["stored"], 16)
            sp.dma_start(scratch["l"][g], ol.bitcast(F32)).then_inc(s["stored"], 16)

        @block.gpsimd
        def _(pool):
            pool.memset(v[:, :, :, AD], 1.0).then_inc(s["ones_set"], 1)
            pool.tensor_copy(repeat[:], identr.bitcast(F32).rearrange("p (a d) -> p a d", d=AD).unsqueeze(2)
                             .to_broadcast([P, 2 * AKV, 2 * REP, AD])).then_inc(s["repeat_set"], 1)
            for t in range(GT):
                pool.wait_ge(s["qk_high"], 2 * t + 2)
                q = rot[:, t % 2, 0:AH * AD].rearrange("p (g d) -> p g d", g=AKV)
                k = rot[:, t % 2, AH * AD:NR * AD].rearrange("p (g d) -> p g d", g=AKV)
                pool.tensor_tensor(qs[:, t, :, 1, :], q, qs[:, t, :, 0, :].bitcast(F32), ALU.subtract).then_inc(s["qk_low"], 1)
                pool.tensor_tensor(ks[:, t, :, 1, :], k, ks[:, t, :, 0, :].bitcast(F32), ALU.subtract).then_inc(s["qk_low"], 1)
            for m in range(AKV):
                pool.wait_ge(s["built_placed"], 3 * m + 1)
                if m >= 2:
                    pool.wait_ge(s["scores_ready"], PER * (m - 1))
                for r in range(REP):
                    if m == 0 and r < FIRST:
                        continue
                    pool.tensor_scalar(qv[:, m % 2, r, :], qb, rows(r), None,
                                       ALU.mult).then_inc(s["q_masked"], 1)

        @block.tensor
        def _(pe):
            transposes_in(pe, xr, ident, TB, KD, s["y_normed"], s["y_turned"])
            pe.wait_ge(s["y_low"], KD)
            for t in range(GT):
                for k in range(KD):
                    ins = split_matmul(pe, ps[t][:, 0:AQKV], (uh[:, k, t * P:(t + 1) * P], ul[:, k, t * P:(t + 1) * P]),
                                       [w[:, k, :] for w in W["aqkv"]], k == 0, k == KD - 1)
                ins.then_inc(s["qkv_projected"], 1)
            pe.wait_ge(s["qk_low"], 2 * GT)

            def build(i):
                m, what = i // 3, i % 3
                bank = BANKS[i] if i < 3 else BB
                if i >= 3:
                    pe.wait_ge(s["built_placed"], i)
                if what:
                    pe.matmul(bank[:], repeat[:, 2 * m + what - 1].rearrange("p a d -> p (a d)"), kT[:], start=True,
                              stop=True).then_inc(s["built_ready"], 1)
                    return
                for t in range(GT):
                    ins = pe.transpose(bank[:, t * P:(t + 1) * P].bitcast(FR), qs[:, t, m].rearrange("p a b -> p (a b)"), identr)
                ins.then_inc(s["built_ready"], 1)

            def scores(n):
                m, b, r = where(n)
                if n % PER == 0:
                    pe.wait_ge(s["built_placed"], 3 * m + 3)
                if n == 0:
                    pe.wait_ge(s["q_masked_by_scalar"], FIRST)
                if n % PER < REP and n >= FIRST:
                    pe.wait_ge(s["q_masked"], REP * m + r + 1 - FIRST)
                if n >= 3:
                    pe.wait_ge(s["scores_masked"], 2 * (n - 2))
                for qt in range(QT):
                    at, w = (b * QT + qt) * P, (qt + 1) * P
                    for part in range(2):
                        ins = pe.matmul(SB[n % 3][:, qt * P:qt * P + w], qv[:, m % 2, r, at:at + P],
                                        kv[:, m % 2, part, b * S:b * S + w], start=part == 0, stop=part == 1)
                ins.then_inc(s["scores_ready"], 1)

            def turn(n):
                pe.wait_ge(s["probs_exp"], 2 * (n + 1))
                if n >= 2:
                    pe.wait_ge((s["probs_placed_by_scalar"], s["probs_placed_by_vector"])[n % 2], n // 2)
                for i in range(NB):
                    ins = pe.transpose(TB[n % 2][:, i * P:(i + 1) * P], pp[:, n % 4, i * P:(i + 1) * P], ident)
                ins.then_inc(s["probs_turned"], 1)

            def values(n):
                u, hp = n // 2, n % 2
                b = where(n)[1]
                pe.wait_ge((s["probs_placed_by_scalar"], s["probs_placed_by_vector"])[n % 2], n // 2 + 1)
                if hp == 0 and u >= 2:
                    pe.wait_ge(s["heads_normalised"], u - 1)
                for qt, i, kt in ((0, 0, 0), (1, 1, 0), (1, 2, 1)):
                    at = (hp * QT + qt) * AKV * AVW
                    ins = pe.matmul(OB[u % 2][:, at:at + AKV * AVW], pt[:, n % 4, i * P:(i + 1) * P],
                                    v[:, b * QT + kt].rearrange("p a b -> p (a b)"), start=kt == 0, stop=kt == qt)
                ins.then_inc(s["values_ready"], 1)

            for t in range(GT):
                ins = pe.transpose(SB[2][:, t * P:(t + 1) * P].bitcast(FR), ks[:, t].rearrange("p g c d -> p (g c d)"), identr)
            ins.then_inc(s["k_turned"], 1)
            def turn_half(hf, src, bank, done):
                for k in range(KD):
                    for t in range(QT):
                        ins = pe.transpose(bank[:, (k * QT + t) * P:(k * QT + t + 1) * P],
                                           src[:, hf * QT + t, k * P:(k + 1) * P], ident)
                ins.then_inc(done, 1)

            pe.wait_ge(s["ones_set"], 1)
            pe.wait_ge(s["repeat_set"], 1)
            pe.wait_ge(s["k_copied"], 1)
            for i in range(3):
                build(i)
            scores(0)
            scores(1)
            for n in range(NHD + 1):
                if n + 2 < NHD:
                    scores(n + 2)
                if n < NHD:
                    turn(n)
                if n % PER in (0, 2, 4) and n // PER + 1 < AKV:
                    build(3 * (n // PER + 1) + n % PER // 2)
                if n >= 1:
                    values(n - 1)
                if n in NEXT:
                    k = NEXT.index(n)
                    if k == 0:
                        pe.wait_ge(s["built_placed"], 3 * AKV)
                        pe.wait_ge(s["next_normed"], GT)
                    else:
                        pe.wait_ge(s["next_low"], k)
                    for t in range(GT):
                        ins = pe.transpose(BB[:, t * P:(t + 1) * P], xr[:, t, k * P:(k + 1) * P], ident)
                    ins.then_inc(s["next_turned"], 1)
                if n == NHD - 2:
                    pe.wait_ge(s["heads_normalised"], (NHD - REP) // 2)
                    turn_half(0, ot, BB, s["heads_turned"])

            def project(t):
                pe.wait_ge(s["heads_low"], t // QT + 1)
                for k in range(KD):
                    ins = split_matmul(pe, RB[t][:, 0:D], (oh[:, k, t * P:(t + 1) * P], ol[:, k, t * P:(t + 1) * P]),
                                       [w[:, k, :] for w in W["awo"]], k == 0, k == KD - 1)
                ins.then_inc(s["out_projected"], 1)

            pe.wait_ge(s["scores_masked"], 2 * NHD)
            project(0)
            project(1)
            pe.wait_ge(s["heads_normalised"], NHD // 2)
            turn_half(1, ot, TB[0], s["heads_turned"])
            project(2)
            project(3)
            for hf in range(2):
                pe.wait_ge(s["h_normed"], QT * (hf + 1))
                turn_half(hf, xr, TB[1 - hf], s["h_turned"])

        @block.scalar
        def _(act):
            for k in range(KD):
                act.wait_ge(s["y_turned"], k + 1)
                part_high(act, uh[:, k, :], TB[k][:], K["g1"][:, k:k + 1]).then_inc(s["y_high"], 1)
            for t in range(GT):
                act.wait_ge(s["qk_rotated"], t + 1)
                q = rot[:, t % 2, 0:AH * AD].rearrange("p (g d) -> p g d", g=AKV)
                k = rot[:, t % 2, AH * AD:NR * AD].rearrange("p (g d) -> p g d", g=AKV)
                act.activation(qs[:, t, :, 0, :], q, ACT.Copy).then_inc(s["qk_high"], 1)
                act.activation(ks[:, t, :, 0, :], k, ACT.Copy).then_inc(s["qk_high"], 1)

            def built(i):
                m, what = i // 3, i % 3
                bank = BANKS[i] if i < 3 else BB
                act.wait_ge(s["built_ready"], i + 1)
                if what == 0:
                    if m:
                        act.wait_ge(s["q_masked"], REP * m - FIRST)
                    else:
                        for r in range(FIRST):
                            act.activation(qv[:, 0, r, :], bank[:], ACT.Copy, scale=rows(r)).then_inc(s["q_masked_by_scalar"], 1)
                    ins = act.activation(qb, bank[:], ACT.Copy)
                else:
                    if m >= 2:
                        act.wait_ge(s["scores_ready"], PER * (m - 1))
                    ins = act.activation(kv[:, m % 2, what - 1, :], bank[:], ACT.Copy)
                ins.then_inc(s["built_placed"], 1)

            act.wait_ge(s["k_turned"], 1)
            act.activation(kT[:], SB[2][:], ACT.Copy).then_inc(s["k_copied"], 1)
            for i in range(3):
                built(i)
            for n in range(NHD + 1):
                if n < NHD:
                    act.wait_ge(s["scores_masked"], 2 * n + 1)
                    act.activation(pp[:, n % 4, 0:P], pp[:, n % 4, 0:P], ACT.Exp, bias=nm[:, n % 4, 0:1],
                                   scale=-1.0).then_inc(s["probs_exp"], 1)
                    act.wait_ge(s["scores_masked"], 2 * n + 2)
                    act.activation(pp[:, n % 4, P:NB * P], pp[:, n % 4, P:NB * P], ACT.Exp, bias=nm[:, n % 4, 1:2],
                                   scale=-1.0).then_inc(s["probs_exp"], 1)
                if n >= 1 and n % 2:
                    place = n - 1
                    act.wait_ge(s["probs_turned"], place + 1)
                    if place >= 4:
                        act.wait_ge(s["values_ready"], place - 3)
                    act.activation(pt[:, place % 4, :], TB[place % 2][:, 0:NB * P], ACT.Copy).then_inc(s["probs_placed_by_scalar"], 1)
                if n % PER in (1, 3, 5) and n // PER + 1 < AKV:
                    built(3 * (n // PER + 1) + n % PER // 2)
                if n - 2 in NEXT:
                    k = NEXT.index(n - 2)
                    act.wait_ge(s["next_turned"], k + 1)
                    part_high(act, uh[:, k, :], BB[:]).then_inc(s["next_high"], 1)
                if n == NHD - 1:
                    act.wait_ge(s["heads_turned"], 1)
                    part_high(act, half(oh, 0), turned(BB)).then_inc(s["heads_high"], 1)

            def squares(t):
                act.wait_ge(s["h_ready"], t + 1)
                if t:
                    act.wait_ge(s["h_squares"], t)
                act.activation(sq[:], ln[:, t, :], ACT.Square, accum_out=ss[:, t:t + 1]).then_inc(s["h_squares"], 1)

            squares(0)
            act.wait_ge(s["heads_turned"], 2)
            part_high(act, half(oh, 1), turned(TB[0])).then_inc(s["heads_high"], 1)
            for t in range(1, GT):
                squares(t)
            act.wait_ge(s["out_projected"], GT)
            for hf in range(2):
                act.wait_ge(s["h_turned"], hf + 1)
                for k in range(KD):
                    part_high(act, half(oh, hf)[:, k, :], turned(TB[1 - hf])[:, k, :], K["g2"][:, k:k + 1]).then_inc(s["h_high"], 1)

        @block.vector
        def _(dve):
            ch = Chain(dve, s["chain"])
            tmp = (nt[:, 0], nt[:, 1])
            ch.link(dve.tensor_scalar(nt2[:, 1, 0], mv[:, :, 1], LN_EPS, None, ALU.add))
            ch.link(dve.scalar_tensor_tensor(out=nt2[:, 1, 1], in0=nt2[:, 1, 0], scalar=RMS_EPS, in1=mv[:, :, 1],
                                             op0=ALU.mult, op1=ALU.add))
            inverse_root_of(dve, ch, roots[:], (nt2[:, 0], nt2[:, 1]))
            for t in range(GT):
                dve.tensor_scalar(xr[:, t, :], XG[:, t, :], mv[:, t, 0:1], scale[:, t:t + 1],
                                  ALU.subtract, ALU.mult).then_inc(s["y_normed"], 1)
            for t in range(GT):
                dve.tensor_scalar(ln[:, t, :], XG[:, t, :], mv[:, t, 0:1], rstd[:, t:t + 1],
                                  ALU.subtract, ALU.mult).then_inc(s["layer_norm_ready"], 1)
            for k in range(KD):
                dve.wait_ge(s["y_high"], k + 1)
                part_low(dve, ul[:, k, :], TB[k][:], uh[:, k, :], K["g1"][:, k:k + 1]).then_inc(s["y_low"], 1)

            def halves(ap):
                return ap.rearrange("p (h c d) -> p h c d", c=2, d=HALF)

            def table(t, i):
                return K["rope"][:, t % QT, i, :].unsqueeze(1).to_broadcast([P, NR, HALF])

            for t in range(GT):
                dve.wait_ge(s["qkv_projected"], t + 1)
                src, a, b = halves(ps[t][:, 0:NR * AD]), halves(ra[:, t % 2]), halves(rb[:, t % 2])
                if t >= 2:
                    dve.wait_ge(s["qk_rotated"], t - 1)
                ch.then(dve.tensor_tensor(a, src, K["rope"][:, t % QT, 0, :].unsqueeze(1).unsqueeze(1)
                                          .to_broadcast([P, NR, 2, HALF]), ALU.mult))
                ch.then(dve.tensor_tensor(b[:, :, 0], src[:, :, 1], table(t, 1), ALU.mult))
                ch.then(dve.tensor_tensor(b[:, :, 1], src[:, :, 0], table(t, 2), ALU.mult))
                ch.then(dve.tensor_copy(v[:, t, :, 0:AD],
                                        ps[t][:, NR * AD:AQKV].rearrange("p (h d) -> p h d", d=AD)))
                ch.sync()
                if t >= 2:
                    dve.wait_ge(s["qk_low"], 2 * (t - 1))
                dve.tensor_tensor(rot[:, t % 2, :], ra[:, t % 2, :], rb[:, t % 2, :], ALU.add).then_inc(s["qk_rotated"], 1)

            def masked(n):
                dve.wait_ge(s["scores_ready"], n + 1)
                if n >= 4:
                    dve.wait_ge(s["probs_turned"], n - 3)
                for qt in range(QT):
                    w = slice(qt * P, qt * P + (qt + 1) * P)
                    dve.tensor_tensor_reduce(out=pp[:, n % 4, w], in0=SB[n % 3][:, w], in1=causal[:, (QT - 1 - qt) * P:QT * P],
                                             scale=-AD ** -0.5, scalar=3e38, op0=ALU.add, op1=ALU.min,
                                             accum_out=nm[:, n % 4, qt:qt + 1]).then_inc(s["scores_masked"], 1)

            def place(n):
                dve.wait_ge(s["probs_turned"], n + 1)
                if n >= 4:
                    dve.wait_ge(s["values_ready"], n - 3)
                dve.tensor_copy(pt[:, n % 4, :], TB[n % 2][:, 0:NB * P]).then_inc(s["probs_placed_by_vector"], 1)

            def normalise(u):
                m, b, r = where(2 * u)
                h = m * REP + r
                dve.wait_ge(s["values_ready"], 2 * u + 2)
                src = OB[u % 2][:, 0:2 * QT * AKV * AVW].rearrange("p (h q d) -> p h q d", h=2, q=QT)
                o = rc[:, u % 2].rearrange("p (h q) -> p h q", h=2)
                ch.link(dve.reciprocal(o, src[:, :, :, m * AVW + AD]))
                dve.tensor_tensor(ot[:, b * QT:(b + 1) * QT, h * AD:(h + 2) * AD].rearrange("p q (h d) -> p h q d", h=2),
                                  src[:, :, :, m * AVW:m * AVW + AD],
                                  o.unsqueeze(3).to_broadcast([P, 2, QT, AD]), ALU.mult).then_inc(s["heads_normalised"], 1)

            dve.wait_ge(s["next_x_in"], 16)
            normed(dve, ch, xr, XN, st, mvn, rstn, nt, s["next_normed"])
            for n in range(NHD + 3):
                if n < NHD:
                    masked(n)
                if n - 3 in NEXT:
                    k = NEXT.index(n - 3)
                    dve.wait_ge(s["next_high"], k + 1)
                    part_low(dve, ul[:, k, :], BB[:], uh[:, k, :]).then_inc(s["next_low"], 1)
                if 1 <= n <= NHD and (n - 1) % 2:
                    place(n - 1)
                if n >= 3 and n % 2:
                    normalise((n - 3) // 2)
                if n == NHD:
                    dve.wait_ge(s["heads_high"], 1)
                    part_low(dve, half(ol, 0), turned(BB), half(oh, 0)).then_inc(s["heads_low"], 1)

            def add(t):
                dve.wait_ge(s["out_projected"], t + 1)
                dve.wait_ge(s["layer_norm_ready"], t + 1)
                dve.tensor_tensor(ln[:, t, :], ln[:, t, :], RB[t][:, 0:D], ALU.add).then_inc(s["h_ready"], 1)

            def add_x(t):
                dve.wait_ge(s["h_ready"], t + 1)
                dve.tensor_tensor(XG[:, t, :], XG[:, t, :], ln[:, t, :], ALU.add).then_inc(s["residual_added"], 1)

            def norm(hf):
                dve.wait_ge(s["h_squares"], QT * (hf + 1))
                two = slice(hf * QT, (hf + 1) * QT)
                inverse_root(dve, ch, rs[:, two], ss[:, two], D * RMS_EPS, (nt[:, 0, two], nt[:, 1, two]))
                for t in range(hf * QT, (hf + 1) * QT):
                    dve.tensor_scalar(xr[:, t, :], ln[:, t, :], rs[:, t:t + 1], float(D) ** 0.5,
                                      ALU.mult, ALU.mult).then_inc(s["h_normed"], 1)

            def low(hf):
                dve.wait_ge(s["h_high"], (hf + 1) * KD)
                for k in range(KD):
                    part_low(dve, half(ol, hf)[:, k, :], turned(TB[1 - hf])[:, k, :], half(oh, hf)[:, k, :],
                             K["g2"][:, k:k + 1]).then_inc(s["h_low"], 1)

            add(0)
            add(1)
            dve.wait_ge(s["heads_high"], 2)
            part_low(dve, half(ol, 1), turned(TB[0]), half(oh, 1)).then_inc(s["heads_low"], 1)
            norm(0)
            add(2)
            add_x(0)
            add(3)
            add_x(1)
            norm(1)
            low(0)
            add_x(2)
            add_x(3)
            low(1)
            ch.sync()



def stage_experts(nc, ctx, I, K, scratch, out, ps, s, stored):
    with ExitStack() as own:
        def sb(name, shape, dt=F32):
            return own.enter_context(nc.sbuf_tensor("e_" + name, shape, dt))

        acc = sb("acc", [P, NG, GT, D])
        yh, yl = sb("yh", [P, NG, KD, GN], FR), sb("yl", [P, NG, KD, GN], FR)
        comb = sb("comb", [P, NG, GT, NE])
        now = sb("now", [P, NG, GT, 2])
        raw = [sb("raw1", [P, KD, HID]), sb("raw3", [P, KD, HID]), sb("raw2", [P, HT, D])]
        weights = [[(sb(f"{n}_high{j}", shape, FR), sb(f"{n}_low{j}", shape, FR)) for n, shape in
                    (("w1", [P, KD, HID]), ("w3", [P, KD, HID]), ("w2", [P, HT, D]))] for j in range(2)]
        U1, U3, DN = ps[0:2], ps[2:4], ps[4:8]

        ident = K["const"][:, C_ID:C_ID + P]
        low_of = K["const"][:, C_LOW:C_LOW + NE * NE].rearrange("p (e j) -> p e j", e=NE)
        NT = NG * GT
        acc_in = ctx.enter_context(nc.semaphore("e_acc_in"))
        y_in = (s["y_in_0"], s["y_in_1"])

        with ExitStack() as own_gate:
            def sg(name, shape, dt=F32):
                return own_gate.enter_context(nc.sbuf_tensor("g_" + name, shape, dt))

            graw, gh, gl = sg("raw", [P, KD, NE]), sg("high", [P, KD, NE], FR), sg("low", [P, KD, NE], FR)
            lgf = sg("lgf", [NE, NG, GN])
            lg, ex, rank, tmp = (sg(n, [P, NT, NE]) for n in "lg ex rank tmp".split())
            mx, sm = sg("mx", [P, NT]), sg("sm", [P, NT])
            gt, eq = sg("gt", [P, NT, NE, NE]), sg("eq", [P, NT, NE, NE])
            block = own_gate.enter_context(nc.Block())

            @block.sync
            def _(sp):
                sp.dma_start(graw[:], I["gate"]).then_inc(s["gate_in"], 16)
                sp.wait_ge(stored, 48)
                for half in range(2):
                    g = slice(half * NG // 2, (half + 1) * NG // 2)
                    for t, src in ((yh, scratch["h"]), (yl, scratch["l"])):
                        sp.dma_start(t[:, g].bitcast(F32).rearrange("p g a b -> p g (a b)"),
                                     src[g].rearrange("g p a b -> p g (a b)")).then_inc(y_in[half], 16)
                sp.dma_start(acc[:].rearrange("p g a b -> p g (a b)"),
                             scratch["res"].rearrange("g p a b -> p g (a b)")).then_inc(acc_in, 16)

            @block.scalar
            def _(act):
                for t, src in zip(raw, (I["w1"], I["w3"], I["w2"])):
                    act.dma_start(t[:], src[0]).then_inc(s["raw_in"], 16)
                act.wait_ge(s["gate_in"], 16)
                act.activation(gh[:], graw[:], ACT.Copy).then_inc(s["gate_high"], 1)
                act.wait_ge(s["raw_in"], 48)
                for i in range(3):
                    act.activation(weights[0][i][0][:], raw[i][:], ACT.Copy).then_inc(s["first_high"], 1)
                for g in range(NG):
                    act.wait_ge(s["logits_ready"], g + 1)
                    act.activation(lgf[:, g, :], ps[g][0:NE, :], ACT.Copy).then_inc(s["logits_copied"], 1)
                act.wait_ge(s["logits_shifted"], 1)
                act.activation(ex[:], ex[:], ACT.Exp).then_inc(s["gate_exp"], 1)

            @block.tensor
            def _(pe):
                pe.wait_ge(s["gate_low"], 1)
                for g in range(NG):
                    if g % (NG // 2) == 0:
                        pe.wait_ge(y_in[g // (NG // 2)], 32)
                    for k in range(KD):
                        ins = split_matmul(pe, ps[g][0:NE, :], (gh[:, k, :], gl[:, k, :]), (yh[:, g, k, :], yl[:, g, k, :]),
                                           k == 0, k == KD - 1)
                    ins.then_inc(s["logits_ready"], 1)
                for g in range(NG):
                    pe.wait_ge(s["logits_copied"], g + 1)
                    for t in range(GT):
                        at = (g * GT + t) * NE
                        ins = pe.transpose(ps[4][:, at:at + NE], lgf[:, g, t * P:(t + 1) * P], ident[0:NE, 0:NE])
                ins.then_inc(s["logits_turned"], 1)

            @block.vector
            def _(dve):
                ch = Chain(dve, s["chain"])
                dve.wait_ge(s["gate_high"], 1)
                dve.tensor_tensor(gl[:], graw[:], gh[:].bitcast(F32), ALU.subtract).then_inc(s["gate_low"], 1)
                for i in range(3):
                    dve.wait_ge(s["first_high"], i + 1)
                    w = weights[0][i]
                    dve.tensor_tensor(w[1][:], raw[i][:], w[0][:].bitcast(F32), ALU.subtract)
                dve.wait_ge(s["logits_turned"], 1)
                ch.link(dve.tensor_copy(lg[:], ps[4][:, 0:NT * NE].rearrange("p (t e) -> p t e", t=NT)))
                ch.link(dve.tensor_reduce(mx[:], lg[:], AX_X, ALU.max))
                dve.tensor_tensor(ex[:], lg[:], mx[:].unsqueeze(2).to_broadcast([P, NT, NE]), ALU.subtract).then_inc(s["logits_shifted"], 1)
                dve.wait_ge(s["gate_exp"], 1)
                mine = ex[:].unsqueeze(3).to_broadcast([P, NT, NE, NE])
                other = ex[:].unsqueeze(2).to_broadcast([P, NT, NE, NE])
                ch.then(dve.tensor_tensor(gt[:], other, mine, ALU.is_gt))
                ch.link(dve.tensor_tensor(eq[:], other, mine, ALU.is_equal))
                ch.link(dve.tensor_tensor(eq[:], eq[:], low_of.unsqueeze(1).to_broadcast([P, NT, NE, NE]), ALU.mult))
                ch.link(dve.tensor_tensor(gt[:], gt[:], eq[:], ALU.add))
                ch.link(dve.tensor_reduce(rank[:], gt[:], AX_X, ALU.add))
                ch.link(dve.scalar_tensor_tensor(out=tmp[:], in0=rank[:], scalar=1.5, in1=ex[:], op0=ALU.is_lt, op1=ALU.mult))
                ch.link(dve.tensor_reduce(sm[:], tmp[:], AX_X, ALU.add))
                ch.link(dve.reciprocal(sm[:], sm[:]))
                ch.link(dve.scalar_tensor_tensor(out=comb[:].rearrange("p g t e -> p (g t) e"), in0=tmp[:], scalar=0.5,
                                                 in1=sm[:].unsqueeze(2).to_broadcast([P, NT, NE]), op0=ALU.mult, op1=ALU.mult))

        th, p3 = sb("th", [P, 2, GN]), sb("p3", [P, 2, GN])
        hh, hl = sb("hh", [P, 2, HT, GN], FR), sb("hl", [P, 2, HT, GN], FR)
        PAIR = 2
        NH_ = NG * HT
        SPLIT = (4, 8, 12)
        sources = (I["w1"], I["w3"], I["w2"])

        with nc.Fori(0, NE // PAIR) as e:
            with nc.Block() as block:
                @block.sync
                def _(sp):
                    for j in range(PAIR):
                        for i, (t, src) in enumerate(zip(raw, sources)):
                            if j:
                                sp.wait_ge(s["weights_low"], i + 1)
                            sp.dma_start(t[:], src[(e * PAIR + 1 + j) % NE]).then_inc(s["next_weights_in"], 16)
                    sp.wait_ge(s["next_weights_in"], PAIR * 48)

                @block.gpsimd
                def _(pool):
                    for n in range(PAIR * 3):
                        j, i = n // 3, n % 3
                        pool.wait_ge(s["weights_high"], n + 1)
                        w = weights[1 - j][i]
                        pool.tensor_tensor(w[1][:], raw[i][:], w[0][:].bitcast(F32), ALU.subtract).then_inc(s["weights_low"], 1)

                def high(act, n):
                    G, m = n // HT, n % HT
                    act.wait_ge(s["hidden_ready"], n + 1)
                    if G >= 2:
                        act.wait_ge(s["down_ready"], GT * (G - 1))
                    act.activation(hh[:, G % 2, m, :], p3[:, n % 2, :], ACT.Copy).then_inc(s["hidden_high"], 1)

                @block.scalar
                def _(act):
                    for n in range(PAIR * NH_):
                        j = n // NH_
                        act.wait_ge(s["up_ready"], n + 1)
                        if n >= 2:
                            act.wait_ge(s["hidden_ready"], n - 1)
                        act.activation(th[:, n % 2, :], U1[n % 2][:], ACT.Tanh, scale=0.5).then_inc(s["up_tanh"], 1)
                        if n >= 1:
                            high(act, n - 1)
                        if n % NH_ in SPLIT:
                            i = SPLIT.index(n % NH_)
                            if i == 0:
                                act.wait_ge(s["next_weights_in"], 48 * (j + 1))
                            if j and i == 0:
                                act.wait_ge(s["down_ready"], NG * GT)
                            act.activation(weights[1 - j][i][0][:], raw[i][:], ACT.Copy).then_inc(s["weights_high"], 1)
                    high(act, PAIR * NH_ - 1)

                @block.vector
                def _(dve):
                    dve.tensor_copy(now[:], comb[:, :, :, bass.ds(e * PAIR, PAIR)]).then_inc(s["weights_picked"], 1)
                    dve.wait_ge(s["weights_picked"], 1)

                    def hidden(n):
                        dve.wait_ge(s["up_tanh"], n + 1)
                        if n >= 2:
                            dve.wait_ge(s["hidden_low"], n - 1)
                        dve.scalar_tensor_tensor(out=th[:, n % 2, :], in0=th[:, n % 2, :], scalar=1.0, in1=U1[n % 2][:],
                                                 op0=ALU.add, op1=ALU.mult).then_inc(s["silu_ready"], 1)
                        dve.wait_ge(s["silu_ready"], n + 1)
                        dve.tensor_tensor(p3[:, n % 2, :], th[:, n % 2, :], U3[n % 2][:], ALU.mult).then_inc(s["hidden_ready"], 1)

                    def low(n):
                        G, m = n // HT, n % HT
                        dve.wait_ge(s["hidden_high"], n + 1)
                        dve.tensor_tensor(hl[:, G % 2, m, :], p3[:, n % 2, :], hh[:, G % 2, m, :].bitcast(F32),
                                          ALU.subtract).then_inc(s["hidden_low"], 1)

                    def add(G):
                        j, g = G // NG, G % NG
                        if j:
                            dve.wait_ge(s["sum_added"], GT * (G - NG + 1))
                        elif g == 0:
                            dve.wait_ge(acc_in, 16)
                        for t in range(GT):
                            dve.wait_ge(s["down_ready"], G * GT + t + 1)
                            dve.scalar_tensor_tensor(out=acc[:, g, t, :], in0=DN[t][:, 0:D], scalar=now[:, g, t, j:j + 1],
                                                     in1=acc[:, g, t, :], op0=ALU.mult, op1=ALU.add).then_inc(s["sum_added"], 1)

                    for n in range(PAIR * NH_ + 1):
                        if n < PAIR * NH_:
                            hidden(n)
                        if n >= 1:
                            low(n - 1)
                        if n % HT == 2 and n // HT >= 1:
                            add(n // HT - 1)
                    add(PAIR * NG - 1)
                    dve.wait_ge(s["sum_added"], PAIR * NG * GT)

                @block.tensor
                def _(pe):
                    def up(n):
                        j, g, m = n // NH_, n // HT % NG, n % HT
                        w1, w3, _ = weights[j]
                        if n >= 2:
                            pe.wait_ge(s["hidden_ready"], n - 1)
                        if n == NH_:
                            pe.wait_ge(s["weights_low"], 3)
                        for w, bank in ((w1, U1[n % 2]), (w3, U3[n % 2])):
                            for k in range(KD):
                                ins = split_matmul(pe, bank[:], [x[:, k, m * P:(m + 1) * P] for x in w],
                                                   (yh[:, g, k, :], yl[:, g, k, :]), k == 0, k == KD - 1)
                        ins.then_inc(s["up_ready"], 1)

                    def down(G):
                        w2 = weights[G // NG][2]
                        pe.wait_ge(s["hidden_low"], HT * (G + 1))
                        for t in range(GT):
                            if G:
                                pe.wait_ge(s["sum_added"], GT * (G - 1) + t + 1)
                            for m in range(HT):
                                ins = split_matmul(pe, DN[t][:, 0:D], (hh[:, G % 2, m, t * P:(t + 1) * P],
                                                                       hl[:, G % 2, m, t * P:(t + 1) * P]),
                                                   [x[:, m, :] for x in w2], m == 0, m == HT - 1)
                            ins.then_inc(s["down_ready"], 1)

                    for n in range(PAIR * NH_):
                        up(n)
                        if n % HT == 1 and n // HT >= 1:
                            down(n // HT - 1)
                    down(PAIR * NG - 1)

            with nc.Block() as block:
                @block.sync
                def _(sp):
                    clear(sp, s)

        with nc.Block() as block:
            @block.sync
            def _(sp):
                sp.dma_start(out.rearrange("(g t p) d -> p g t d", p=P, t=GT), acc[:]).then_inc(s["out_stored"], 16)
                sp.wait_ge(s["out_stored"], 16)



SEM_A = ("next_ctx next_mask x_times_dt decay_rates decay_sums decays_masked dt_projected dt_copied dt_turned "
         "conv_done conv_projected z_projected conv_silu x_bank_read x_turned small_bank_read chunk_scores "
         "decays_exp z_gated decay_sums_half scores_decayed y_bank_read y_product x_decayed state_part "
         "state_product y_gated y_low y_turned residual_added out_projected conv_begun conv_tanh minus_abs_dt "
         "exp_dt z_tanh y_high y_squares chunk_decays_exp chain")
SEM_B = ("probs_placed_by_scalar probs_placed_by_vector q_moved_even q_moved_odd k_moved_even k_moved_odd "
         "q_low k_high ones_set v_placed_by_scalar v_placed_by_vector v_projected k_low qk_projected "
         "scores_masked scores_ready probs_exp probs_turned heads_normalised values_ready heads_low "
         "heads_turned context_low x_normed x_turned x_low out_projected context_high q_high heads_high "
         "x_high chain residual_added")
SEM_C = ("next_x_in residual_added stored h_low ones_set repeat_set qk_high qk_low built_placed scores_ready "
         "q_masked y_normed y_turned y_low qkv_projected built_ready q_masked_by_scalar scores_masked "
         "probs_exp probs_placed_by_scalar probs_placed_by_vector probs_turned heads_normalised values_ready "
         "k_turned k_copied next_normed next_low next_turned heads_turned heads_low out_projected h_normed "
         "h_turned y_high qk_rotated next_high heads_high h_ready h_squares h_high chain layer_norm_ready")
SEM_E = ("y_in_0 y_in_1 gate_in raw_in gate_high first_high logits_ready logits_copied logits_shifted "
         "gate_exp gate_low logits_turned chain weights_low next_weights_in weights_high hidden_ready "
         "down_ready hidden_high up_ready up_tanh weights_picked hidden_low silu_ready sum_added out_stored")



def decoder_layer(nc, I, out):
    with ExitStack() as ctx:
        def sb(name, shape, dt=F32):
            return ctx.enter_context(nc.sbuf_tensor(name, shape, dt))

        ps = [ctx.enter_context(nc.psum_tensor(f"bank{i}", [P, 512], F32)) for i in range(8)]
        K = {"const": sb("const", [P, C_N])}
        scratch = dict(
            res=nc.dram_tensor("residual", (NG, P, GT, D), F32, kind="Internal").ap(),
            h=nc.dram_tensor("x2_high", (NG, P, KD, GN), F32, kind="Internal").ap(),
            l=nc.dram_tensor("x2_low", (NG, P, KD, GN), F32, kind="Internal").ap())
        sC = semaphores(nc, ctx, "c", SEM_C)
        with ExitStack() as attn:
            sA = semaphores(nc, attn, "a", SEM_A)
            sB = semaphores(nc, attn, "b", SEM_B)

            def sb(name, shape, dt=F32):
                return attn.enter_context(nc.sbuf_tensor(name, shape, dt))

            K["rope"], K["taps"], K["tapb"], K["nw"] = sb("rope", [P, QT, 3, AD // 2]), sb("taps", [P, CT, TAPS]), sb("tapb", [P, CT]), sb("nw", [P, XT])
            K["moments"] = sb("moments", [P, GT, 2])
            K["uh"], K["ul"] = sb("uh", [P, KD, GN], FR), sb("ul", [P, KD, GN], FR)
            K["identr"] = sb("identr", [P, P], FR)
            K["g1"], K["g2"] = sb("g1", [P, KD]), sb("g2", [P, KD])
            K["dtb"], K["alog"], K["A"], K["dpar"] = sb("dtb", [P, NH]), sb("alog", [P, NH]), sb("A", [P, NH]), sb("dpar", [P, NH])
            W = {}
            for n, shape in (("win", [P, KD, PROJ]), ("wout", [P, XT, D]), ("wq", [P, KD, XI]), ("wk", [P, KD, XI]),
                             ("wv", [P, KD, XI]), ("wo", [P, ET, D]), ("aqkv", [P, KD, AQKV]), ("awo", [P, KD, D])):
                W[n] = (sb(n + "_high", shape, FR), sb(n + "_low", shape, FR))
            XN, XG = sb("XN", [P, GT, D]), sb("XG", [P, GT, D])
            CX = sb("context", [P, KD, GN]), sb("mask", [P, GT, S])
            load_weights(nc, ctx, I, W, K, XN, ps, sC["stored"])
            with nc.Fori(0, NG) as g:
                stage_mamba(nc, ctx, g, I, W, K, XN, XG, CX, ps, sA, sC)
                stage_cross(nc, ctx, g, W, K, XG, CX, ps, sB, sA)
                stage_attention(nc, ctx, g, I, W, K, XN, XG, scratch, ps, sC, sB)
        sE = semaphores(nc, ctx, "e", SEM_E)
        stage_experts(nc, ctx, I, K, scratch, out, ps, sE, sC["stored"])


def kernel(x, ctx_1024, fside_Bx1xSxS2_0, L0_attn_in_proj_w, L0_attn_conv_weight, L0_attn_conv_bias, L0_attn_dt_bias,
           L0_attn_A_log, L0_attn_D_param, L0_attn_norm_weight, L0_attn_out_proj_w, L0_xattn_Wq, L0_xattn_Wk,
           L0_xattn_Wv, L0_xattn_Wo, L0_ffn_g1, L0_ffn_g2, L0_ffn_wq, L0_ffn_wk, L0_ffn_wv, L0_ffn_wo, L0_ffn_gate,
           L0_ffn_w1, L0_ffn_w2, L0_ffn_w3):
    import numpy as _np
    import concourse.bacc as _bacc
    from concourse.bass_utils import run_bass_kernel_spmd as _run

    def rows(w):
        w = _np.asarray(w)
        return w.reshape(w.shape[0] // P, P, -1).transpose(1, 0, 2)

    def every(v):
        return _np.broadcast_to(_np.asarray(v), (P, _np.shape(v)[0]))

    laid = {
        "x": _np.asarray(x).reshape(NG, GT, P, D).transpose(0, 2, 1, 3),
        "ctxT": _np.asarray(ctx_1024).reshape(NG, GN, KD, P).transpose(0, 3, 2, 1),
        "mask": _np.asarray(fside_Bx1xSxS2_0).reshape(NG, GT, P, S).transpose(0, 2, 1, 3),
        "win": rows(L0_attn_in_proj_w), "wout": rows(L0_attn_out_proj_w),
        "taps": _np.asarray(L0_attn_conv_weight).reshape(CT, P, TAPS).transpose(1, 0, 2),
        "tapb": _np.asarray(L0_attn_conv_bias).reshape(CT, P).T,
        "nw": _np.asarray(L0_attn_norm_weight).reshape(XT, P).T,
        "dtb": every(L0_attn_dt_bias), "alog": every(L0_attn_A_log), "dpar": every(L0_attn_D_param),
        "wq": rows(_np.asarray(L0_xattn_Wq).T), "wk": rows(_np.asarray(L0_xattn_Wk).T), "wv": rows(_np.asarray(L0_xattn_Wv).T),
        "wo": rows(_np.asarray(L0_xattn_Wo).T),
        "aqkv": _np.concatenate([rows(L0_ffn_wq), rows(L0_ffn_wk), rows(L0_ffn_wv)], axis=2),
        "awo": rows(L0_ffn_wo), "gate": rows(L0_ffn_gate),
        "g1": _np.asarray(L0_ffn_g1).reshape(KD, P).T, "g2": _np.asarray(L0_ffn_g2).reshape(KD, P).T,
        "w1": _np.stack([rows(w) for w in _np.asarray(L0_ffn_w1)]), "w3": _np.stack([rows(w) for w in _np.asarray(L0_ffn_w3)]),
        "w2": _np.stack([rows(w) for w in _np.asarray(L0_ffn_w2)]),
        "const": constants(), "rope": rope_tables(),
    }
    nc = _bacc.Bacc("TRN2", target_bir_lowering=False, num_devices=1)
    arrays = {f"in_{n}": _np.ascontiguousarray(a) for n, a in laid.items()}
    I = {n: nc.dram_tensor(f"in_{n}", a.shape, F32, kind="ExternalInput").ap()
                           for n, a in ((n, arrays[f"in_{n}"]) for n in laid)}
    out = nc.dram_tensor("out", (TOK, D), F32, kind="ExternalOutput").ap()
    decoder_layer(nc, I, out)
    r = _run(nc, [arrays], core_ids=[0])
    return r.results[0]["out"].reshape(B, S, D)
```
